# Optimizing a Trainium2 kernel written in Bass

```python
import numpy as np
import jax
import jax.numpy as jnp

def _softmax(x, axis=-1):
    return jax.nn.softmax(x, axis=axis)

def _gelu(x):
    return jax.nn.gelu(x, approximate=True)

def _silu(x):
    return jax.nn.silu(x)

def _sigmoid(x):
    return jax.nn.sigmoid(x)

def _layernorm(x, axis=-1, eps=1e-05):
    m = jnp.mean(x, axis=axis, keepdims=True)
    v = jnp.var(x, axis=axis, keepdims=True)
    return (x - m) / jnp.sqrt(v + eps)

def _scatter_add(tgt, idx, src, axis=0):
    return tgt.at[idx].add(src)

def _segment_sum(src, seg, n):
    return jax.ops.segment_sum(src, seg, n)
kernel_name = 'mk_decoder_postln_d2_seqx_r8_a9dfeb'

def setup_inputs(seed: int=0):
    np.random.seed(seed)
    _w = jnp.asarray

    def _rec_inputs():
        import jax
        import jax.numpy as jnp
        _rk = jax.random.key(seed)
        x = 7.22e-05 + 1 * jax.random.normal(jax.random.fold_in(_rk, 1), (16, 128, 128), jnp.float32)
        _lenS = 128 - jax.random.randint(jax.random.fold_in(_rk, 7), (16,), 0, max(1, 128 // 4) + 1, jnp.int32)
        _lenS2 = 128 - jax.random.randint(jax.random.fold_in(_rk, 8), (16,), 0, max(1, 128 // 4) + 1, jnp.int32)
        _ctx_1024P = jax.random.normal(jax.random.fold_in(_rk, 11), (16, 16, 128), jnp.float32)
        _ctx_1024c = jax.random.dirichlet(jax.random.fold_in(_rk, 511), 0.3 * jnp.ones((16,), jnp.float32), (16, 128))
        _ctx_1024t = jnp.einsum('bsk,bkd->bsd', _ctx_1024c, _ctx_1024P)
        _ctx_1024t = _ctx_1024t * jax.lax.rsqrt(jnp.mean(jnp.square(_ctx_1024t)) + 1e-12) * 0.953939
        ctx_1024 = -1.39393e-06 + 0.999914 * (_ctx_1024t + 0.3 * jax.random.normal(jax.random.fold_in(_rk, 611), (16, 128, 128), jnp.float32))
        return (x, ctx_1024)
    x, ctx_1024 = _rec_inputs()

    def _L0_attn_setup():
        import jax, jax.numpy as jnp
        import numpy as np
        B, T, D, H = (4, 128, 128, 16)
        key = jax.random.key(seed)
        ks = jax.random.split(key, 7)
        x = jax.random.normal(ks[0], (B, T, D), dtype=jnp.float32)
        scale = 0.02
        Wq = jax.random.normal(ks[1], (D, D), dtype=jnp.float32) * scale
        Wk = jax.random.normal(ks[2], (D, D), dtype=jnp.float32) * scale
        Wv = jax.random.normal(ks[3], (D, D), dtype=jnp.float32) * scale
        bq = jax.random.normal(ks[4], (D,), dtype=jnp.float32) * scale
        bk = jax.random.normal(ks[5], (D,), dtype=jnp.float32) * scale
        bv = jax.random.normal(ks[6], (D,), dtype=jnp.float32) * scale
        temperature = jnp.ones((H, 1, 1), dtype=jnp.float32)
        return {'x': x, 'Wq': Wq, 'bq': bq, 'Wk': Wk, 'bk': bk, 'Wv': Wv, 'bv': bv, 'temperature': temperature}
    _L0_attn_all = _L0_attn_setup()
    _L0_attn_in = {k: v for k, v in _L0_attn_all.items() if k in ('Wq', 'bq', 'Wk', 'bk', 'Wv', 'bv', 'temperature')}
    del _L0_attn_all

    def _L0_xattn_setup():
        import jax, jax.numpy as jnp
        import numpy as np
        DIM = 128
        NH = 8
        HD = DIM // NH
        E = 8
        EPS = 1e-05

        def rope_cos_sin(L, hd):
            inv_freq = 1.0 / 10000.0 ** (jnp.arange(0, hd, 2, dtype=jnp.float32) / hd)
            freqs = jnp.arange(L, dtype=jnp.float32)[:, None] * inv_freq[None, :]
            emb = jnp.concatenate([freqs, freqs], axis=-1)
            return (jnp.cos(emb), jnp.sin(emb))

        def rotate_half(x):
            x1 = x[..., 0::2]
            x2 = x[..., 1::2]
            return jnp.stack((-x2, x1), axis=-1).reshape(x.shape)

        def rope(t, cos, sin):
            return t * cos[None, None] + rotate_half(t) * sin[None, None]

        def heads(t):
            B, L, C = t.shape
            return t.reshape(B, L, NH, HD).transpose(0, 2, 1, 3)
        key = jax.random.key(seed)
        ks = jax.random.split(key, 32)
        std = 0.02
        d = {}
        d['x'] = jax.random.normal(ks[0], (16, 64, DIM), jnp.float32)
        d['h_a'] = jax.random.normal(ks[1], (16, 32, DIM), jnp.float32)
        d['h_t'] = jax.random.normal(ks[2], (16, 32, DIM), jnp.float32)
        names = ['qa', 'ka', 'va', 'qt', 'kt', 'vt', 'o', 'ffn']
        for i, n in enumerate(names):
            d['W_' + n] = jax.random.normal(ks[3 + 2 * i], (E, DIM, DIM), jnp.float32) * std
            d['b_' + n] = jax.random.normal(ks[4 + 2 * i], (E, DIM), jnp.float32) * std
        d['gamma'] = jnp.ones((E, DIM), jnp.float32)
        d['beta'] = jnp.zeros((E, DIM), jnp.float32)
        d['gating_factor'] = jnp.zeros((E,), jnp.float32)
        d['expert_idx'] = 3
        return d
    _L0_xattn_all = _L0_xattn_setup()
    _L0_xattn_in = {k: v for k, v in _L0_xattn_all.items() if k in ('W_qa', 'b_qa', 'W_ka', 'b_ka', 'W_va', 'b_va', 'W_qt', 'b_qt', 'W_kt', 'b_kt', 'W_vt', 'b_vt', 'W_o', 'b_o', 'W_ffn', 'b_ffn', 'gamma', 'beta', 'gating_factor')}
    del _L0_xattn_all

    def _L0_ffn_setup():
        import jax, jax.numpy as jnp
        import numpy as np
        DIM = 128
        DEPTH = 6
        HEADS = 16
        DIM_HEAD = 64
        WINDOW = 32
        INNER = HEADS * DIM_HEAD
        DIM_INNER = int(DIM * 4 * 2 / 3)
        QK_SCALE = 8.0

        def shift_tokens(t):
            a, s = jnp.split(t, 2, -1)
            s = jnp.pad(s, ((0, 0), (1, 0), (0, 0)))[:, :-1]
            return jnp.concatenate([a, s], -1)

        def l2norm(t):
            return t / jnp.maximum(jnp.linalg.norm(t, axis=-1, keepdims=True), 1e-12)

        def rotate_half(x):
            x1, x2 = jnp.split(x, 2, -1)
            return jnp.concatenate([-x2, x1], -1)

        def rotary_tables(n):
            half = jnp.arange(0, DIM_HEAD, 2, dtype=jnp.float32)
            inv_freq = 1.0 / 10000.0 ** (half / DIM_HEAD)
            t = jnp.arange(n, dtype=jnp.float32)
            freqs = t[:, None] * inv_freq[None, :]
            freqs = jnp.concatenate([freqs, freqs], -1)
            base_scale = (half + 0.4 * DIM_HEAD) / (1.4 * DIM_HEAD)
            power = (t - n // 2) / (WINDOW // 2)
            scale = base_scale[None, :] ** power[:, None]
            scale = jnp.concatenate([scale, scale], -1)
            return (freqs, scale)

        def local_attention(q, k, v):
            b, h, n, d = q.shape
            w = WINDOW
            nw = n // w
            bq = q.reshape(b, h, nw, w, d)
            bk = k.reshape(b, h, nw, w, d)
            bv = v.reshape(b, h, nw, w, d)

            def look(t):
                p = jnp.pad(t, ((0, 0), (0, 0), (1, 0), (0, 0), (0, 0)))
                return jnp.concatenate([p[:, :, :nw], p[:, :, 1:]], axis=3)
            bk2, bv2 = (look(bk), look(bv))
            seq = jnp.arange(n).reshape(nw, w)
            seq_p = jnp.pad(seq, ((1, 0), (0, 0)), constant_values=-1)
            jt = jnp.concatenate([seq_p[:nw], seq_p[1:]], axis=1)
            it = seq[:, :, None]
            jb = jt[:, None, :]
            mask = (it < jb) | (it > jb + w) | (jb == -1)
            sim = jnp.einsum('bhwie,bhwje->bhwij', bq, bk2) * QK_SCALE
            sim = jnp.where(mask, -jnp.finfo(sim.dtype).max, sim)
            attn = jax.nn.softmax(sim, -1)
            out = jnp.einsum('bhwij,bhwje->bhwie', attn, bv2)
            return out.reshape(b, h, n, d)

        def attn_layer(x, Wqkv, qs, ksc, Wo):
            b, n, _ = x.shape
            qkv = x @ Wqkv
            q, k, v = jnp.split(qkv, 3, -1)
            sh = lambda t: t.reshape(b, n, HEADS, DIM_HEAD).transpose(0, 2, 1, 3)
            q, k, v = (sh(q), sh(k), sh(v))
            q = l2norm(q) * qs
            k = l2norm(k) * ksc
            freqs, scale = rotary_tables(n)
            cos, sin = (jnp.cos(freqs), jnp.sin(freqs))
            q = q * cos * scale + rotate_half(q) * sin * scale
            inv = 1.0 / scale
            k = k * cos * inv + rotate_half(k) * sin * inv
            out = local_attention(q, k, v)
            out = out.transpose(0, 2, 1, 3).reshape(b, n, INNER)
            return out @ Wo

        def ffn_layer(x, g, bln, W1, b1, W2, b2):
            mu = x.mean(-1, keepdims=True)
            var = ((x - mu) ** 2).mean(-1, keepdims=True)
            xn = (x - mu) / jnp.sqrt(var + 1e-05) * g + bln
            hg = xn @ W1 + b1
            a, gate = jnp.split(hg, 2, -1)
            return a * jax.nn.gelu(gate, approximate=False) @ W2 + b2
        key = jax.random.key(seed)
        ks = jax.random.split(key, 8)
        B, N = (2, 256)
        init = lambda k, shape: jax.random.normal(k, shape, jnp.float32) * 0.02
        return {'x': jax.random.normal(ks[0], (B, N, DIM), jnp.float32), 'Wqkv': init(ks[1], (DEPTH, DIM, 3 * INNER)), 'q_scale': jnp.ones((DEPTH, DIM_HEAD), jnp.float32), 'k_scale': jnp.ones((DEPTH, DIM_HEAD), jnp.float32), 'Wo': init(ks[2], (DEPTH, INNER, DIM)), 'ln_g': jnp.ones((DEPTH, DIM), jnp.float32), 'ln_b': jnp.zeros((DEPTH, DIM), jnp.float32), 'W1': init(ks[3], (DEPTH, DIM, 2 * DIM_INNER)), 'b1': jnp.zeros((DEPTH, 2 * DIM_INNER), jnp.float32), 'W2': init(ks[4], (DEPTH, DIM_INNER, DIM)), 'b2': jnp.zeros((DEPTH, DIM), jnp.float32)}
    _L0_ffn_all = _L0_ffn_setup()
    _L0_ffn_in = {k: v for k, v in _L0_ffn_all.items() if k in ('Wqkv', 'q_scale', 'k_scale', 'Wo', 'ln_g', 'ln_b', 'W1', 'b1', 'W2', 'b2')}
    del _L0_ffn_all

    def _L1_attn_setup():
        import jax, jax.numpy as jnp
        import numpy as np
        HIDDEN = 128
        NUM_HEADS = 16
        HEAD_DIM = HIDDEN // NUM_HEADS
        MASK_BIAS = -10000.0

        def _split_heads(t):
            B, S, _ = t.shape
            return t.reshape(B, S, NUM_HEADS, HEAD_DIM).transpose(0, 2, 1, 3)
        key = jax.random.key(seed)
        ks = jax.random.split(key, 5)
        B, S = (4, 256)
        hidden_states = jax.random.normal(ks[0], (B, S, HIDDEN), dtype=jnp.float32)
        w_qkv = jax.random.normal(ks[1], (HIDDEN, 3 * HIDDEN), dtype=jnp.float32) * HIDDEN ** (-0.5)
        b_qkv = jax.random.normal(ks[2], (3 * HIDDEN,), dtype=jnp.float32) * 0.02
        w_dense = jax.random.normal(ks[3], (HIDDEN, HIDDEN), dtype=jnp.float32) * HIDDEN ** (-0.5)
        b_dense = jax.random.normal(ks[4], (HIDDEN,), dtype=jnp.float32) * 0.02
        return {'hidden_states': hidden_states, 'w_qkv': w_qkv, 'b_qkv': b_qkv, 'w_dense': w_dense, 'b_dense': b_dense}
    _L1_attn_all = _L1_attn_setup()
    _L1_attn_in = {k: v for k, v in _L1_attn_all.items() if k in ('w_qkv', 'b_qkv', 'w_dense', 'b_dense')}
    del _L1_attn_all

    def _L1_xattn_setup():
        import jax, jax.numpy as jnp
        import numpy as np
        NUM_HEADS = 8

        def _split_heads(x, h):
            b, n, c = x.shape
            return x.reshape(b, n, h, c // h).transpose(0, 2, 1, 3)
        key = jax.random.key(seed)
        ks = jax.random.split(key, 5)
        B, N, K, C = (16, 512, 64, 128)
        return {'img_fea': jax.random.normal(ks[0], (B, N, C), dtype=jnp.float32), 'aud_fea': jax.random.normal(ks[1], (B, K, C), dtype=jnp.float32), 'Wq': jax.random.normal(ks[2], (C, C), dtype=jnp.float32) * 0.02, 'Wk': jax.random.normal(ks[3], (C, C), dtype=jnp.float32) * 0.02, 'Wv': jax.random.normal(ks[4], (C, C), dtype=jnp.float32) * 0.02, 'aq': 1, 'sigmoid': 0, 'softmax': 1}
    _L1_xattn_all = _L1_xattn_setup()
    _L1_xattn_in = {k: v for k, v in _L1_xattn_all.items() if k in ('Wq', 'Wk', 'Wv')}
    del _L1_xattn_all

    def _L1_ffn_setup():
        import jax, jax.numpy as jnp
        import numpy as np
        TOP_K = 2

        def _mlp(x, w1, b1, w2, b2):
            h = jax.nn.gelu(jnp.einsum('bsd,di->bsi', x, w1) + b1)
            return jnp.einsum('bsi,id->bsd', h, w2) + b2
        key = jax.random.key(seed)
        ks = jax.random.split(key, 8)
        B, S, D, I, E = (2, 256, 128, 512, 8)
        s_in = 1.0 / np.sqrt(D)
        s_mid = 1.0 / np.sqrt(I)
        return {'x': jax.random.normal(ks[0], (B, S, D), jnp.float32), 'gate_w': jax.random.normal(ks[1], (D, E), jnp.float32) * s_in, 'gate_b': jnp.zeros((E,), jnp.float32), 'sh_w1': jax.random.normal(ks[2], (D, I), jnp.float32) * s_in, 'sh_b1': jnp.zeros((I,), jnp.float32), 'sh_w2': jax.random.normal(ks[3], (I, D), jnp.float32) * s_mid, 'sh_b2': jnp.zeros((D,), jnp.float32), 'ew1': jax.random.normal(ks[4], (E, D, I), jnp.float32) * s_in, 'eb1': jnp.zeros((E, I), jnp.float32), 'ew2': jax.random.normal(ks[5], (E, I, D), jnp.float32) * s_mid, 'eb2': jnp.zeros((E, D), jnp.float32)}
    _L1_ffn_all = _L1_ffn_setup()
    _L1_ffn_in = {k: v for k, v in _L1_ffn_all.items() if k in ('gate_w', 'gate_b', 'sh_w1', 'sh_b1', 'sh_w2', 'sh_b2', 'ew1', 'eb1', 'ew2', 'eb2')}
    del _L1_ffn_all
    return {'x': x, 'ctx_1024': ctx_1024, 'L0_attn_Wq': _L0_attn_in['Wq'], 'L0_attn_bq': _L0_attn_in['bq'], 'L0_attn_Wk': _L0_attn_in['Wk'], 'L0_attn_bk': _L0_attn_in['bk'], 'L0_attn_Wv': _L0_attn_in['Wv'], 'L0_attn_bv': _L0_attn_in['bv'], 'L0_attn_temperature': _L0_attn_in['temperature'], 'L0_xattn_W_qa': _L0_xattn_in['W_qa'], 'L0_xattn_b_qa': _L0_xattn_in['b_qa'], 'L0_xattn_W_ka': _L0_xattn_in['W_ka'], 'L0_xattn_b_ka': _L0_xattn_in['b_ka'], 'L0_xattn_W_va': _L0_xattn_in['W_va'], 'L0_xattn_b_va': _L0_xattn_in['b_va'], 'L0_xattn_W_qt': _L0_xattn_in['W_qt'], 'L0_xattn_b_qt': _L0_xattn_in['b_qt'], 'L0_xattn_W_kt': _L0_xattn_in['W_kt'], 'L0_xattn_b_kt': _L0_xattn_in['b_kt'], 'L0_xattn_W_vt': _L0_xattn_in['W_vt'], 'L0_xattn_b_vt': _L0_xattn_in['b_vt'], 'L0_xattn_W_o': _L0_xattn_in['W_o'], 'L0_xattn_b_o': _L0_xattn_in['b_o'], 'L0_xattn_W_ffn': _L0_xattn_in['W_ffn'], 'L0_xattn_b_ffn': _L0_xattn_in['b_ffn'], 'L0_xattn_gamma': _L0_xattn_in['gamma'], 'L0_xattn_beta': _L0_xattn_in['beta'], 'L0_xattn_gating_factor': _L0_xattn_in['gating_factor'], 'L0_ffn_Wqkv': _L0_ffn_in['Wqkv'], 'L0_ffn_q_scale': _L0_ffn_in['q_scale'], 'L0_ffn_k_scale': _L0_ffn_in['k_scale'], 'L0_ffn_Wo': _L0_ffn_in['Wo'], 'L0_ffn_ln_g': _L0_ffn_in['ln_g'], 'L0_ffn_ln_b': _L0_ffn_in['ln_b'], 'L0_ffn_W1': _L0_ffn_in['W1'], 'L0_ffn_b1': _L0_ffn_in['b1'], 'L0_ffn_W2': _L0_ffn_in['W2'], 'L0_ffn_b2': _L0_ffn_in['b2'], 'L1_attn_w_qkv': _L1_attn_in['w_qkv'], 'L1_attn_b_qkv': _L1_attn_in['b_qkv'], 'L1_attn_w_dense': _L1_attn_in['w_dense'], 'L1_attn_b_dense': _L1_attn_in['b_dense'], 'L1_xattn_Wq': _L1_xattn_in['Wq'], 'L1_xattn_Wk': _L1_xattn_in['Wk'], 'L1_xattn_Wv': _L1_xattn_in['Wv'], 'L1_ffn_gate_w': _L1_ffn_in['gate_w'], 'L1_ffn_gate_b': _L1_ffn_in['gate_b'], 'L1_ffn_sh_w1': _L1_ffn_in['sh_w1'], 'L1_ffn_sh_b1': _L1_ffn_in['sh_b1'], 'L1_ffn_sh_w2': _L1_ffn_in['sh_w2'], 'L1_ffn_sh_b2': _L1_ffn_in['sh_b2'], 'L1_ffn_ew1': _L1_ffn_in['ew1'], 'L1_ffn_eb1': _L1_ffn_in['eb1'], 'L1_ffn_ew2': _L1_ffn_in['ew2'], 'L1_ffn_eb2': _L1_ffn_in['eb2']}

def reference(x, ctx_1024, L0_attn_Wq, L0_attn_bq, L0_attn_Wk, L0_attn_bk, L0_attn_Wv, L0_attn_bv, L0_attn_temperature, L0_xattn_W_qa, L0_xattn_b_qa, L0_xattn_W_ka, L0_xattn_b_ka, L0_xattn_W_va, L0_xattn_b_va, L0_xattn_W_qt, L0_xattn_b_qt, L0_xattn_W_kt, L0_xattn_b_kt, L0_xattn_W_vt, L0_xattn_b_vt, L0_xattn_W_o, L0_xattn_b_o, L0_xattn_W_ffn, L0_xattn_b_ffn, L0_xattn_gamma, L0_xattn_beta, L0_xattn_gating_factor, L0_ffn_Wqkv, L0_ffn_q_scale, L0_ffn_k_scale, L0_ffn_Wo, L0_ffn_ln_g, L0_ffn_ln_b, L0_ffn_W1, L0_ffn_b1, L0_ffn_W2, L0_ffn_b2, L1_attn_w_qkv, L1_attn_b_qkv, L1_attn_w_dense, L1_attn_b_dense, L1_xattn_Wq, L1_xattn_Wk, L1_xattn_Wv, L1_ffn_gate_w, L1_ffn_gate_b, L1_ffn_sh_w1, L1_ffn_sh_b1, L1_ffn_sh_w2, L1_ffn_sh_b2, L1_ffn_ew1, L1_ffn_eb1, L1_ffn_ew2, L1_ffn_eb2):
    import jax
    import jax.numpy as jnp

    def _L0_attn_ref(x, Wq, bq, Wk, bk, Wv, bv, temperature):
        import jax, jax.numpy as jnp
        import numpy as np
        B, T, D, H = (4, 128, 128, 16)
        b, t, d = x.shape
        h = temperature.shape[0]
        dh = d // h
        q = (x @ Wq + bq).reshape(b, h, dh, t)
        k = (x @ Wk + bk).reshape(b, h, dh, t)
        v = (x @ Wv + bv).reshape(b, h, dh, t)
        attn = jnp.einsum('bhdt,bhds->bhts', k, v) * temperature
        attn = jax.nn.softmax(attn, axis=-1)
        out = jnp.einsum('bhdt,bhts->bhds', q, attn)
        return out.reshape(b, t, d)

    def _L0_xattn_ref(x, h_a, h_t, W_qa, b_qa, W_ka, b_ka, W_va, b_va, W_qt, b_qt, W_kt, b_kt, W_vt, b_vt, W_o, b_o, W_ffn, b_ffn, gamma, beta, gating_factor, expert_idx):
        import jax, jax.numpy as jnp
        import numpy as np
        DIM = 128
        NH = 8
        HD = DIM // NH
        E = 8
        EPS = 1e-05

        def rope_cos_sin(L, hd):
            inv_freq = 1.0 / 10000.0 ** (jnp.arange(0, hd, 2, dtype=jnp.float32) / hd)
            freqs = jnp.arange(L, dtype=jnp.float32)[:, None] * inv_freq[None, :]
            emb = jnp.concatenate([freqs, freqs], axis=-1)
            return (jnp.cos(emb), jnp.sin(emb))

        def rotate_half(x):
            x1 = x[..., 0::2]
            x2 = x[..., 1::2]
            return jnp.stack((-x2, x1), axis=-1).reshape(x.shape)

        def rope(t, cos, sin):
            return t * cos[None, None] + rotate_half(t) * sin[None, None]

        def heads(t):
            B, L, C = t.shape
            return t.reshape(B, L, NH, HD).transpose(0, 2, 1, 3)
        e = expert_idx

        def lin(t, W, b):
            return t @ W[e].T + b[e]
        B, T, C = x.shape
        Ka = h_a.shape[1]
        Kt = h_t.shape[1]
        q_a = heads(lin(x, W_qa, b_qa))
        q_t = heads(lin(x, W_qt, b_qt))
        k_a = heads(lin(h_a, W_ka, b_ka))
        v_a = heads(lin(h_a, W_va, b_va))
        k_t = heads(lin(h_t, W_kt, b_kt))
        v_t = heads(lin(h_t, W_vt, b_vt))
        cos_m, sin_m = rope_cos_sin(T, HD)
        q_a = rope(q_a, cos_m, sin_m)
        q_t = rope(q_t, cos_m, sin_m)
        cos_a, sin_a = rope_cos_sin(Ka, HD)
        k_a = rope(k_a, cos_a, sin_a)
        cos_t, sin_t = rope_cos_sin(Kt, HD)
        k_t = rope(k_t, cos_t, sin_t)
        ratio_g = jax.nn.sigmoid(gating_factor[e])
        s_a = jnp.einsum('bhtd,bhkd->bhtk', q_a, k_a)
        s_t = jnp.einsum('bhtd,bhkd->bhtk', q_t, k_t) * ratio_g
        scores = jnp.concatenate([s_a, s_t], axis=-1) / np.sqrt(HD)
        w = jax.nn.softmax(scores, axis=-1)
        v = jnp.concatenate([v_a, v_t], axis=2)
        out = jnp.einsum('bhtk,bhkd->bhtd', w, v)
        out = out.transpose(0, 2, 1, 3).reshape(B, T, C)
        out = lin(out, W_o, b_o)
        x = out + x
        mu = jnp.mean(x, axis=-1, keepdims=True)
        var = jnp.var(x, axis=-1, keepdims=True)
        xn = (x - mu) / jnp.sqrt(var + EPS) * gamma[e] + beta[e]
        x = jax.nn.relu(lin(xn, W_ffn, b_ffn))
        return x

    def _L0_ffn_ref(x, Wqkv, q_scale, k_scale, Wo, ln_g, ln_b, W1, b1, W2, b2):
        import jax, jax.numpy as jnp
        import numpy as np
        DIM = 128
        DEPTH = 6
        HEADS = 16
        DIM_HEAD = 64
        WINDOW = 32
        INNER = HEADS * DIM_HEAD
        DIM_INNER = int(DIM * 4 * 2 / 3)
        QK_SCALE = 8.0

        def shift_tokens(t):
            a, s = jnp.split(t, 2, -1)
            s = jnp.pad(s, ((0, 0), (1, 0), (0, 0)))[:, :-1]
            return jnp.concatenate([a, s], -1)

        def l2norm(t):
            return t / jnp.maximum(jnp.linalg.norm(t, axis=-1, keepdims=True), 1e-12)

        def rotate_half(x):
            x1, x2 = jnp.split(x, 2, -1)
            return jnp.concatenate([-x2, x1], -1)

        def rotary_tables(n):
            half = jnp.arange(0, DIM_HEAD, 2, dtype=jnp.float32)
            inv_freq = 1.0 / 10000.0 ** (half / DIM_HEAD)
            t = jnp.arange(n, dtype=jnp.float32)
            freqs = t[:, None] * inv_freq[None, :]
            freqs = jnp.concatenate([freqs, freqs], -1)
            base_scale = (half + 0.4 * DIM_HEAD) / (1.4 * DIM_HEAD)
            power = (t - n // 2) / (WINDOW // 2)
            scale = base_scale[None, :] ** power[:, None]
            scale = jnp.concatenate([scale, scale], -1)
            return (freqs, scale)

        def local_attention(q, k, v):
            b, h, n, d = q.shape
            w = WINDOW
            nw = n // w
            bq = q.reshape(b, h, nw, w, d)
            bk = k.reshape(b, h, nw, w, d)
            bv = v.reshape(b, h, nw, w, d)

            def look(t):
                p = jnp.pad(t, ((0, 0), (0, 0), (1, 0), (0, 0), (0, 0)))
                return jnp.concatenate([p[:, :, :nw], p[:, :, 1:]], axis=3)
            bk2, bv2 = (look(bk), look(bv))
            seq = jnp.arange(n).reshape(nw, w)
            seq_p = jnp.pad(seq, ((1, 0), (0, 0)), constant_values=-1)
            jt = jnp.concatenate([seq_p[:nw], seq_p[1:]], axis=1)
            it = seq[:, :, None]
            jb = jt[:, None, :]
            mask = (it < jb) | (it > jb + w) | (jb == -1)
            sim = jnp.einsum('bhwie,bhwje->bhwij', bq, bk2) * QK_SCALE
            sim = jnp.where(mask, -jnp.finfo(sim.dtype).max, sim)
            attn = jax.nn.softmax(sim, -1)
            out = jnp.einsum('bhwij,bhwje->bhwie', attn, bv2)
            return out.reshape(b, h, n, d)

        def attn_layer(x, Wqkv, qs, ksc, Wo):
            b, n, _ = x.shape
            qkv = x @ Wqkv
            q, k, v = jnp.split(qkv, 3, -1)
            sh = lambda t: t.reshape(b, n, HEADS, DIM_HEAD).transpose(0, 2, 1, 3)
            q, k, v = (sh(q), sh(k), sh(v))
            q = l2norm(q) * qs
            k = l2norm(k) * ksc
            freqs, scale = rotary_tables(n)
            cos, sin = (jnp.cos(freqs), jnp.sin(freqs))
            q = q * cos * scale + rotate_half(q) * sin * scale
            inv = 1.0 / scale
            k = k * cos * inv + rotate_half(k) * sin * inv
            out = local_attention(q, k, v)
            out = out.transpose(0, 2, 1, 3).reshape(b, n, INNER)
            return out @ Wo

        def ffn_layer(x, g, bln, W1, b1, W2, b2):
            mu = x.mean(-1, keepdims=True)
            var = ((x - mu) ** 2).mean(-1, keepdims=True)
            xn = (x - mu) / jnp.sqrt(var + 1e-05) * g + bln
            hg = xn @ W1 + b1
            a, gate = jnp.split(hg, 2, -1)
            return a * jax.nn.gelu(gate, approximate=False) @ W2 + b2
        for i in range(DEPTH):
            x = attn_layer(shift_tokens(x), Wqkv[i], q_scale[i], k_scale[i], Wo[i]) + x
            x = ffn_layer(shift_tokens(x), ln_g[i], ln_b[i], W1[i], b1[i], W2[i], b2[i]) + x
        return x

    def _L1_attn_ref(hidden_states, w_qkv, b_qkv, w_dense, b_dense):
        import jax, jax.numpy as jnp
        import numpy as np
        HIDDEN = 128
        NUM_HEADS = 16
        HEAD_DIM = HIDDEN // NUM_HEADS
        MASK_BIAS = -10000.0

        def _split_heads(t):
            B, S, _ = t.shape
            return t.reshape(B, S, NUM_HEADS, HEAD_DIM).transpose(0, 2, 1, 3)
        B, S, _ = hidden_states.shape
        kvq = hidden_states @ w_qkv + b_qkv
        k, v, q = jnp.split(kvq, 3, axis=-1)
        q = _split_heads(q) * HEAD_DIM ** (-0.5)
        k = _split_heads(k)
        v = _split_heads(v)
        scores = jnp.einsum('bhqd,bhkd->bhqk', q, k)
        causal = jnp.tril(jnp.ones((S, S), dtype=bool))
        scores = jnp.where(causal[None, None], scores, jnp.asarray(MASK_BIAS, scores.dtype))
        dt = scores.dtype
        attn = jax.nn.softmax(scores.astype(jnp.float32), axis=-1).astype(dt)
        ctx = jnp.einsum('bhqk,bhkd->bhqd', attn, v)
        ctx = ctx.transpose(0, 2, 1, 3).reshape(B, S, HIDDEN)
        return ctx @ w_dense + b_dense

    def _L1_xattn_ref(img_fea, aud_fea, Wq, Wk, Wv, aq, sigmoid, softmax):
        import jax, jax.numpy as jnp
        import numpy as np
        NUM_HEADS = 8

        def _split_heads(x, h):
            b, n, c = x.shape
            return x.reshape(b, n, h, c // h).transpose(0, 2, 1, 3)
        if aq:
            query, key, value = (aud_fea, img_fea, img_fea)
        else:
            query, key, value = (img_fea, aud_fea, aud_fea)
        B, Nq, C = query.shape
        h = NUM_HEADS
        scale = (C // h) ** (-0.5)
        q = _split_heads(query @ Wq.T, h)
        k = _split_heads(key @ Wk.T, h)
        v = _split_heads(value @ Wv.T, h)
        attn = jnp.einsum('bhnd,bhmd->bhnm', q, k) * scale
        if sigmoid:
            attn = jax.nn.sigmoid(attn)
        if softmax:
            attn = jax.nn.softmax(attn, axis=-1)
        x = jnp.einsum('bhnm,bhmd->bhnd', attn, v)
        return x.transpose(0, 2, 1, 3).reshape(B, Nq, C)

    def _L1_ffn_ref(x, gate_w, gate_b, sh_w1, sh_b1, sh_w2, sh_b2, ew1, eb1, ew2, eb2):
        import jax, jax.numpy as jnp
        import numpy as np
        TOP_K = 2

        def _mlp(x, w1, b1, w2, b2):
            h = jax.nn.gelu(jnp.einsum('bsd,di->bsi', x, w1) + b1)
            return jnp.einsum('bsi,id->bsd', h, w2) + b2
        E = ew1.shape[0]
        router_probs = jax.nn.softmax(jnp.einsum('bsd,de->bse', x, gate_w) + gate_b, axis=-1)
        expert_values, expert_indices = jax.lax.top_k(router_probs, k=TOP_K)
        expert_values = expert_values / (jnp.sum(expert_values, axis=-1, keepdims=True) + 1e-09)
        h = jax.nn.gelu(jnp.einsum('bsd,edi->bsei', x, ew1) + eb1)
        all_outputs = jnp.einsum('bsei,eid->bsed', h, ew2) + eb2
        one_hot = jax.nn.one_hot(expert_indices, E, dtype=x.dtype)
        weights_E = (one_hot * expert_values[..., None]).sum(axis=2)
        moe_out = jnp.einsum('bse,bsed->bsd', weights_E, all_outputs)
        return x + _mlp(x, sh_w1, sh_b1, sh_w2, sh_b2) + moe_out
    x = _layernorm(x + _L0_attn_ref(x, L0_attn_Wq, L0_attn_bq, L0_attn_Wk, L0_attn_bk, L0_attn_Wv, L0_attn_bv, L0_attn_temperature), axis=-1)
    x = _layernorm(x + _L0_xattn_ref(x, ctx_1024, ctx_1024, L0_xattn_W_qa, L0_xattn_b_qa, L0_xattn_W_ka, L0_xattn_b_ka, L0_xattn_W_va, L0_xattn_b_va, L0_xattn_W_qt, L0_xattn_b_qt, L0_xattn_W_kt, L0_xattn_b_kt, L0_xattn_W_vt, L0_xattn_b_vt, L0_xattn_W_o, L0_xattn_b_o, L0_xattn_W_ffn, L0_xattn_b_ffn, L0_xattn_gamma, L0_xattn_beta, L0_xattn_gating_factor, 3), axis=-1)
    x = _layernorm(x + _L0_ffn_ref(x, L0_ffn_Wqkv, L0_ffn_q_scale, L0_ffn_k_scale, L0_ffn_Wo, L0_ffn_ln_g, L0_ffn_ln_b, L0_ffn_W1, L0_ffn_b1, L0_ffn_W2, L0_ffn_b2), axis=-1)
    x = _layernorm(x + _L1_attn_ref(x, L1_attn_w_qkv, L1_attn_b_qkv, L1_attn_w_dense, L1_attn_b_dense), axis=-1)
    x = _layernorm(x + _L1_xattn_ref(ctx_1024, x, L1_xattn_Wq, L1_xattn_Wk, L1_xattn_Wv, 1, 0, 1), axis=-1)
    x = _layernorm(x + _L1_ffn_ref(x, L1_ffn_gate_w, L1_ffn_gate_b, L1_ffn_sh_w1, L1_ffn_sh_b1, L1_ffn_sh_w2, L1_ffn_sh_b2, L1_ffn_ew1, L1_ffn_eb1, L1_ffn_ew2, L1_ffn_eb2), axis=-1)
    return x

_drawn_inputs = setup_inputs


def setup_inputs(seed=0):
    import zlib

    import numpy as np

    out = dict(_drawn_inputs(seed))
    spreads = {'L0_attn_temperature': (1.0, 0.6),
     'L0_xattn_gamma': (1.0, 0.2),
     'L0_xattn_beta': (0.0, 0.1),
     'L0_xattn_gating_factor': (0.0, 0.8),
     'L0_ffn_q_scale': (1.0, 0.6),
     'L0_ffn_k_scale': (1.0, 0.6),
     'L0_ffn_ln_g': (1.0, 0.6),
     'L0_ffn_ln_b': (0.0, 0.8),
     'L0_ffn_b1': (0.0, 0.386),
     'L0_ffn_b2': (0.0, 0.1),
     'L1_ffn_gate_b': (0.0, 0.1),
     'L1_ffn_sh_b1': (0.0, 0.275),
     'L1_ffn_sh_b2': (0.0, 0.1),
     'L1_ffn_eb1': (0.0, 0.357),
     'L1_ffn_eb2': (0.0, 0.1)}
    factors = {'L0_attn_Wq': 5.212,
     'L0_attn_bq': 8.0,
     'L0_attn_Wk': 4.826,
     'L0_attn_bk': 8.0,
     'L0_attn_Wv': 4.939,
     'L0_attn_bv': 8.0,
     'L0_xattn_W_qa': 8.0,
     'L0_xattn_b_qa': 8.0,
     'L0_xattn_W_ka': 8.0,
     'L0_xattn_b_ka': 21.661,
     'L0_xattn_W_va': 8.0,
     'L0_xattn_b_va': 24.313,
     'L0_xattn_W_qt': 8.0,
     'L0_xattn_b_qt': 34.978,
     'L0_xattn_W_kt': 8.0,
     'L0_xattn_b_kt': 37.247,
     'L0_xattn_W_vt': 8.0,
     'L0_xattn_b_vt': 34.886,
     'L0_xattn_W_o': 6.186,
     'L0_xattn_b_o': 16.853,
     'L1_xattn_Wq': 5.56,
     'L1_xattn_Wk': 8.0}
    for name, (base, spread) in spreads.items():
        noise = np.random.default_rng([zlib.crc32(name.encode()), seed]).standard_normal(out[name].shape)
        drawn = base * np.exp(spread * noise) if base else spread * noise
        out[name] = jnp.asarray(drawn.astype(out[name].dtype))
    for name, factor in factors.items():
        out[name] = (out[name] * factor).astype(out[name].dtype)
    return out
```

```python
import numpy as np
import concourse.bass as bass
from concourse import mybir
from contextlib import ExitStack

fp32 = mybir.dt.float32
bf16 = mybir.dt.bfloat16
u32 = mybir.dt.uint32
ALU = mybir.AluOpType
ACT = mybir.ActivationFunctionType
AX = mybir.AxisListType

BATCH, T, D = 16, 128, 128
LANES = range(2)
PAIRS = BATCH // 2
EXPERT = 3
DEPTH, LH, LD = 6, 16, 64
INNER = LH * LD
HALF = int(D * 4 * 2 / 3)
HCH = [(c, min(128, HALF - c)) for c in range(0, HALF, 128)]
NE, EI = 8, 512
EPS = 1e-5
TILES = 4
GROUPS = BATCH // TILES


def program(nc, t, out):
    ctx = ExitStack()
    with ctx:
        def sb(name, shape, dt=fp32):
            return ctx.enter_context(nc.sbuf_tensor(name, shape, dt))

        def sem(name):
            return ctx.enter_context(nc.semaphore(name))

        def sems(prefix, names):
            return {n: sem(f"{prefix}_{n}") for n in names.split()}

        x_all = sb("x_all", [T, BATCH, D])
        x_base = sb("x_base", [T, BATCH, D])
        ctx_all = sb("ctx_all", [T, BATCH, D])
        ident = sb("ident", [128, 128])
        ident_bf = sb("ident_bf", [128, 128], bf16)
        shift = sb("shift", [128, 128])
        local_mask = sb("local_mask", [128, 512], bf16)
        causal_mask = sb("causal_mask", [128, 512], bf16)
        ones_row = sb("ones_row", [1, 128])
        const_eps = sb("const_eps", [128, 1])
        const_mhalf = sb("const_mhalf", [128, 2 * LH])
        expert_no = sb("expert_no", [128, TILES, NE])
        a_wkv = sb("a_wkv", [D, 2 * D])
        a_wq = sb("a_wq", [D, D])
        a_bias = sb("a_bias", [1, 3 * D])
        head_mask = sb("head_mask", [128, 4])
        head_temp = sb("head_temp", [128, 1])
        mask_temp = sb("mask_temp", [128, 4])
        xwT = sb("xwT", [D, 11, D])
        x_bias = sb("x_bias", [1, 8 * D])
        x_cos = sb("x_cos", [T, 4 * D])
        x_sin = sb("x_sin", [T, 4 * D])
        gate_col = sb("gate_col", [128, 1])
        gate_e = sb("gate_e", [128, 1])
        gate_1e = sb("gate_1e", [128, 1])
        ratio = sb("ratio", [128, 1])
        x_gamma = sb("x_gamma", [D, 1])
        x_beta = sb("x_beta", [D, 1])
        f_wqkv = sb("f_wqkv", [D, 2, 3 * INNER])
        f_wo = sb("f_wo", [128, 2, INNER // 128, D])
        f_w1 = sb("f_w1", [D, 2, 2 * HALF])
        f_w2 = sb("f_w2", [128, 2, len(HCH), D])
        f_b1 = sb("f_b1", [128, 2, 2, len(HCH)])
        f_ln = sb("f_ln", [D, 2, 2])
        f_b2 = sb("f_b2", [1, 2, D])
        f_scale = sb("f_scale", [T, 2, 2, LD])
        f_cosb = sb("f_cosb", [T, 2, LD])
        f_sinb = sb("f_sinb", [T, 2, LD])
        f_cos = sb("f_cos", [T, 2, 2, LD])
        f_sin = sb("f_sin", [T, 2, 2, LD])
        c_wqkv = sb("c_wqkv", [D, 3 * D])
        c_wd = sb("c_wd", [D, D])
        c_bias = sb("c_bias", [1, 4 * D])
        m_gate = sb("m_gate", [D, NE])
        m_gate_b = sb("m_gate_b", [1, NE])
        m_w1 = sb("m_w1", [D, NE + 1, EI])
        m_b1 = sb("m_b1", [128, NE + 1, EI // 128])
        m_w2 = sb("m_w2", [128, NE + 1, EI // 128, D])
        m_b2 = sb("m_b2", [NE, D])
        m_sb2 = sb("m_sb2", [1, D])

        xl = sb("xl", [T, 2, D])
        cl = sb("cl", [T, 2, D])
        xcT = sb("xcT", [D, 2, 2 * D])
        bufA = sb("bufA", [128, 2, 2048])
        xw_raw = bufA[:, 0, 0:11 * D].rearrange("p (k d) -> p k d", d=D)
        bufB = sb("bufB", [128, 2, 2048])
        bufC = sb("bufC", [128, 2, 2048])
        vals = sb("vals", [128, 2, LH * (LD + 1)])
        pad = sb("pad", [128, 2, 1536])
        res = sb("res", [T, 2, D])
        nrm = sb("nrm", [T, 2, D])
        negmax = sb("negmax", [128, 2, 16])
        bias = sb("bias", [128, 2, 16])
        zsum = sb("zsum", [128, 2, 16])
        rz = sb("rz", [128, 2, 16])
        sumsq = sb("sumsq", [128, 2, 2 * LH])
        sumsq_g = sb("sumsq_g", [128, 2, 2 * LH])
        rnorm = sb("rnorm", [128, 2, 2 * LH])
        st = sb("st", [128, TILES, 6])
        mv = sb("mv", [128, TILES, 2])
        veps = sb("veps", [128, TILES, 1])
        rstd = sb("rstd", [128, TILES, 1])

        nrmT = cl
        idx = bufC[:, 1, 1472:1504].bitcast(u32).rearrange("p (t e) -> p t e", e=NE)

        P = ctx.enter_context(nc.psum_tensor("P", [128, 2, 2048], fp32))

        load = sems("load", "a x c m consts out")
        wt = [sem("layer_weights_even"), sem("layer_weights_odd")]
        setup = sems("setup", "const wT_ps wT temp gate_exp gate_1e ratio fold vals_b pad_c")
        gate_seen = sem("gate_seen")
        norm = sems("norm", "stats mv veps rstd")
        core = sems("core", "scores nb probs probsT probsT_act probsT_dve av rz o oT oT_sb proj")
        a = sems("mix", "x_in xT xT_sb kvq kvq_sb scores nb probs z rz qn oT oT_sb attn sum x1")
        x = sems("xat", "xT xT_sb qkv rope qk v qkT qkT_sb sum yn ynT ynT_sb ffn sum2 x_done")
        f = sems("loc", "x_in xT xT_sb qk sq_q sq_k t12q ss ssg rn kn t1k t2k v v_sb qT qT_sb kT kT_sb negmax x1 tables "
                        "sh xs xn xnT xnT_sb h gl g ffn x_done")
        c = sems("cau", "x_raw x_in xT xT_sb kvq kvq_sb qkT qkT_sb sum x1")
        y = sems("crs", "xT xT_sb qkv qkv_sb qkT qkT_sb sum x_done")
        m = sems("moe", "x2 x_in xT xT_sb logits lg nmax sub ex z rz prob top idx idxf den den_eps rden share hot w wT wT_sb "
                        "h g y acc x_done")

        CORE_B, CORE_C = BATCH, BATCH + DEPTH * BATCH
        NORM_B = 3 * BATCH
        NORM_C = NORM_B + DEPTH * BATCH
        NORM_D = NORM_C + 3 * BATCH

        block = ctx.enter_context(nc.Block())

        BY_ROW_8 = [4 * b + r for r in range(4) for b in range(2)]
        BY_ROW_16 = [4 * b + r for r in range(4) for b in range(4)]
        BY_ROW_LOCAL = [2 * b + r for r in range(2) for b in range(LH // 2)]

        def slots(ap, n, w):
            return ap.rearrange("p (s w) -> p s w", w=w)[:, 0:n, :]

        def cols(ap, n):
            return ap.unsqueeze(2).broadcast_to([ap.shape[0], ap.shape[1], n])

        def one(buf, n):
            return buf[:, bass.ds(n, 1), :].rearrange("p a d -> p (a d)")

        LAYER_DMAS = 8 + 3 * len(HCH)
        N_CONSTS, N_A, N_X, N_C, N_M = 10, 9, 22, 4, 8 + 2 * NE

        @block.sync
        def _(sp):
            for name, dst in [("ident", ident[:]), ("head_mask", head_mask[:]),
                              ("x_cos", x_cos[:]), ("x_sin", x_sin[:]), ("shift", shift[:]),
                              ("local_mask", bufB[:, 0, 0:512]), ("causal_mask", bufB[:, 0, 512:1024]),
                              ("f_cos", f_cosb[:]), ("f_sin", f_sinb[:]), ("expert_no", expert_no[:])]:
                sp.dma_start(dst, t[name]).then_inc(load["consts"], 16)
            sp.dma_start(x_all[:], t["x"].rearrange("b t d -> t b d")).then_inc(load["a"], 16)
            sp.dma_start(ctx_all[:], t["ctx_1024"].rearrange("b t d -> t b d")).then_inc(load["a"], 16)
            for k, wn in enumerate(["Wk", "Wv"]):
                sp.dma_start(a_wkv[:, k * D:(k + 1) * D], t["L0_attn_" + wn]).then_inc(load["a"], 16)
            sp.dma_start(a_wq[:], t["L0_attn_Wq"]).then_inc(load["a"], 16)
            for k, bn in enumerate(["bk", "bv", "bq"]):
                sp.dma_start(a_bias[:, k * D:(k + 1) * D], t["L0_attn_" + bn].unsqueeze(0)).then_inc(load["a"], 16)
            temp = t["L0_attn_temperature"]
            sp.dma_start(head_temp[:], bass.AP(temp.tensor, 0, [[1, 16], [0, 8], [1, 1]])).then_inc(load["a"], 16)
            for k, wn in enumerate(["qa", "qt", "ka", "kt", "va", "vt", "o", "ffn"]):
                sp.dma_start(xw_raw[:, k, :], t["L0_xattn_W_" + wn][EXPERT]).then_inc(load["x"], 16)
                sp.dma_start(x_bias[:, k * D:(k + 1) * D], t["L0_xattn_b_" + wn][EXPERT:EXPERT + 1, :]).then_inc(load["x"], 16)
            for k, wn in enumerate(["Wq", "Wk", "Wv"]):
                sp.dma_start(xw_raw[:, 8 + k, :], t["L1_xattn_" + wn]).then_inc(load["x"], 16)
            sp.dma_start(gate_col[:], t["L0_xattn_gating_factor"][EXPERT:EXPERT + 1].partition_broadcast(128)).then_inc(load["x"], 16)
            sp.dma_start(x_gamma[:], t["L0_xattn_gamma"][EXPERT].unsqueeze(1)).then_inc(load["x"], 16)
            sp.dma_start(x_beta[:], t["L0_xattn_beta"][EXPERT].unsqueeze(1)).then_inc(load["x"], 16)

            def layer(p, L):
                def pick(name):
                    ap = t["L0_ffn_" + name]
                    if isinstance(L, int):
                        return ap[L]
                    ap = ap[bass.ds(L, 1)]
                    return ap.rearrange("a b c -> (a b) c") if len(ap.shape) == 3 else ap.rearrange("a b -> (a b)")
                w2, b1 = pick("W2"), pick("b1")
                moves = [(f_wqkv[:, p, :], pick("Wqkv")),
                         (f_scale[:, p, 0, :], pick("q_scale").partition_broadcast(128)),
                         (f_scale[:, p, 1, :], pick("k_scale").partition_broadcast(128)),
                         (f_wo[:, p], pick("Wo").rearrange("(k p) d -> p k d", p=128)),
                         (f_w1[:, p, :], pick("W1")),
                         (f_ln[:, p, 0:1], pick("ln_g").unsqueeze(1)),
                         (f_ln[:, p, 1:2], pick("ln_b").unsqueeze(1)),
                         (f_b2[:, p, :], pick("b2").unsqueeze(0))]
                for k, (lo, w) in enumerate(HCH):
                    moves.append((f_w2[0:w, p, k, :], w2[lo:lo + w, :]))
                    for s in range(2):
                        moves.append((f_b1[0:w, p, s, k:k + 1], b1[s * HALF + lo:s * HALF + lo + w].unsqueeze(1)))
                for dst, src in moves:
                    sp.dma_start(dst, src).then_inc(wt[p], 16)
                assert len(moves) == LAYER_DMAS

            layer(0, 0)
            layer(1, 1)
            sp.dma_start(c_wqkv[:], t["L1_attn_w_qkv"]).then_inc(load["c"], 16)
            sp.dma_start(c_wd[:], t["L1_attn_w_dense"]).then_inc(load["c"], 16)
            sp.dma_start(c_bias[:, 0:3 * D], t["L1_attn_b_qkv"].unsqueeze(0)).then_inc(load["c"], 16)
            sp.dma_start(c_bias[:, 3 * D:4 * D], t["L1_attn_b_dense"].unsqueeze(0)).then_inc(load["c"], 16)
            sp.dma_start(m_gate[:], t["L1_ffn_gate_w"]).then_inc(load["m"], 16)
            sp.dma_start(m_gate_b[:], t["L1_ffn_gate_b"].unsqueeze(0)).then_inc(load["m"], 16)
            sp.dma_start(m_w1[:, 0:NE, :], t["L1_ffn_ew1"].rearrange("e d i -> d e i")).then_inc(load["m"], 16)
            sp.dma_start(m_w1[:, NE, :], t["L1_ffn_sh_w1"]).then_inc(load["m"], 16)
            sp.dma_start(m_w2[:, NE], t["L1_ffn_sh_w2"].rearrange("(k p) d -> p k d", p=128)).then_inc(load["m"], 16)
            sp.dma_start(m_b1[:, NE, :], t["L1_ffn_sh_b1"].rearrange("(k p) -> p k", p=128), allow_slow_non_contiguous=True).then_inc(load["m"], 16)
            sp.dma_start(m_b2[:], t["L1_ffn_eb2"]).then_inc(load["m"], 16)
            sp.dma_start(m_sb2[:], t["L1_ffn_sh_b2"].unsqueeze(0)).then_inc(load["m"], 16)
            for e in range(NE):
                sp.dma_start(m_w2[:, e], t["L1_ffn_ew2"][e].rearrange("(k p) d -> p k d", p=128)).then_inc(load["m"], 16)
                sp.dma_start(m_b1[:, e, :], t["L1_ffn_eb1"][e].rearrange("(k p) -> p k", p=128), allow_slow_non_contiguous=True).then_inc(load["m"], 16)
            with sp.Fori(0, DEPTH // 2 - 1) as d2:
                for p in range(2):
                    sp.wait_ge(f["x_done"], BATCH * (2 * d2 + p + 1) + 2)
                    layer(p, 2 * d2 + 2 + p)
            with sp.Fori(0, GROUPS) as g:
                sp.wait_ge(m["x_done"], TILES * (g + 1) + 1)
                sp.dma_start(out[bass.ds(g * TILES, TILES)].rearrange("b t d -> t b d"),
                             x_all[:, bass.ds(g * TILES, TILES), :]).then_inc(load["out"], 16)
            sp.wait_ge(load["out"], 16 * GROUPS)


        @block.tensor
        def _(pe):
            def project(dst, lhsT, rhs, bias_row, stop=True):
                pe.matmul(dst, ones_row[:], bias_row, start=True, stop=False, skip_group_check=True)
                return pe.matmul(dst, lhsT, rhs, start=False, stop=stop, skip_group_check=True)

            def transposes(j, src, n, at=0):
                for k in range(n):
                    ins = pe.transpose(P[:, j, (at + k) * 128:(at + k + 1) * 128],
                                       src[:, k * 128:(k + 1) * 128], ident[:])
                return ins

            def attend(cnt, n_blocks, order, per_head, width, slot, o_cols, vcol):
                for j in LANES:
                    pe.wait_ge(core["probs"], cnt(j))
                    transposes(j, bufA[:, j, :], n_blocks).then_inc(core["probsT"], 1)
                for j in LANES:
                    pe.wait_ge(core["probsT_act"], cnt(j))
                    pe.wait_ge(core["probsT_dve"], cnt(j))
                    for n, h in enumerate(order):
                        for k in range(per_head):
                            lo = vcol(h, k)
                            ins = pe.matmul(P[:, j, h * slot:h * slot + width + 1],
                                            bufC[:, j, (n * per_head + k) * 128:(n * per_head + k + 1) * 128],
                                            vals[:, j, lo:lo + width + 1], start=k == 0, stop=k == per_head - 1)
                    ins.then_inc(core["av"], 1)
                if o_cols is None:
                    return
                for j in LANES:
                    pe.wait_ge(core["o"], cnt(j))
                    transposes(j, o_cols(j), len(order) * width // 128).then_inc(core["oT"], 1)

            pe.wait_ge(load["consts"], 16 * N_CONSTS)
            pe.wait_ge(load["x"], 16 * N_X)
            for k in range(11):
                ins = pe.transpose(P[:, 0, k * 128:(k + 1) * 128], xw_raw[:, k, :], ident[:])
            ins.then_inc(setup["wT_ps"], 1)
            pe.wait_ge(setup["const"], 1)
            pe.wait_ge(load["a"], 16 * N_A)
            pe.wait_ge(setup["wT"], 1)

            with pe.Fori(0, PAIRS) as i:
                def cnt(j):
                    return 2 * i + j + 1

                def norm_cnt(k, j):
                    return 6 * i + 2 * k + j + 1
                for j in LANES:
                    pe.wait_ge(a["x_in"], cnt(j))
                    pe.transpose(P[:, j, 0:128], xl[:, j, :], ident[:])
                    pe.transpose(P[:, j, 128:256], cl[:, j, :], ident[:]).then_inc(a["xT"], 1)
                for j in LANES:
                    pe.wait_ge(a["xT_sb"], cnt(j))
                    xT = xcT[:, j, 0:D]
                    project(P[:, j, 0:2 * D], xT, a_wkv[:], a_bias[:, 0:2 * D])
                    pe.matmul(P[:, j, 512:512 + D], a_bias[:, 2 * D:3 * D], ones_row[:], start=True, stop=False)
                    pe.matmul(P[:, j, 512:512 + D], a_wq[:], xT, start=False, stop=True).then_inc(a["kvq"], 1)
                for j in LANES:
                    pe.wait_ge(a["kvq_sb"], cnt(j))
                    for v in range(4):
                        for g in range(4):
                            h = 4 * g + v
                            ins = pe.matmul(P[:, j, h * 128:(h + 1) * 128],
                                            bufA[32 * g:32 * g + 32, j, v * 128:(v + 1) * 128],
                                            bufA[32 * g:32 * g + 32, j, 512:640], start=True, stop=True)
                    ins.then_inc(a["scores"], 1)
                for j in LANES:
                    pe.wait_ge(a["probs"], cnt(j))
                    pe.wait_ge(a["qn"], cnt(j))
                    for h in range(16):
                        ins = pe.matmul(P[:, j, 8 * h:8 * h + 8], bufB[:, j, h * 128:(h + 1) * 128],
                                        bufA[:, j, 768 + 8 * h:768 + 8 * h + 8], start=True, stop=True)
                    ins.then_inc(a["oT"], 1)
                for j in LANES:
                    pe.wait_ge(a["oT_sb"], cnt(j))
                    pe.transpose(P[:, j, 0:128], bufC[:, j, 0:128], ident[:]).then_inc(a["attn"], 1)
                for j in LANES:
                    pe.wait_ge(a["x1"], cnt(j))
                    pe.transpose(P[:, j, 0:128], xl[:, j, :], ident[:]).then_inc(x["xT"], 1)
                for j in LANES:
                    pe.wait_ge(x["xT_sb"], cnt(j))
                    xT, cT = xcT[:, j, 0:D], xcT[:, j, D:2 * D]
                    w = xwT[:, 0:6, :].rearrange("p k d -> p (k d)")
                    pe.matmul(P[:, j, 0:512], ones_row[:], x_bias[:, 0:512], start=True, stop=False, skip_group_check=True)
                    pe.matmul(P[:, j, 0:256], xT, w[:, 0:256], start=False, stop=False, skip_group_check=True)
                    pe.matmul(P[:, j, 256:512], cT, w[:, 256:512], start=False, stop=True, skip_group_check=True)
                    project(P[:, j, 512:768], cT, w[:, 512:768], x_bias[:, 512:768]).then_inc(x["qkv"], 1)
                for j in LANES:
                    pe.wait_ge(x["qk"], cnt(j))
                    pe.wait_ge(x["v"], cnt(j))
                    transposes(j, pad[:, j, :], 8).then_inc(x["qkT"], 1)
                for j in LANES:
                    pe.wait_ge(x["qkT_sb"], cnt(j))
                    for k in range(2):
                        for c4 in range(2):
                            for r in range(4):
                                at = r * 512 + c4 * 256 + k * 128
                                q = (2 * k + c4) * 128
                                ins = pe.matmul(P[:, j, at:at + 128],
                                                bufB[32 * r:32 * r + 32, j, q:q + 128],
                                                bufB[32 * r:32 * r + 32, j, 512 + q:512 + q + 128], start=True, stop=True)
                    ins.then_inc(core["scores"], 1)
                attend(cnt, 16, BY_ROW_8, 2, 16, 32, lambda j: bufB[:, j, 1024:1152], lambda h, k: (8 * k + h) * 17)
                for j in LANES:
                    pe.wait_ge(core["oT_sb"], cnt(j))
                    project(P[:, j, 0:128], bufB[:, j, 1152:1280], xwT[:, 6, :], x_bias[:, 768:896]).then_inc(core["proj"], 1)
                for j in LANES:
                    pe.wait_ge(x["yn"], cnt(j))
                    pe.transpose(P[:, j, 0:128], nrm[:, j, :], ident[:]).then_inc(x["ynT"], 1)
                for j in LANES:
                    pe.wait_ge(x["ynT_sb"], cnt(j))
                    project(P[:, j, 0:128], nrmT[:, j, :], xwT[:, 7, :], x_bias[:, 896:1024]).then_inc(x["ffn"], 1)

            with pe.Fori(0, DEPTH // 2) as d2:
                for p in range(2):
                    pe.wait_ge(wt[p], 16 * LAYER_DMAS * (d2 + 1))
                    pe.sem_inc(gate_seen, 1)
                    with pe.Fori(0, PAIRS) as i:
                        def cnt(j):
                            return (2 * d2 + p) * BATCH + 2 * i + j + 1

                        def core_cnt(j):
                            return CORE_B + cnt(j)
                        for j in LANES:
                            pe.wait_ge(f["x_in"], cnt(j))
                            pe.transpose(P[:, j, 0:128], xl[:, j, :], ident[:]).then_inc(f["xT"], 1)
                        for j in LANES:
                            pe.wait_ge(f["xT_sb"], cnt(j))
                            for k in range(4):
                                ins = pe.matmul(P[:, j, k * 512:(k + 1) * 512], xcT[:, j, 0:D],
                                                f_wqkv[:, p, k * 512:(k + 1) * 512], start=True, stop=True)
                            ins.then_inc(f["qk"], 1)
                        for j in LANES:
                            pe.wait_ge(f["t1k"], cnt(j))
                            for k in range(2):
                                ins = pe.matmul(P[:, j, k * 512:(k + 1) * 512], xcT[:, j, 0:D],
                                                f_wqkv[:, p, (4 + k) * 512:(5 + k) * 512], start=True, stop=True)
                            ins.then_inc(f["v"], 1)

                        def rotated(j, lo):
                            for k in range(8):
                                at = lo + k * 128
                                pe.matmul(P[:, j, at:at + 128], bufA[:, j, at:at + 128], ident[:],
                                          is_transpose=True, start=True, stop=False)
                                ins = pe.matmul(P[:, j, at:at + 128], bufC[:, j, at:at + 128], ident[:],
                                                is_transpose=True, start=False, stop=True)
                            return ins
                        for j in LANES:
                            pe.wait_ge(f["t2k"], cnt(j))
                            rotated(j, 1024).then_inc(f["kT"], 1)
                            pe.wait_ge(f["v_sb"], cnt(j))
                            rotated(j, 0).then_inc(f["qT"], 1)
                        for j in LANES:
                            pe.wait_ge(f["kT_sb"], cnt(j))
                            pe.wait_ge(f["qT_sb"], cnt(j))
                            for b in range(4):
                                pe.matmul(P[:, j, b * 512:(b + 1) * 512], ident_bf[:], local_mask[:],
                                          start=True, stop=False, skip_group_check=True)
                            for s in (0, 8, 1, 9, 2, 10, 3, 11, 4, 12, 5, 13, 6, 14, 7, 15):
                                r, at = 64 * (s // 8), s % 8 * 128
                                ins = pe.matmul(P[:, j, s * 128:(s + 1) * 128], bufB[r:r + 64, j, at:at + 128],
                                                bufB[r:r + 64, j, 1024 + at:1024 + at + 128],
                                                start=False, stop=s % 4 == 3, skip_group_check=True)
                            ins.then_inc(core["scores"], 1)
                        attend(core_cnt, 16, BY_ROW_LOCAL, 1, LD, 128, lambda j: bufB[:, j, 0:INNER], lambda h, k: h * (LD + 1))
                        for j in LANES:
                            pe.wait_ge(core["oT_sb"], core_cnt(j))
                            for k in range(INNER // 128):
                                ins = pe.matmul(P[:, j, 0:128], bufB[:, j, INNER + k * 128:INNER + (k + 1) * 128],
                                                f_wo[:, p, k, :], start=k == 0, stop=k == INNER // 128 - 1)
                            ins.then_inc(core["proj"], 1)
                        for j in LANES:
                            pe.wait_ge(f["x1"], cnt(j))
                            pe.matmul(P[:, j, 0:64], shift[:], xl[:, j, 64:128], start=True, stop=True).then_inc(f["sh"], 1)
                        for j in LANES:
                            pe.wait_ge(f["xn"], cnt(j))
                            pe.transpose(P[:, j, 0:128], nrm[:, j, :], ident[:]).then_inc(f["xnT"], 1)
                        for j in LANES:
                            pe.wait_ge(f["xnT_sb"], cnt(j))
                            for s in range(2):
                                for k, (lo, w) in enumerate(HCH):
                                    at = s * 512 + k * 128
                                    ins = pe.matmul(P[0:w, j, at:at + 128], f_w1[:, p, s * HALF + lo:s * HALF + lo + w],
                                                    nrmT[:, j, :], start=True, stop=True)
                            ins.then_inc(f["h"], 1)
                        for j in LANES:
                            pe.wait_ge(f["g"], cnt(j))
                            pe.matmul(P[:, j, 0:128], ones_row[:], f_b2[:, p, :], start=True, stop=False)
                            for k, (lo, w) in enumerate(HCH):
                                ins = pe.matmul(P[:, j, 0:128], bufA[0:w, j, 512 + k * 128:512 + (k + 1) * 128],
                                                f_w2[0:w, p, k, :], start=False, stop=k == len(HCH) - 1)
                            ins.then_inc(f["ffn"], 1)

            pe.wait_ge(load["c"], 16 * N_C)
            with pe.Fori(0, PAIRS) as i:
                def cnt(j):
                    return 2 * i + j + 1

                def cau_cnt(j):
                    return CORE_C + 4 * i + j + 1

                def crs_cnt(j):
                    return CORE_C + 4 * i + 2 + j + 1

                def norm_cnt(k, j):
                    return NORM_C + 6 * i + 2 * k + j + 1
                for j in LANES:
                    pe.wait_ge(c["x_in"], cnt(j))
                    pe.transpose(P[:, j, 0:128], xl[:, j, :], ident[:])
                    pe.transpose(P[:, j, 128:256], cl[:, j, :], ident[:]).then_inc(c["xT"], 1)
                for j in LANES:
                    pe.wait_ge(c["xT_sb"], cnt(j))
                    project(P[:, j, 0:384], xcT[:, j, 0:D], c_wqkv[:], c_bias[:, 0:384]).then_inc(c["kvq"], 1)
                for j in LANES:
                    pe.wait_ge(c["kvq_sb"], cnt(j))
                    transposes(j, pad[:, j, :], 8).then_inc(c["qkT"], 1)
                for j in LANES:
                    pe.wait_ge(c["qkT_sb"], cnt(j))
                    for b in range(4):
                        pe.matmul(P[:, j, b * 512:(b + 1) * 512], ident_bf[:], causal_mask[:],
                                  start=True, stop=False, skip_group_check=True)
                    for b in range(4):
                        for r in range(4):
                            at = r * 512 + b * 128
                            ins = pe.matmul(P[:, j, at:at + 128], bufB[32 * r:32 * r + 32, j, b * 128:(b + 1) * 128],
                                            bufB[32 * r:32 * r + 32, j, 512 + b * 128:512 + (b + 1) * 128],
                                            start=False, stop=b == 3, skip_group_check=True)
                    ins.then_inc(core["scores"], 1)
                attend(cau_cnt, 16, BY_ROW_16, 1, 8, 16, lambda j: bufB[:, j, 1024:1152], lambda h, k: h * 9)
                for j in LANES:
                    pe.wait_ge(core["oT_sb"], CORE_C + cnt(j))
                    project(P[:, j, 0:128], bufB[:, j, 1152:1280], c_wd[:], c_bias[:, 384:512]).then_inc(core["proj"], 1)
                for j in LANES:
                    pe.wait_ge(c["x1"], cnt(j))
                    pe.transpose(P[:, j, 0:128], xl[:, j, :], ident[:]).then_inc(y["xT"], 1)
                for j in LANES:
                    pe.wait_ge(y["xT_sb"], cnt(j))
                    w = xwT[:, 8:11, :].rearrange("p k d -> p (k d)")
                    pe.matmul(P[:, j, 0:128], xcT[:, j, 0:D], w[:, 0:128], start=True, stop=True)
                    pe.matmul(P[:, j, 128:384], xcT[:, j, D:2 * D], w[:, 128:384], start=True, stop=True).then_inc(y["qkv"], 1)
                for j in LANES:
                    pe.wait_ge(y["qkv_sb"], cnt(j))
                    transposes(j, pad[:, j, 1024:1536], 4).then_inc(y["qkT"], 1)
                for j in LANES:
                    pe.wait_ge(y["qkT_sb"], cnt(j))
                    for b in range(2):
                        for r in range(4):
                            at = r * 512 + b * 128
                            ins = pe.matmul(P[:, j, at:at + 128], bufB[32 * r:32 * r + 32, j, b * 128:(b + 1) * 128],
                                            bufB[32 * r:32 * r + 32, j, 256 + b * 128:256 + (b + 1) * 128], start=True, stop=True)
                    ins.then_inc(core["scores"], 1)
                attend(crs_cnt, 8, BY_ROW_8, 1, 16, 32, None, lambda h, k: 256 + h * 17)

            pe.wait_ge(load["m"], 16 * N_M)
            with pe.Fori(0, GROUPS) as g:
                pe.wait_ge(m["x_in"], g + 1)
                for k in range(TILES):
                    ins = pe.transpose(P[:, 0, k * 128:(k + 1) * 128], bufC[:, 0, k * 128:(k + 1) * 128], ident[:])
                ins.then_inc(m["xT"], 1)
                pe.wait_ge(m["xT_sb"], g + 1)
                xT = bufC[:, 0, 512:1024]
                for k in range(TILES):
                    ins = project(P[:, 1, k * NE:(k + 1) * NE], xT[:, k * 128:(k + 1) * 128], m_gate[:], m_gate_b[:])
                ins.then_inc(m["logits"], 1)

                def inner(e):
                    for k in range(EI // 128):
                        turn = e * (EI // 128) + k
                        if turn >= 4:
                            pe.wait_ge(m["g"], g * 36 + turn - 3)
                        pe.matmul(P[:, 0, k * 512:(k + 1) * 512], m_w1[:, e, k * 128:(k + 1) * 128], xT,
                                  start=True, stop=True).then_inc(m["h"], 1)

                def outer(e):
                    pe.wait_ge(m["g"], g * 36 + 4 * e + 4)
                    if e >= 4:
                        pe.wait_ge(m["acc"], g * (NE + 1) + e - 3)
                    bank = P[:, 1, (e % 4) * 512:(e % 4 + 1) * 512]
                    src = (bufA, bufB)[e % 2]
                    for q in range(TILES):
                        dst = bank[:, q * 128:(q + 1) * 128]
                        if e == NE:
                            pe.matmul(dst, ones_row[:], m_sb2[:], start=True, stop=False)
                            pe.matmul(dst, bufC[0:NE, 1, q * 128:(q + 1) * 128], m_b2[:], start=False, stop=False)
                        for k in range(EI // 128):
                            ins = pe.matmul(dst, src[:, 0, k * 512 + q * 128:k * 512 + (q + 1) * 128], m_w2[:, e, k, :],
                                            start=e < NE and k == 0, stop=k == EI // 128 - 1)
                    ins.then_inc(m["y"], 1)

                inner(0)
                pe.wait_ge(m["w"], g + 1)
                for k in range(TILES):
                    ins = pe.transpose(P[0:NE, 1, 1536 + k * 128:1536 + (k + 1) * 128], bufC[:, 1, 1024 + k * NE:1024 + (k + 1) * NE], ident[:])
                ins.then_inc(m["wT"], 1)
                pe.wait_ge(m["wT_sb"], g + 1)
                for e in range(NE + 1):
                    if e < NE:
                        inner(e + 1)
                    outer(e)

        @block.vector
        def _(dve):
            def hold():
                dve.sem_inc(gate_seen, 1)

            def moments(cnt, src, k):
                dve.bn_stats(st[:, k, :], src).then_inc(norm["stats"], 1)
                dve.wait_ge(norm["stats"], cnt)
                hold()
                dve.bn_aggr(mv[:, k, :], st[:, k, :]).then_inc(norm["mv"], 1)

            def normalise(cnt, dst, src, k):
                dve.wait_ge(norm["rstd"], cnt)
                return dve.tensor_scalar(dst, src, mv[:, k, 0:1], rstd[:, k, :], ALU.subtract, ALU.mult)

            def row_max(s, cnt, heads, keys):
                for j in LANES:
                    dve.wait_ge(s["scores"], cnt(j))
                    dve.tensor_reduce(bias[:, j, 0:heads], slots(P[:, j, :], heads, keys), AX.X, ALU.max,
                                      negate=True).then_inc(s["nb"], 1)

            def probs_half(cnt, n):
                for j in LANES:
                    dve.wait_ge(core["probsT"], cnt(j))
                    dve.tensor_copy(bufC[:, j, n:2 * n], P[:, j, n:2 * n]).then_inc(core["probsT_dve"], 1)

            def heads_out(cnt, heads, width, slot, dst):
                for j in LANES:
                    dve.wait_ge(core["av"], cnt(j))
                    o = slots(P[:, j, :], heads, slot)
                    dve.reciprocal(rz[:, j, 0:heads], o[:, :, width]).then_inc(core["rz"], 1)
                    dve.wait_ge(core["rz"], cnt(j))
                    dve.tensor_tensor(dst(j).rearrange("p (h w) -> p h w", w=width), o[:, :, 0:width],
                                      cols(rz[:, j, 0:heads], width), ALU.mult).then_inc(core["o"], 1)

            dve.memset(ones_row[:], 1.0)
            dve.memset(const_eps[:], EPS)
            dve.memset(const_mhalf[:], -0.5)
            dve.memset(vals[:], 1.0)
            dve.memset(pad[:], 0.0).then_inc(setup["const"], 1)
            dve.sem_inc(x["x_done"], 2)
            dve.sem_inc(f["x_done"], 2)
            dve.sem_inc(y["x_done"], 2)
            dve.sem_inc(m["x_done"], 1)
            dve.wait_ge(load["consts"], 16 * N_CONSTS)
            dve.wait_ge(load["a"], 16 * N_A)
            dve.tensor_copy(local_mask[:], bufB[:, 0, 0:512])
            dve.tensor_copy(causal_mask[:], bufB[:, 0, 512:1024])
            dve.tensor_copy(ident_bf[:], ident[:])
            dve.tensor_scalar(mask_temp[:], head_mask[:], head_temp[:, 0:1], None, ALU.mult).then_inc(setup["temp"], 1)
            dve.wait_ge(setup["gate_exp"], 1)
            dve.tensor_scalar(gate_1e[:], gate_e[:], 1.0, None, ALU.add).then_inc(setup["gate_1e"], 1)
            dve.wait_ge(setup["gate_1e"], 1)
            dve.reciprocal(ratio[:], gate_1e[:]).then_inc(setup["ratio"], 1)
            dve.wait_ge(setup["ratio"], 1)
            dve.tensor_scalar(x_cos[:, D:2 * D], x_cos[:, D:2 * D], ratio[:, 0:1], None, ALU.mult)
            dve.tensor_scalar(x_sin[:, D:2 * D], x_sin[:, D:2 * D], ratio[:, 0:1], None, ALU.mult).then_inc(setup["fold"], 1)
            dve.wait_ge(setup["fold"], 1)
            dve.wait_ge(setup["wT_ps"], 1)
            dve.tensor_copy(xwT[:].rearrange("p k d -> p (k d)"), P[:, 0, 0:11 * 128]).then_inc(setup["wT"], 1)

            with dve.Fori(0, PAIRS) as i:
                def cnt(j):
                    return 2 * i + j + 1

                def norm_cnt(k, j):
                    return 6 * i + 2 * k + j + 1
                for j in LANES:
                    dve.wait_ge(x["x_done"], cnt(j))
                    dve.tensor_scalar(xl[:, j, :], one(x_all, 2 * i + j), 1.0, None, ALU.mult)
                    dve.tensor_scalar(cl[:, j, :], one(ctx_all, 2 * i + j), 1.0, None, ALU.mult).then_inc(a["x_in"], 1)
                for j in LANES:
                    dve.wait_ge(a["xT"], cnt(j))
                    dve.tensor_copy(xcT[:, j, :], P[:, j, 0:256]).then_inc(a["xT_sb"], 1)
                row_max(a, cnt, 16, 128)
                for j in LANES:
                    dve.wait_ge(a["probs"], cnt(j))
                    dve.tensor_reduce(zsum[:, j, :], slots(bufB[:, j, :], 16, 128), AX.X, ALU.add).then_inc(a["z"], 1)
                    dve.wait_ge(a["z"], cnt(j))
                    dve.reciprocal(rz[:, j, :], zsum[:, j, :]).then_inc(a["rz"], 1)
                    dve.wait_ge(a["rz"], cnt(j))
                    dve.tensor_tensor(slots(bufA[:, j, 768:896], 16, 8), slots(bufA[:, j, 640:768], 16, 8),
                                      cols(rz[:, j, :], 8), ALU.mult).then_inc(a["qn"], 1)
                for j in LANES:
                    dve.wait_ge(a["oT"], cnt(j))
                    dve.tensor_copy(bufC[:, j, 0:128], P[:, j, 0:128]).then_inc(a["oT_sb"], 1)
                for j in LANES:
                    dve.wait_ge(a["attn"], cnt(j))
                    dve.tensor_tensor(res[:, j, :], P[:, j, 0:128], xl[:, j, :], ALU.add).then_inc(a["sum"], 1)
                    dve.wait_ge(a["sum"], cnt(j))
                    moments(norm_cnt(0, j), res[:, j, :], j)
                for j in LANES:
                    normalise(norm_cnt(0, j), xl[:, j, :], res[:, j, :], j).then_inc(a["x1"], 1)
                for j in LANES:
                    dve.wait_ge(x["xT"], cnt(j))
                    dve.tensor_copy(xcT[:, j, 0:D], P[:, j, 0:D]).then_inc(x["xT_sb"], 1)
                for j in LANES:
                    dve.wait_ge(x["qkv"], cnt(j))
                    qk = P[:, j, 0:512].rearrange("p (s two) -> p s two", two=2)
                    t2 = bufA[:, j, 512:1024].rearrange("p (s two) -> p s two", two=2)
                    sn = x_sin[:].rearrange("p (s two) -> p s two", two=2)
                    dve.tensor_tensor(bufA[:, j, 0:512], P[:, j, 0:512], x_cos[:], ALU.mult)
                    for s in range(2):
                        ins = dve.tensor_tensor(t2[:, :, s], qk[:, :, 1 - s], sn[:, :, s], ALU.mult)
                    ins.then_inc(x["rope"], 1)
                    dve.wait_ge(x["rope"], cnt(j))
                    dve.tensor_tensor(slots(pad[:, j, 0:1024], 32, 32)[:, :, 0:16], slots(bufA[:, j, 0:512], 32, 16),
                                      slots(bufA[:, j, 512:1024], 32, 16), ALU.add).then_inc(x["qk"], 1)
                row_max(core, cnt, 8, 256)
                probs_half(cnt, 1024)
                heads_out(cnt, 8, 16, 32, lambda j: bufB[:, j, 1024:1152])
                for j in LANES:
                    dve.wait_ge(core["oT"], cnt(j))
                    dve.tensor_copy(bufB[:, j, 1152:1280], P[:, j, 0:128]).then_inc(core["oT_sb"], 1)
                for j in LANES:
                    dve.wait_ge(core["proj"], cnt(j))
                    dve.tensor_tensor(res[:, j, :], P[:, j, 0:128], xl[:, j, :], ALU.add).then_inc(x["sum"], 1)
                    dve.wait_ge(x["sum"], cnt(j))
                    moments(norm_cnt(1, j), res[:, j, :], j)
                for j in LANES:
                    normalise(norm_cnt(1, j), nrm[:, j, :], res[:, j, :], j).then_inc(x["yn"], 1)
                for j in LANES:
                    dve.wait_ge(x["ynT"], cnt(j))
                    dve.tensor_scalar(nrmT[:, j, :], P[:, j, 0:128], x_gamma[:, 0:1], x_beta[:, 0:1],
                                      ALU.mult, ALU.add).then_inc(x["ynT_sb"], 1)
                for j in LANES:
                    dve.wait_ge(x["ffn"], cnt(j))
                    dve.scalar_tensor_tensor(res[:, j, :], P[:, j, 0:128], 0.0, xl[:, j, :], ALU.max, ALU.add).then_inc(x["sum2"], 1)
                    dve.wait_ge(x["sum2"], cnt(j))
                    moments(norm_cnt(2, j), res[:, j, :], j)
                for j in LANES:
                    normalise(norm_cnt(2, j), one(x_all, 2 * i + j), res[:, j, :], j).then_inc(x["x_done"], 1)

            dve.wait_ge(x["x_done"], BATCH + 2)
            dve.tensor_copy(x_base[:], x_all[:])
            dve.memset(vals[:], 1.0)
            dve.memset(xcT[64:128, :, 0:1], 0.0).then_inc(setup["vals_b"], 1)
            dve.wait_ge(setup["vals_b"], 1)
            with dve.Fori(0, DEPTH // 2) as d2:
                for p in range(2):
                    dve.wait_ge(wt[p], 16 * LAYER_DMAS * (d2 + 1))
                    dve.wait_ge(f["x_done"], (2 * d2 + p) * BATCH + 2)
                    dve.tensor_tensor(f_cos[:, p], f_cosb[:], f_scale[:, p], ALU.mult)
                    for s in range(2):
                        ins = dve.tensor_tensor(f_sin[:, p, :, 32 * s:32 * s + 32], f_sinb[:, :, 32 * s:32 * s + 32],
                                                f_scale[:, p, :, 32 - 32 * s:64 - 32 * s], ALU.mult)
                    ins.then_inc(f["tables"], 1)
                    dve.wait_ge(f["tables"], 2 * d2 + p + 1)
                    hold()
                    with dve.Fori(0, PAIRS) as i:
                        def cnt(j):
                            return (2 * d2 + p) * BATCH + 2 * i + j + 1

                        def core_cnt(j):
                            return CORE_B + cnt(j)

                        def heads(ap):
                            return ap.rearrange("p (h w) -> p h w", w=LD)

                        def table(tab, k, lo, w):
                            return tab[:, p, k, lo:lo + w].unsqueeze(1).broadcast_to([T, LH, w])
                        for j in LANES:
                            dve.wait_ge(f["x_done"], cnt(j))
                            dve.tensor_scalar(xl[:, j, :], one(x_all, 2 * i + j), 1.0, None, ALU.mult).then_inc(f["x_in"], 1)
                        for j in LANES:
                            dve.wait_ge(f["xT"], cnt(j))
                            dve.tensor_copy(xcT[0:64, j, 0:T], P[0:64, j, 0:T])
                            dve.tensor_copy(xcT[64:128, j, 1:T], P[64:128, j, 0:T - 1]).then_inc(f["xT_sb"], 1)
                        for j in LANES:
                            dve.wait_ge(f["sq_q"], cnt(j))
                            q = heads(P[:, j, 0:INNER])
                            dve.tensor_tensor(heads(bufA[:, j, 0:INNER]), q, table(f_cos, 0, 0, LD), ALU.mult)
                            t2 = heads(bufC[:, j, 0:INNER])
                            for s in range(2):
                                ins = dve.tensor_tensor(t2[:, :, 32 * s:32 * s + 32], q[:, :, 32 - 32 * s:64 - 32 * s],
                                                        table(f_sin, 0, 32 * s, 32), ALU.mult)
                            ins.then_inc(f["t12q"], 1)
                            dve.wait_ge(f["sq_k"], cnt(j))
                            dve.tensor_reduce(sumsq[:, j, :], slots(bufB[:, j, :], 2 * LH, LD), AX.X, ALU.add).then_inc(f["ss"], 1)
                            dve.wait_ge(f["ss"], cnt(j))
                            dve.tensor_scalar(sumsq_g[:, j, :], sumsq[:, j, :], 1e-24, None, ALU.max).then_inc(f["ssg"], 1)
                        for j in LANES:
                            dve.wait_ge(f["rn"], cnt(j))
                            kn = heads(bufB[:, j, 0:INNER])
                            dve.tensor_tensor(kn, heads(P[:, j, INNER:2 * INNER]), cols(rnorm[:, j, LH:], LD),
                                              ALU.mult).then_inc(f["kn"], 1)
                            dve.wait_ge(f["kn"], cnt(j))
                            dve.tensor_tensor(heads(bufA[:, j, INNER:2 * INNER]), kn, table(f_cos, 1, 0, LD),
                                              ALU.mult).then_inc(f["t1k"], 1)
                        for j in LANES:
                            dve.wait_ge(core["scores"], core_cnt(j))
                            dve.tensor_reduce(negmax[:, j, :], slots(P[:, j, :], LH, 128), AX.X, ALU.max,
                                              negate=True).then_inc(f["negmax"], 1)
                            dve.wait_ge(f["negmax"], cnt(j))
                            dve.tensor_tensor(bias[:, j, :].rearrange("p (r b) -> p r b", r=2), negmax[:, j, :].rearrange("p (r b) -> p r b", r=2),
                                              rnorm[:, j, 0:LH].rearrange("p (b r) -> p r b", r=2), ALU.mult).then_inc(core["nb"], 1)
                        probs_half(core_cnt, 1024)
                        heads_out(core_cnt, LH, LD, 128, lambda j: bufB[:, j, 0:INNER])
                        for j in LANES:
                            dve.wait_ge(core["proj"], core_cnt(j))
                            dve.tensor_tensor(xl[:, j, :], P[:, j, 0:128], xl[:, j, :], ALU.add).then_inc(f["x1"], 1)
                        for j in LANES:
                            dve.wait_ge(f["x1"], cnt(j))
                            dve.tensor_copy(res[:, j, 0:64], xl[:, j, 0:64])
                            dve.wait_ge(f["sh"], cnt(j))
                            dve.tensor_copy(res[:, j, 64:128], P[:, j, 0:64]).then_inc(f["xs"], 1)
                            dve.wait_ge(f["xs"], cnt(j))
                            moments(NORM_B + cnt(j), res[:, j, :], j)
                        for j in LANES:
                            normalise(NORM_B + cnt(j), nrm[:, j, :], res[:, j, :], j).then_inc(f["xn"], 1)
                        for j in LANES:
                            dve.wait_ge(f["xnT"], cnt(j))
                            dve.tensor_scalar(nrmT[:, j, :], P[:, j, 0:128], f_ln[:, p, 0:1], f_ln[:, p, 1:2],
                                              ALU.mult, ALU.add).then_inc(f["xnT_sb"], 1)
                        for j in LANES:
                            dve.wait_ge(f["gl"], cnt(j))
                            for k, (lo, w) in enumerate(HCH):
                                ins = dve.scalar_tensor_tensor(bufA[0:w, j, 512 + k * 128:512 + (k + 1) * 128],
                                                               P[0:w, j, k * 128:(k + 1) * 128], f_b1[0:w, p, 0, k:k + 1],
                                                               bufA[0:w, j, k * 128:(k + 1) * 128], ALU.add, ALU.mult)
                            ins.then_inc(f["g"], 1)
                        for j in LANES:
                            dve.wait_ge(f["ffn"], cnt(j))
                            dve.tensor_tensor(one(x_all, 2 * i + j), P[:, j, 0:128], xl[:, j, :], ALU.add).then_inc(f["x_done"], 1)

            dve.wait_ge(f["x_done"], DEPTH * BATCH + 2)
            dve.memset(vals[:], 1.0)
            dve.memset(pad[:], 0.0).then_inc(setup["pad_c"], 1)
            dve.wait_ge(setup["pad_c"], 1)


            with dve.Fori(0, PAIRS) as i:
                def cnt(j):
                    return 2 * i + j + 1

                def cau_cnt(j):
                    return CORE_C + 4 * i + j + 1

                def crs_cnt(j):
                    return CORE_C + 4 * i + 2 + j + 1

                def norm_cnt(k, j):
                    return NORM_C + 6 * i + 2 * k + j + 1
                for j in LANES:
                    dve.wait_ge(y["x_done"], cnt(j))
                    dve.tensor_scalar(cl[:, j, :], one(ctx_all, 2 * i + j), 1.0, None, ALU.mult)
                    dve.tensor_tensor(res[:, j, :], one(x_all, 2 * i + j), one(x_base, 2 * i + j), ALU.add).then_inc(c["x_raw"], 1)
                    dve.wait_ge(c["x_raw"], cnt(j))
                    moments(norm_cnt(0, j), res[:, j, :], j)
                for j in LANES:
                    normalise(norm_cnt(0, j), xl[:, j, :], res[:, j, :], j).then_inc(c["x_in"], 1)
                for j in LANES:
                    dve.wait_ge(c["xT"], cnt(j))
                    dve.tensor_copy(xcT[:, j, :], P[:, j, 0:256]).then_inc(c["xT_sb"], 1)
                row_max(core, cau_cnt, 16, 128)
                probs_half(cau_cnt, 1024)
                heads_out(cau_cnt, 16, 8, 16, lambda j: bufB[:, j, 1024:1152])
                for j in LANES:
                    dve.wait_ge(core["oT"], CORE_C + cnt(j))
                    dve.tensor_copy(bufB[:, j, 1152:1280], P[:, j, 0:128]).then_inc(core["oT_sb"], 1)
                for j in LANES:
                    dve.wait_ge(core["proj"], CORE_C + cnt(j))
                    dve.tensor_tensor(res[:, j, :], P[:, j, 0:128], xl[:, j, :], ALU.add).then_inc(c["sum"], 1)
                    dve.wait_ge(c["sum"], cnt(j))
                    moments(norm_cnt(1, j), res[:, j, :], j)
                for j in LANES:
                    normalise(norm_cnt(1, j), xl[:, j, :], res[:, j, :], j).then_inc(c["x1"], 1)
                for j in LANES:
                    dve.wait_ge(y["xT"], cnt(j))
                    dve.tensor_copy(xcT[:, j, 0:D], P[:, j, 0:D]).then_inc(y["xT_sb"], 1)
                for j in LANES:
                    dve.wait_ge(core["scores"], crs_cnt(j))
                    dve.tensor_reduce(bias[:, j, 0:8].rearrange("p (r b) -> p r b", b=2),
                                      P[:, j, :].rearrange("p (r b k) -> p r b k", b=4, k=128)[:, :, 0:2, :], AX.X, ALU.max,
                                      negate=True).then_inc(core["nb"], 1)
                probs_half(crs_cnt, 512)
                heads_out(crs_cnt, 8, 16, 32, lambda j: bufB[:, j, 1024:1152])
                for j in LANES:
                    dve.wait_ge(core["o"], crs_cnt(j))
                    dve.tensor_tensor(res[:, j, :], bufB[:, j, 1024:1152], xl[:, j, :], ALU.add).then_inc(y["sum"], 1)
                    dve.wait_ge(y["sum"], cnt(j))
                    moments(norm_cnt(2, j), res[:, j, :], j)
                for j in LANES:
                    normalise(norm_cnt(2, j), one(x_all, 2 * i + j), res[:, j, :], j).then_inc(y["x_done"], 1)

            dve.wait_ge(y["x_done"], BATCH + 2)
            lg, ex, prob, top, idxf, hot1, hot2, w = (
                bufC[:, 1, 1024 + 32 * k:1056 + 32 * k].rearrange("p (t e) -> p t e", e=NE) for k in (1, 2, 3, 4, 5, 6, 7, 0))
            nmax, z, zr, den, rden = (bufC[:, 1, 1408 + 4 * k:1412 + 4 * k] for k in range(5))
            share = bufC[:, 1, 1440:1448].rearrange("p (t e) -> p t e", e=2)
            xg = bufC[:, 0, 0:512]
            acc = bufB[:, 1, 0:512]
            x2 = bufB[:, 1, 512:1024]
            with dve.Fori(0, GROUPS) as g:
                dve.wait_ge(m["x_done"], TILES * g + 1)
                dve.tensor_scalar(xg.rearrange("p (t d) -> p t d", d=D), x_all[:, bass.ds(g * TILES, TILES), :], 1.0, None,
                                  ALU.mult).then_inc(m["x_in"], 1)
                dve.wait_ge(m["xT"], g + 1)
                dve.tensor_copy(bufC[:, 0, 512:1024], P[:, 0, 0:512]).then_inc(m["xT_sb"], 1)
                dve.tensor_scalar(x2, xg, 2.0, None, ALU.mult).then_inc(m["x2"], 1)
                dve.wait_ge(m["logits"], g + 1)
                dve.tensor_copy(lg, P[:, 1, 0:TILES * NE].rearrange("p (t e) -> p t e", e=NE)).then_inc(m["lg"], 1)
                dve.wait_ge(m["lg"], g + 1)
                dve.tensor_reduce(nmax, lg, AX.X, ALU.max, negate=True).then_inc(m["nmax"], 1)
                dve.wait_ge(m["nmax"], g + 1)
                dve.tensor_tensor(lg, lg, cols(nmax, NE), ALU.add).then_inc(m["sub"], 1)
                dve.wait_ge(m["ex"], g + 1)
                dve.tensor_reduce(z, ex, AX.X, ALU.add).then_inc(m["z"], 1)
                dve.wait_ge(m["z"], g + 1)
                dve.reciprocal(zr, z).then_inc(m["rz"], 1)
                dve.wait_ge(m["rz"], g + 1)
                dve.tensor_tensor(prob, ex, cols(zr, NE), ALU.mult).then_inc(m["prob"], 1)
                dve.wait_ge(m["prob"], g + 1)
                hold()
                for k in range(TILES):
                    ins = dve.max(top[:, k, :], prob[:, k, :])
                ins.then_inc(m["top"], 1)
                dve.wait_ge(m["top"], g + 1)
                hold()
                for k in range(TILES):
                    ins = dve.max_index(idx[:, k, :], top[:, k, :], prob[:, k, :])
                ins.then_inc(m["idx"], 1)
                dve.wait_ge(m["idx"], g + 1)
                dve.tensor_copy(idxf, idx).then_inc(m["idxf"], 1)
                dve.tensor_tensor(den, top[:, :, 0], top[:, :, 1], ALU.add).then_inc(m["den"], 1)
                dve.wait_ge(m["den"], g + 1)
                dve.tensor_scalar(den, den, 1e-9, None, ALU.add).then_inc(m["den_eps"], 1)
                dve.wait_ge(m["den_eps"], g + 1)
                dve.reciprocal(rden, den).then_inc(m["rden"], 1)
                dve.wait_ge(m["rden"], g + 1)
                dve.tensor_tensor(share, top[:, :, 0:2], cols(rden, 2), ALU.mult).then_inc(m["share"], 1)
                dve.wait_ge(m["idxf"], g + 1)
                for k, hot in enumerate((hot1, hot2)):
                    dve.tensor_tensor(hot, expert_no[:], idxf[:, :, k:k + 1].broadcast_to([128, TILES, NE]), ALU.is_equal).then_inc(m["hot"], 1)
                dve.wait_ge(m["share"], g + 1)
                for k, hot in enumerate((hot1, hot2)):
                    dve.wait_ge(m["hot"], 4 * g + 1 + k)
                    dve.tensor_tensor(hot, hot, share[:, :, k:k + 1].broadcast_to([128, TILES, NE]), ALU.mult).then_inc(m["hot"], 1)
                dve.wait_ge(m["hot"], 4 * g + 4)
                dve.tensor_tensor(w, hot1, hot2, ALU.add).then_inc(m["w"], 1)
                dve.wait_ge(m["wT"], g + 1)
                dve.tensor_copy(bufC[0:NE, 1, 0:512], P[0:NE, 1, 1536:2048]).then_inc(m["wT_sb"], 1)
                dve.wait_ge(m["w"], g + 1)
                dve.wait_ge(m["x2"], g + 1)
                for e in range(NE + 1):
                    last = x2 if e == 0 else acc
                    bank = P[:, 1, (e % 4) * 512:(e % 4 + 1) * 512]
                    dve.wait_ge(m["y"], g * (NE + 1) + e + 1)
                    if e > 0:
                        dve.wait_ge(m["acc"], g * (NE + 1) + e)
                    if e == NE:
                        ins = dve.tensor_tensor(acc, bank, acc, ALU.add)
                    else:
                        for k in range(TILES):
                            tk = slice(k * D, (k + 1) * D)
                            ins = dve.scalar_tensor_tensor(acc[:, tk], bank[:, tk], w[:, k, e:e + 1], last[:, tk], ALU.mult, ALU.add)
                    ins.then_inc(m["acc"], 1)
                dve.wait_ge(m["acc"], (g + 1) * (NE + 1))
                for k in range(TILES):
                    moments(NORM_D + g * TILES + k + 1, acc[:, k * D:(k + 1) * D], k)
                for k in range(TILES):
                    normalise(NORM_D + g * TILES + k + 1, one(x_all, g * TILES + k), acc[:, k * D:(k + 1) * D], k).then_inc(m["x_done"], 1)

        @block.gpsimd
        def _(pool):
            def inv_std(cnt, k):
                pool.wait_ge(norm["mv"], cnt)
                pool.tensor_tensor(veps[:, k, :], mv[:, k, 1:2], const_eps[:], ALU.add).then_inc(norm["veps"], 1)
                pool.wait_ge(norm["veps"], cnt)
                pool.tensor_tensor(rstd[:, k, :], veps[:, k, :], const_mhalf[:, 0:1], ALU.pow).then_inc(norm["rstd"], 1)

            pool.wait_ge(setup["const"], 1)
            with pool.Fori(0, PAIRS) as i:
                for k in range(3):
                    for j in LANES:
                        inv_std(6 * i + 2 * k + j + 1, j)
            with pool.Fori(0, DEPTH // 2) as d2:
                for p in range(2):
                    with pool.Fori(0, PAIRS) as i:
                        def cnt(j):
                            return (2 * d2 + p) * BATCH + 2 * i + j + 1
                        for j in LANES:
                            pool.wait_ge(f["ssg"], cnt(j))
                            pool.tensor_tensor(rnorm[:, j, :], sumsq_g[:, j, :], const_mhalf[:], ALU.pow).then_inc(f["rn"], 1)
                        for j in LANES:
                            pool.wait_ge(f["kn"], cnt(j))
                            kn = bufB[:, j, 0:INNER].rearrange("p (h w) -> p h w", w=LD)
                            t2 = bufC[:, j, INNER:2 * INNER].rearrange("p (h w) -> p h w", w=LD)
                            for s in range(2):
                                ins = pool.tensor_tensor(t2[:, :, 32 * s:32 * s + 32], kn[:, :, 32 - 32 * s:64 - 32 * s],
                                                         f_sin[:, p, 1, 32 * s:32 * s + 32].unsqueeze(1).broadcast_to([T, LH, 32]), ALU.mult)
                            ins.then_inc(f["t2k"], 1)
                        for j in LANES:
                            inv_std(NORM_B + cnt(j), j)
            with pool.Fori(0, PAIRS) as i:
                for k in range(3):
                    for j in LANES:
                        inv_std(NORM_C + 6 * i + 2 * k + j + 1, j)
            with pool.Fori(0, GROUPS) as g:
                for k in range(TILES):
                    inv_std(NORM_D + g * TILES + k + 1, k)

        @block.scalar
        def _(act):
            def exps(s, cnt, heads, keys, dst, scale=None, src=lambda n, keys: n * keys):
                for j in LANES:
                    act.wait_ge(s["nb"], cnt(j))
                    for n in range(heads):
                        at = src(n, keys)
                        ins = act.activation(dst[:, j, n * keys:(n + 1) * keys], P[:, j, at:at + keys], ACT.Exp,
                                             bias=bias[:, j, n:n + 1], scale=1.0 if scale is None else scale(j, n))
                    ins.then_inc(s["probs"], 1)

            def copy(dst, src, scale=1.0):
                return act.activation(dst, src, ACT.Copy, scale=scale)

            def probs_half(cnt, n):
                for j in LANES:
                    act.wait_ge(core["probsT"], cnt(j))
                    copy(bufC[:, j, 0:n], P[:, j, 0:n]).then_inc(core["probsT_act"], 1)

            def block_copy(done, ready, cnt, dst, src):
                for j in LANES:
                    act.wait_ge(ready, cnt(j))
                    copy(dst(j), src(j)).then_inc(done, 1)

            act.wait_ge(load["x"], 16 * N_X)
            act.activation(gate_e[:], gate_col[:], ACT.Exp, scale=-1.0).then_inc(setup["gate_exp"], 1)
            act.wait_ge(setup["temp"], 1)
            act.wait_ge(setup["const"], 1)

            with act.Fori(0, PAIRS) as i:
                def cnt(j):
                    return 2 * i + j + 1

                def norm_cnt(k, j):
                    return 6 * i + 2 * k + j + 1
                for j in LANES:
                    act.wait_ge(a["kvq"], cnt(j))
                    for v in range(4):
                        copy(bufA[:, j, v * 128:(v + 1) * 128], P[:, j, 0:128], mask_temp[:, v:v + 1])
                    copy(bufA[:, j, 512:640], P[:, j, 128:256])
                    copy(bufA[:, j, 640:768], P[:, j, 512:640]).then_inc(a["kvq_sb"], 1)
                exps(a, cnt, 16, 128, bufB)
                for j in LANES:
                    act.wait_ge(x["qkv"], cnt(j))
                    copy(slots(vals[:, j, 0:272], 16, 17)[:, :, 0:16], slots(P[:, j, 512:768], 16, 16)).then_inc(x["v"], 1)
                block_copy(x["qkT_sb"], x["qkT"], cnt, lambda j: bufB[:, j, 0:1024], lambda j: P[:, j, 0:1024])
                exps(core, cnt, 8, 256, bufA)
                probs_half(cnt, 1024)

            act.wait_ge(setup["vals_b"], 1)
            with act.Fori(0, DEPTH // 2) as d2:
                for p in range(2):
                    act.wait_ge(wt[p], 16 * LAYER_DMAS * (d2 + 1))
                    with act.Fori(0, PAIRS) as i:
                        def cnt(j):
                            return (2 * d2 + p) * BATCH + 2 * i + j + 1

                        def core_cnt(j):
                            return CORE_B + cnt(j)
                        for j in LANES:
                            act.wait_ge(f["qk"], cnt(j))
                            act.activation(bufB[:, j, 0:INNER], P[:, j, 0:INNER], ACT.Square).then_inc(f["sq_q"], 1)
                            act.activation(bufB[:, j, INNER:2 * INNER], P[:, j, INNER:2 * INNER], ACT.Square).then_inc(f["sq_k"], 1)
                        for j in LANES:
                            act.wait_ge(f["v"], cnt(j))
                            copy(slots(vals[:, j, :], LH, LD + 1)[:, :, 0:LD], slots(P[:, j, 0:INNER], LH, LD)).then_inc(f["v_sb"], 1)
                        for j in LANES:
                            act.wait_ge(f["kT"], cnt(j))
                            copy(bufB[:, j, INNER:2 * INNER], P[:, j, INNER:2 * INNER]).then_inc(f["kT_sb"], 1)
                            act.wait_ge(f["qT"], cnt(j))
                            copy(bufB[:, j, 0:INNER], P[:, j, 0:INNER]).then_inc(f["qT_sb"], 1)
                        exps(core, core_cnt, LH, 128, bufA, lambda j, n: rnorm[:, j, BY_ROW_LOCAL[n]:BY_ROW_LOCAL[n] + 1])
                        probs_half(core_cnt, 1024)
                        block_copy(core["oT_sb"], core["oT"], core_cnt, lambda j: bufB[:, j, INNER:2 * INNER], lambda j: P[:, j, 0:INNER])
                        for j in LANES:
                            act.wait_ge(f["h"], cnt(j))
                            for k, (lo, w) in enumerate(HCH):
                                at = slice(k * 128, (k + 1) * 128)
                                ins = act.activation(bufA[0:w, j, at], P[0:w, j, 512 + k * 128:512 + (k + 1) * 128], ACT.Gelu,
                                                     bias=f_b1[0:w, p, 1, k:k + 1])
                            ins.then_inc(f["gl"], 1)

            act.wait_ge(setup["pad_c"], 1)
            with act.Fori(0, PAIRS) as i:
                def cnt(j):
                    return 2 * i + j + 1

                def cau_cnt(j):
                    return CORE_C + 4 * i + j + 1

                def crs_cnt(j):
                    return CORE_C + 4 * i + 2 + j + 1

                def norm_cnt(k, j):
                    return NORM_C + 6 * i + 2 * k + j + 1
                for j in LANES:
                    act.wait_ge(c["kvq"], cnt(j))
                    copy(slots(pad[:, j, 512:1024], 16, 32)[:, :, 0:8], slots(P[:, j, 0:128], 16, 8))
                    copy(slots(vals[:, j, 0:144], 16, 9)[:, :, 0:8], slots(P[:, j, 128:256], 16, 8))
                    copy(slots(pad[:, j, 0:512], 16, 32)[:, :, 0:8], slots(P[:, j, 256:384], 16, 8), 8 ** -0.5).then_inc(c["kvq_sb"], 1)
                block_copy(c["qkT_sb"], c["qkT"], cnt, lambda j: bufB[:, j, 0:1024], lambda j: P[:, j, 0:1024])
                exps(core, cau_cnt, 16, 128, bufA)
                probs_half(cau_cnt, 1024)
                for j in LANES:
                    act.wait_ge(y["qkv"], cnt(j))
                    copy(slots(pad[:, j, 1024:1280], 8, 32)[:, :, 0:16], slots(P[:, j, 0:128], 8, 16), 16 ** -0.5)
                    copy(slots(pad[:, j, 1280:1536], 8, 32)[:, :, 0:16], slots(P[:, j, 128:256], 8, 16))
                    copy(slots(vals[:, j, 256:392], 8, 17)[:, :, 0:16], slots(P[:, j, 256:384], 8, 16)).then_inc(y["qkv_sb"], 1)
                block_copy(y["qkT_sb"], y["qkT"], cnt, lambda j: bufB[:, j, 0:512], lambda j: P[:, j, 0:512])
                exps(core, crs_cnt, 8, 128, bufA, src=lambda n, keys: n // 2 * 512 + n % 2 * keys)
                probs_half(crs_cnt, 512)

            act.wait_ge(load["m"], 16 * N_M)
            with act.Fori(0, GROUPS) as g:
                act.wait_ge(m["sub"], g + 1)
                act.activation(bufC[:, 1, 1088:1120], bufC[:, 1, 1056:1088], ACT.Exp).then_inc(m["ex"], 1)
                for e in range(NE + 1):
                    if e >= 2:
                        act.wait_ge(m["y"], g * (NE + 1) + e - 1)
                    for k in range(EI // 128):
                        turn = e * (EI // 128) + k
                        act.wait_ge(m["h"], g * 36 + turn + 1)
                        act.activation((bufA, bufB)[e % 2][:, 0, k * 512:(k + 1) * 512], P[:, 0, k * 512:(k + 1) * 512],
                                       ACT.Gelu_apprx_tanh, bias=m_b1[:, e, k:k + 1]).then_inc(m["g"], 1)


def constants():
    tok = np.arange(T, dtype=np.float32)
    hd = 16
    inv = (1.0 / 10000.0 ** (np.arange(0, hd, 2, dtype=np.float32) / hd)).astype(np.float32)
    fr = tok[:, None] * inv[None, :]
    emb = np.concatenate([fr, fr], -1)
    sign = np.where(np.arange(hd) % 2 == 0, -1.0, 1.0)
    fold = np.repeat([0.25, 0.25, 1.0, 1.0], D)[None, :]
    x_cos = np.tile(np.cos(emb), (1, 4 * D // hd)) * fold
    x_sin = np.tile(np.sin(emb) * sign, (1, 4 * D // hd)) * fold
    half = np.arange(0, LD, 2, dtype=np.float32)
    inv = (1.0 / 10000.0 ** (half / LD)).astype(np.float32)
    fr = tok[:, None] * inv[None, :]
    emb = np.concatenate([fr, fr], -1)
    base = (half + 0.4 * LD) / (1.4 * LD)
    scale = base[None, :] ** ((tok - T // 2) / 16.0)[:, None]
    scale = np.concatenate([scale, scale], -1)
    sign = np.where(np.arange(LD) < LD // 2, -1.0, 1.0)
    f_cos = np.stack([8.0 * np.cos(emb) * scale, np.cos(emb) / scale], 1)
    f_sin = np.stack([8.0 * np.sin(emb) * sign * scale, np.sin(emb) * sign / scale], 1)
    q, k = np.arange(T)[:, None], np.arange(T)[None, :]
    local = (k <= q) & (q <= k + 32) & (k // 32 >= q // 32 - 1)
    low = np.float32(-1e30)
    return {
        "ident": np.eye(128, dtype=np.float32),
        "shift": np.eye(128, k=1, dtype=np.float32),
        "local_mask": np.tile(np.where(local, 0, low), (1, 4)).astype(np.float32),
        "causal_mask": np.tile(np.where(k <= q, 0, low), (1, 4)).astype(np.float32),
        "head_mask": (np.arange(128)[:, None] % 32 // 8 == np.arange(4)[None, :]).astype(np.float32),
        "x_cos": x_cos.astype(np.float32), "x_sin": x_sin.astype(np.float32),
        "f_cos": f_cos.astype(np.float32), "f_sin": f_sin.astype(np.float32),
        "expert_no": np.tile(np.arange(NE, dtype=np.float32), (128, TILES, 1)),
    }


def kernel(**inputs):
    import concourse.bacc as bacc
    from concourse.bass_utils import run_bass_kernel_spmd as run

    nc = bacc.Bacc("TRN2", target_bir_lowering=False, num_devices=1)
    arrays, args = {}, {}
    for name, value in [*inputs.items(), *constants().items()]:
        a = np.ascontiguousarray(value)
        arrays[f"in_{name}"] = a
        args[name] = nc.dram_tensor(f"in_{name}", a.shape, mybir.dt.from_np(a.dtype), kind="ExternalInput").ap()
    out = nc.dram_tensor("out_x", (BATCH, T, D), fp32, kind="ExternalOutput").ap()
    program(nc, args, out)
    return run(nc, [arrays], core_ids=[0]).results[0]["out_x"]
```

```python
import numpy as np
import concourse.bass as bass
from concourse import mybir
from contextlib import ExitStack

fp32 = mybir.dt.float32
bf16 = mybir.dt.bfloat16
u32 = mybir.dt.uint32
ALU = mybir.AluOpType
ACT = mybir.ActivationFunctionType
AX = mybir.AxisListType

BATCH, T, D = 16, 128, 128
HALVES = range(2)
PAIRS = BATCH // 2
EXPERT = 3
DEPTH, LH, LD = 6, 16, 64
INNER = LH * LD
HALF = int(D * 4 * 2 / 3)
HCH = [(c, min(128, HALF - c)) for c in range(0, HALF, 128)]
NE, EI = 8, 512
EPS = 1e-5
TILES = 4
GROUPS = BATCH // TILES


def weave(*streams):
    streams = list(streams)
    while streams:
        for s in list(streams):
            try:
                next(s)
            except StopIteration:
                streams.remove(s)


def over_sequences(eng, front, back):
    with eng.Fori(0, PAIRS) as i:
        weave(front(0, 2 * i), front(1, 2 * i + 1))
        weave(back(0, 2 * i), back(1, 2 * i + 1))


def in_turn(*steps):
    for step, seq, *half in steps:
        if seq is not None:
            step(*seq, *half)


def over_layers(eng, period, start=None):
    def seq(r, p, q, lane):
        return lane, p, q, (2 * r + p) * BATCH + q

    def layer(r, p, last):
        with eng.Fori(0, PAIRS - 1) as i:
            period(seq(r, p, 2 * i, 0), seq(r, p, 2 * i + 1, 1))
            period(seq(r, p, 2 * i + 1, 1), seq(r, p, 2 * i + 2, 0))
        period(seq(r, p, BATCH - 2, 0), seq(r, p, BATCH - 1, 1))
        if last:
            period(seq(r, p, BATCH - 1, 1), None)
        else:
            if start:
                start(r + p, 1 - p)
            period(seq(r, p, BATCH - 1, 1), seq(r + p, 1 - p, 0, 0))

    if start:
        start(0, 0)
    period(None, seq(0, 0, 0, 0))
    with eng.Fori(0, DEPTH // 2 - 1) as r:
        layer(r, 0, False)
        layer(r, 1, False)
    layer(DEPTH // 2 - 1, 0, False)
    layer(DEPTH // 2 - 1, 1, True)


def part(cnt, u):
    return 2 * cnt - 1 + u


def program(nc, t, out):
    ctx = ExitStack()
    with ctx:
        def sb(name, shape, dt=fp32):
            return ctx.enter_context(nc.sbuf_tensor(name, shape, dt))

        def sem(name):
            return ctx.enter_context(nc.semaphore(name))

        def sems(prefix, names):
            return {n: sem(f"{prefix}_{n}") for n in names.split()}

        x_all = sb("x_all", [T, BATCH, D])
        x_base = sb("x_base", [T, BATCH, D])
        ctx_all = sb("ctx_all", [T, BATCH, D])
        ident = sb("ident", [128, 128])
        ident_bf = sb("ident_bf", [128, 128], bf16)
        shift = sb("shift", [128, 128])
        local_mask = sb("local_mask", [128, 512], bf16)
        causal_mask = sb("causal_mask", [128, 512], bf16)
        ones_row = sb("ones_row", [1, 128])
        const_eps = sb("const_eps", [128, 1])
        const_mhalf = sb("const_mhalf", [128, LH])
        expert_no = sb("expert_no", [128, TILES, NE])
        a_wkv = sb("a_wkv", [D, 2 * D])
        a_wq = sb("a_wq", [D, D])
        a_bias = sb("a_bias", [1, 3 * D])
        head_mask = sb("head_mask", [128, 4])
        head_temp = sb("head_temp", [128, 1])
        mask_temp = sb("mask_temp", [128, 4])
        xwT = sb("xwT", [D, 11, D])
        x_bias = sb("x_bias", [1, 8 * D])
        x_cos = sb("x_cos", [T, 4 * D])
        x_sin = sb("x_sin", [T, 4 * D])
        gate_col = sb("gate_col", [128, 1])
        gate_e = sb("gate_e", [128, 1])
        gate_1e = sb("gate_1e", [128, 1])
        ratio = sb("ratio", [128, 1])
        x_gamma = sb("x_gamma", [D, 1])
        x_beta = sb("x_beta", [D, 1])
        f_wqkv = sb("f_wqkv", [D, 2, 3 * INNER])
        f_wo = sb("f_wo", [128, 2, INNER // 128, D])
        f_w1 = sb("f_w1", [D, 2, 2 * HALF])
        f_w2 = sb("f_w2", [128, 2, len(HCH), D])
        f_b1 = sb("f_b1", [128, 2, 2, len(HCH)])
        f_ln = sb("f_ln", [D, 2, 2])
        f_b2 = sb("f_b2", [1, 2, D])
        f_scale = sb("f_scale", [T, 2, 2, LD])
        f_cosb = sb("f_cosb", [T, 2, LD])
        f_sinb = sb("f_sinb", [T, 2, LD])
        f_cos = sb("f_cos", [T, 2, 2, LD])
        f_sin = sb("f_sin", [T, 2, 2, LD])
        c_wqkv = sb("c_wqkv", [D, 3 * D])
        c_wd = sb("c_wd", [D, D])
        c_bias = sb("c_bias", [1, 4 * D])
        m_gate = sb("m_gate", [D, NE])
        m_gate_b = sb("m_gate_b", [1, NE])
        m_w1 = sb("m_w1", [D, NE + 1, EI])
        m_b1 = sb("m_b1", [128, NE + 1, EI // 128])
        m_w2 = sb("m_w2", [128, NE + 1, EI // 128, D])
        m_b2 = sb("m_b2", [NE, D])
        m_sb2 = sb("m_sb2", [1, D])

        xl = sb("xl", [T, 2, D])
        cl = sb("cl", [T, 2, D])
        xcT = sb("xcT", [D, 2, 2 * D])
        bufA = sb("bufA", [128, 2, 2048])
        xw_raw = bufA[:, 0, 0:11 * D].rearrange("p (k d) -> p k d", d=D)
        bufB = sb("bufB", [128, 2, 2048])
        bufC = sb("bufC", [128, 2, 2048])
        vals = sb("vals", [128, 2, LH * (LD + 1)])
        pad = sb("pad", [128, 2, 1536])
        res = sb("res", [T, 2, D])
        nrm = sb("nrm", [T, 2, D])
        negmax = sb("negmax", [128, 2, 16])
        bias = sb("bias", [128, 2, 16])
        zsum = sb("zsum", [128, 2, 16])
        rz = sb("rz", [128, 2, 16])
        sumsq = sb("sumsq", [128, 2, 2 * LH])
        sumsq_g = sb("sumsq_g", [128, 2, 2 * LH])
        rnorm = sb("rnorm", [128, 2, 2 * LH])
        st = sb("st", [128, TILES, 6])
        mv = sb("mv", [128, TILES, 2])
        veps = sb("veps", [128, TILES, 1])
        rstd = sb("rstd", [128, TILES, 1])

        xin = pad[:, :, 0:D]
        nrmT = cl
        idx = bufC[:, 1, 1472:1504].bitcast(u32).rearrange("p (t e) -> p t e", e=NE)

        P = ctx.enter_context(nc.psum_tensor("P", [128, 2, 2048], fp32))

        load = sems("load", "a x c m consts out")
        wt = [sem("layer_weights_even"), sem("layer_weights_odd")]
        setup = sems("setup", "const wT_ps wT temp gate shift_zero pad_c")
        gate_seen = sem("gate_seen")
        norm_front, norm_mid, norm_back = (sems("norm_" + k, "stats mv veps rstd") for k in ("front", "mid", "back"))
        core, cau = (sems(k, "scores nb probs probsT probsT_sb av rz o oT oT_sb proj") for k in ("core", "cau_core"))
        a = sems("mix", "x_in xT xT_sb kvq kvq_sb scores nb probs z rz qn oT oT_sb attn sum x1")
        x = sems("xat", "xT xT_sb qkv rope qk v qkT qkT_sb sum yn ynT ynT_sb ffn sum2 x_done")
        f = sems("loc", "x_in xT xT_sb k q v sq_k sq_q ss_k ss_q ssg_k ssg_q rn_k rn_q t12q kn t2k v_sb qT qT_sb kT kT_sb "
                        "negmax pn x1 tables sh xs xn xnT xnT_sb h gl g ffn x_done")
        c = sems("cau", "x_raw x_in xT xT_sb kvq kvq_sb qkT qkT_sb sum x1")
        y = sems("crs", "xT xT_sb qkv qkv_sb qkT qkT_sb sum x_done")
        m = sems("moe", "x2 x_in xT xT_sb logits router sub ex idxf share hot w wT wT_sb h g y acc x_done")
        LOGITS, NMAX, ZSUM, RZ, PROB, TOP, IDX, DEN, DEN_EPS, ROUTER_STEPS = range(1, 11)
        CORE_B = BATCH
        CORE_C = CORE_B + DEPTH * BATCH
        CORE_AV_C = BATCH + 2 * DEPTH * BATCH
        NORM_C = BATCH + DEPTH * BATCH
        NORM_D = 2 * BATCH

        def av_cnt(n, u):
            return CORE_B + 2 * n + u + 1

        block = ctx.enter_context(nc.Block())

        BY_ROW_8 = [4 * b + r for r in range(4) for b in range(2)]
        BY_ROW_16 = [4 * b + r for r in range(4) for b in range(4)]
        BY_ROW_LOCAL = [2 * (4 * u + i) + r for u in HALVES for r in range(2) for i in range(4)]

        def slots(ap, n, w):
            return ap.rearrange("p (s w) -> p s w", w=w)[:, 0:n, :]

        def cols(ap, n):
            return ap.unsqueeze(2).broadcast_to([ap.shape[0], ap.shape[1], n])

        def one(buf, n):
            return buf[:, n, :] if isinstance(n, int) else buf[:, bass.ds(n, 1), :].rearrange("p a d -> p (a d)")

        LAYER_DMAS = 8 + 3 * len(HCH)
        N_CONSTS, N_A, N_X, N_C, N_M = 10, 9, 22, 4, 8 + 2 * NE

        @block.sync
        def _(sp):
            for name, dst in [("ident", ident[:]), ("head_mask", head_mask[:]),
                              ("x_cos", x_cos[:]), ("x_sin", x_sin[:]), ("shift", shift[:]),
                              ("local_mask", bufB[:, 0, 0:512]), ("causal_mask", bufB[:, 0, 512:1024]),
                              ("f_cos", f_cosb[:]), ("f_sin", f_sinb[:]), ("expert_no", expert_no[:])]:
                sp.dma_start(dst, t[name]).then_inc(load["consts"], 16)
            sp.dma_start(x_all[:], t["x"].rearrange("b t d -> t b d")).then_inc(load["a"], 16)
            sp.dma_start(ctx_all[:], t["ctx_1024"].rearrange("b t d -> t b d")).then_inc(load["a"], 16)
            for k, wn in enumerate(["Wk", "Wv"]):
                sp.dma_start(a_wkv[:, k * D:(k + 1) * D], t["L0_attn_" + wn]).then_inc(load["a"], 16)
            sp.dma_start(a_wq[:], t["L0_attn_Wq"]).then_inc(load["a"], 16)
            for k, bn in enumerate(["bk", "bv", "bq"]):
                sp.dma_start(a_bias[:, k * D:(k + 1) * D], t["L0_attn_" + bn].unsqueeze(0)).then_inc(load["a"], 16)
            temp = t["L0_attn_temperature"]
            sp.dma_start(head_temp[:], bass.AP(temp.tensor, 0, [[1, 16], [0, 8], [1, 1]])).then_inc(load["a"], 16)
            for k, wn in enumerate(["qa", "qt", "ka", "kt", "va", "vt", "o", "ffn"]):
                sp.dma_start(xw_raw[:, k, :], t["L0_xattn_W_" + wn][EXPERT]).then_inc(load["x"], 16)
                sp.dma_start(x_bias[:, k * D:(k + 1) * D], t["L0_xattn_b_" + wn][EXPERT:EXPERT + 1, :]).then_inc(load["x"], 16)
            for k, wn in enumerate(["Wq", "Wk", "Wv"]):
                sp.dma_start(xw_raw[:, 8 + k, :], t["L1_xattn_" + wn]).then_inc(load["x"], 16)
            sp.dma_start(gate_col[:], t["L0_xattn_gating_factor"][EXPERT:EXPERT + 1].partition_broadcast(128)).then_inc(load["x"], 16)
            sp.dma_start(x_gamma[:], t["L0_xattn_gamma"][EXPERT].unsqueeze(1)).then_inc(load["x"], 16)
            sp.dma_start(x_beta[:], t["L0_xattn_beta"][EXPERT].unsqueeze(1)).then_inc(load["x"], 16)

            def layer(p, L):
                def pick(name):
                    ap = t["L0_ffn_" + name]
                    if isinstance(L, int):
                        return ap[L]
                    ap = ap[bass.ds(L, 1)]
                    return ap.rearrange("a b c -> (a b) c") if len(ap.shape) == 3 else ap.rearrange("a b -> (a b)")
                w2, b1 = pick("W2"), pick("b1")
                moves = [(f_wqkv[:, p, :], pick("Wqkv")),
                         (f_scale[:, p, 0, :], pick("q_scale").partition_broadcast(128)),
                         (f_scale[:, p, 1, :], pick("k_scale").partition_broadcast(128)),
                         (f_wo[:, p], pick("Wo").rearrange("(k p) d -> p k d", p=128)),
                         (f_w1[:, p, :], pick("W1")),
                         (f_ln[:, p, 0:1], pick("ln_g").unsqueeze(1)),
                         (f_ln[:, p, 1:2], pick("ln_b").unsqueeze(1)),
                         (f_b2[:, p, :], pick("b2").unsqueeze(0))]
                for k, (lo, w) in enumerate(HCH):
                    moves.append((f_w2[0:w, p, k, :], w2[lo:lo + w, :]))
                    for s in range(2):
                        moves.append((f_b1[0:w, p, s, k:k + 1], b1[s * HALF + lo:s * HALF + lo + w].unsqueeze(1)))
                for dst, src in moves:
                    sp.dma_start(dst, src).then_inc(wt[p], 16)
                assert len(moves) == LAYER_DMAS

            layer(0, 0)
            layer(1, 1)
            sp.dma_start(c_wqkv[:], t["L1_attn_w_qkv"]).then_inc(load["c"], 16)
            sp.dma_start(c_wd[:], t["L1_attn_w_dense"]).then_inc(load["c"], 16)
            sp.dma_start(c_bias[:, 0:3 * D], t["L1_attn_b_qkv"].unsqueeze(0)).then_inc(load["c"], 16)
            sp.dma_start(c_bias[:, 3 * D:4 * D], t["L1_attn_b_dense"].unsqueeze(0)).then_inc(load["c"], 16)
            sp.dma_start(m_gate[:], t["L1_ffn_gate_w"]).then_inc(load["m"], 16)
            sp.dma_start(m_gate_b[:], t["L1_ffn_gate_b"].unsqueeze(0)).then_inc(load["m"], 16)
            sp.dma_start(m_w1[:, 0:NE, :], t["L1_ffn_ew1"].rearrange("e d i -> d e i")).then_inc(load["m"], 16)
            sp.dma_start(m_w1[:, NE, :], t["L1_ffn_sh_w1"]).then_inc(load["m"], 16)
            sp.dma_start(m_w2[:, NE], t["L1_ffn_sh_w2"].rearrange("(k p) d -> p k d", p=128)).then_inc(load["m"], 16)
            sp.dma_start(m_b1[:, NE, :], t["L1_ffn_sh_b1"].rearrange("(k p) -> p k", p=128), allow_slow_non_contiguous=True).then_inc(load["m"], 16)
            sp.dma_start(m_b2[:], t["L1_ffn_eb2"]).then_inc(load["m"], 16)
            sp.dma_start(m_sb2[:], t["L1_ffn_sh_b2"].unsqueeze(0)).then_inc(load["m"], 16)
            for e in range(NE):
                sp.dma_start(m_w2[:, e], t["L1_ffn_ew2"][e].rearrange("(k p) d -> p k d", p=128)).then_inc(load["m"], 16)
                sp.dma_start(m_b1[:, e, :], t["L1_ffn_eb1"][e].rearrange("(k p) -> p k", p=128), allow_slow_non_contiguous=True).then_inc(load["m"], 16)
            with sp.Fori(0, DEPTH // 2 - 1) as d2:
                for p in range(2):
                    sp.wait_ge(f["x_done"], BATCH * (2 * d2 + p + 2))
                    layer(p, 2 * d2 + 2 + p)
            with sp.Fori(0, GROUPS) as g:
                sp.wait_ge(m["x_done"], TILES * (g + 1) + 1)
                sp.dma_start(out[bass.ds(g * TILES, TILES)].rearrange("b t d -> t b d"),
                             x_all[:, bass.ds(g * TILES, TILES), :]).then_inc(load["out"], 16)
            sp.wait_ge(load["out"], 16 * GROUPS)

        @block.tensor
        def _(pe):
            def project(dst, lhsT, rhs, bias_row, stop=True):
                pe.matmul(dst, ones_row[:], bias_row, start=True, stop=False, skip_group_check=True)
                return pe.matmul(dst, lhsT, rhs, start=False, stop=stop, skip_group_check=True)

            def transposes(j, src, n, at=0):
                for k in range(n):
                    ins = pe.transpose(P[:, j, (at + k) * 128:(at + k + 1) * 128],
                                       src[:, k * 128:(k + 1) * 128], ident[:])
                return ins

            def turn_probs(s, cnt, j, n_blocks):
                for u in HALVES:
                    pe.wait_ge(s["probs"], part(cnt, u))
                    for k in range(u * n_blocks // 2, (u + 1) * n_blocks // 2):
                        ins = pe.transpose(P[:, j, k * 2048 // n_blocks:k * 2048 // n_blocks + 128],
                                           bufA[:, j, k * 128:(k + 1) * 128], ident[:])
                    ins.then_inc(s["probsT"], 1)

            def weigh_values(s, cnt, j, order, per_head, width, slot, vcol):
                for u in HALVES:
                    pe.wait_ge(s["probsT_sb"], part(cnt, u))
                    for n in range(u * len(order) // 2, (u + 1) * len(order) // 2):
                        for k in range(per_head):
                            lo = vcol(order[n], k)
                            at = (n if slot == 128 else order[n]) * slot
                            ins = pe.matmul(P[:, j, at:at + width + 1],
                                            bufC[:, j, (n * per_head + k) * 128:(n * per_head + k + 1) * 128],
                                            vals[:, j, lo:lo + width + 1], start=k == 0, stop=k == per_head - 1)
                    if slot == 128 or u == 1:
                        ins.then_inc(s["av"], 1)

            pe.wait_ge(load["consts"], 16 * N_CONSTS)
            pe.wait_ge(load["x"], 16 * N_X)
            for k in range(11):
                ins = pe.transpose(P[:, 0, k * 128:(k + 1) * 128], xw_raw[:, k, :], ident[:])
            ins.then_inc(setup["wT_ps"], 1)
            pe.wait_ge(setup["const"], 1)
            pe.wait_ge(load["a"], 16 * N_A)
            pe.wait_ge(setup["wT"], 1)

            def mixing(j, n):
                pe.wait_ge(a["x_in"], n + 1)
                pe.transpose(P[:, j, 0:128], xl[:, j, :], ident[:])
                pe.transpose(P[:, j, 128:256], cl[:, j, :], ident[:]).then_inc(a["xT"], 1)
                yield
                pe.wait_ge(a["xT_sb"], n + 1)
                xT = xcT[:, j, 0:D]
                project(P[:, j, 0:2 * D], xT, a_wkv[:], a_bias[:, 0:2 * D])
                pe.matmul(P[:, j, 512:512 + D], a_bias[:, 2 * D:3 * D], ones_row[:], start=True, stop=False)
                pe.matmul(P[:, j, 512:512 + D], a_wq[:], xT, start=False, stop=True).then_inc(a["kvq"], 1)
                yield
                yield
                yield
                yield
                pe.wait_ge(a["kvq_sb"], n + 1)
                for u in HALVES:
                    for v in range(4):
                        for g in (2 * u, 2 * u + 1):
                            h = 4 * g + v
                            ins = pe.matmul(P[:, j, h * 128:(h + 1) * 128],
                                            bufA[32 * g:32 * g + 32, j, v * 128:(v + 1) * 128],
                                            bufA[32 * g:32 * g + 32, j, 512:640], start=True, stop=True)
                    ins.then_inc(a["scores"], 1)
                yield
                for u in HALVES:
                    pe.wait_ge(a["probs"], part(n + 1, u))
                    pe.wait_ge(a["qn"], part(n + 1, u))
                    if u == 0:
                        pe.wait_ge(a["probs"], part(n + 1, 1))
                    for h in range(8 * u, 8 * u + 8):
                        ins = pe.matmul(P[:, j, 8 * h:8 * h + 8], bufB[:, j, h * 128:(h + 1) * 128],
                                        bufA[:, j, 768 + 8 * h:768 + 8 * h + 8], start=True, stop=True)
                ins.then_inc(a["oT"], 1)
                yield
                pe.wait_ge(a["oT_sb"], n + 1)
                pe.transpose(P[:, j, 0:128], bufC[:, j, 0:128], ident[:]).then_inc(a["attn"], 1)
                yield
                yield
                yield

            def expert(j, n):
                pe.wait_ge(a["x1"], n + 1)
                pe.transpose(P[:, j, 0:128], xl[:, j, :], ident[:]).then_inc(x["xT"], 1)
                yield
                pe.wait_ge(x["xT_sb"], n + 1)
                xT, cT = xcT[:, j, 0:D], xcT[:, j, D:2 * D]
                w = xwT[:, 0:6, :].rearrange("p k d -> p (k d)")
                pe.matmul(P[:, j, 0:512], ones_row[:], x_bias[:, 0:512], start=True, stop=False, skip_group_check=True)
                pe.matmul(P[:, j, 0:256], xT, w[:, 0:256], start=False, stop=False, skip_group_check=True)
                pe.matmul(P[:, j, 256:512], cT, w[:, 256:512], start=False, stop=True, skip_group_check=True)
                project(P[:, j, 512:768], cT, w[:, 512:768], x_bias[:, 512:768]).then_inc(x["qkv"], 1)
                yield
                pe.wait_ge(x["qk"], n + 1)
                pe.wait_ge(x["v"], n + 1)
                transposes(j, pad[:, j, :], 8).then_inc(x["qkT"], 1)
                yield
                pe.wait_ge(x["qkT_sb"], n + 1)
                for u in HALVES:
                    for k in range(2):
                        for c4 in range(2):
                            for r in (2 * u, 2 * u + 1):
                                at = r * 512 + c4 * 256 + k * 128
                                q = (2 * k + c4) * 128
                                ins = pe.matmul(P[:, j, at:at + 128], bufB[32 * r:32 * r + 32, j, q:q + 128],
                                                bufB[32 * r:32 * r + 32, j, 512 + q:512 + q + 128], start=True, stop=True)
                    ins.then_inc(core["scores"], 1)
                yield
                turn_probs(core, n + 1, j, 16)
                yield
                weigh_values(core, n + 1, j, BY_ROW_8, 2, 16, 32, lambda h, k: (8 * k + h) * 17)
                yield
                pe.wait_ge(core["o"], n + 1)
                transposes(j, bufB[:, j, 1024:1152], 1).then_inc(core["oT"], 1)
                yield
                pe.wait_ge(core["oT_sb"], n + 1)
                project(P[:, j, 0:128], bufB[:, j, 1152:1280], xwT[:, 6, :], x_bias[:, 768:896]).then_inc(core["proj"], 1)
                yield
                pe.wait_ge(x["yn"], n + 1)
                pe.transpose(P[:, j, 0:128], nrm[:, j, :], ident[:]).then_inc(x["ynT"], 1)
                yield
                pe.wait_ge(x["ynT_sb"], n + 1)
                project(P[:, j, 0:128], nrmT[:, j, :], xwT[:, 7, :], x_bias[:, 896:1024]).then_inc(x["ffn"], 1)
                yield
                yield

            over_sequences(pe, mixing, expert)

            def x_turned(j, p, q, n):
                pe.wait_ge(f["x_in"], n + 1)
                pe.transpose(P[:, j, 1024:1152], xin[:, j, :], ident[:]).then_inc(f["xT"], 1)

            def project_local(j, p, at, which, done):
                for k in range(2):
                    lo = which * INNER + k * 512
                    ins = pe.matmul(P[:, j, at + k * 512:at + (k + 1) * 512], xcT[:, j, 0:D], f_wqkv[:, p, lo:lo + 512],
                                    start=True, stop=True)
                ins.then_inc(f[done], 1)

            def k_proj(j, p, q, n):
                pe.wait_ge(f["xT_sb"], n + 1)
                project_local(j, p, INNER, 1, "k")

            def q_proj(j, p, q, n):
                pe.wait_ge(f["xT_sb"], n + 1)
                pe.wait_ge(f["x_done"], n + BATCH - 1)
                project_local(j, p, 0, 0, "q")

            def v_proj(j, p, q, n):
                pe.wait_ge(f["t12q"], n + 1)
                project_local(j, p, 0, 2, "v")

            def rotated(j, lo, n):
                for k in range(n):
                    at = lo + k * 128
                    pe.matmul(P[:, j, at:at + 128], bufA[:, j, at:at + 128], ident[:], is_transpose=True, start=True, stop=False)
                    ins = pe.matmul(P[:, j, at:at + 128], bufC[:, j, at:at + 128], ident[:], is_transpose=True, start=False, stop=True)
                return ins

            def q_turned(j, p, q, n):
                pe.wait_ge(f["v_sb"], n + 1)
                rotated(j, 0, 8).then_inc(f["qT"], 1)

            def k_turned(j, p, q, n, u):
                pe.wait_ge(f["t2k"], n + 1)
                rotated(j, INNER + 512 * u, 4).then_inc(f["kT"], 1)

            def score(j, p, q, n, u):
                pe.wait_ge(f["qT_sb"], n + 1)
                pe.wait_ge(f["kT_sb"], part(n + 1, u))
                for b in (2 * u, 2 * u + 1):
                    pe.matmul(P[:, j, b * 512:(b + 1) * 512], ident_bf[:], local_mask[:],
                              start=True, stop=False, skip_group_check=True)
                for i in range(4):
                    for r2 in range(2):
                        at, s = (4 * u + i) * 128, (2 * u + r2) * 512 + i * 128
                        ins = pe.matmul(P[:, j, s:s + 128], bufB[64 * r2:64 * r2 + 64, j, at:at + 128],
                                        bufB[64 * r2:64 * r2 + 64, j, INNER + at:INNER + at + 128],
                                        start=False, stop=i == 3, skip_group_check=True)
                ins.then_inc(core["scores"], 1)

            def probs_turned(j, p, q, n, u):
                pe.wait_ge(f["pn"], part(n + 1, u))
                transposes(j, bufA[:, j, u * 1024:(u + 1) * 1024], 8, 8 * u).then_inc(core["probsT"], 1)

            def weigh(j, p, q, n, u):
                pe.wait_ge(core["probsT_sb"], part(CORE_B + n + 1, u))
                for r2 in range(2):
                    for i in range(4):
                        h, s = 2 * (4 * u + i) + r2, (8 * u + 4 * r2 + i) * 128
                        ins = pe.matmul(P[64 * r2:64 * r2 + 64, j, 1024 * u + i * 128:1024 * u + (i + 1) * 128],
                                        vals[:, j, h * LD:(h + 1) * LD], bufC[:, j, s:s + 128], start=True, stop=True)
                ins.then_inc(core["av"], 1)

            def out_proj(j, p, q, n, u):
                pe.wait_ge(core["oT_sb"], av_cnt(n, u))
                for k in range(4 * u, 4 * u + 4):
                    ins = pe.matmul(P[:, j, 512:640], bufB[:, j, INNER + k * 128:INNER + (k + 1) * 128],
                                    f_wo[:, p, k, :], start=k == 0, stop=k == INNER // 128 - 1)
                if u == 1:
                    ins.then_inc(core["proj"], 1)

            def x_shifted(j, p, q, n):
                pe.wait_ge(f["x1"], n + 3)
                pe.matmul(P[:, j, 0:64], shift[:], xl[:, j, 64:128], start=True, stop=True).then_inc(f["sh"], 1)

            def norm_turned(j, p, q, n):
                pe.wait_ge(f["xn"], n + 1)
                pe.transpose(P[:, j, 0:128], nrm[:, j, :], ident[:]).then_inc(f["xnT"], 1)

            def inner(j, p, q, n, s):
                pe.wait_ge(f["xnT_sb"], n + 1)
                for k, (lo, w) in enumerate(HCH):
                    at = s * 512 + k * 128
                    ins = pe.matmul(P[0:w, j, at:at + 128], f_w1[:, p, s * HALF + lo:s * HALF + lo + w],
                                    nrmT[:, j, :], start=True, stop=True)
                ins.then_inc(f["h"], 1)

            def outer(j, p, q, n):
                pe.wait_ge(f["g"], n + 1)
                pe.matmul(P[:, j, 0:128], ones_row[:], f_b2[:, p, :], start=True, stop=False)
                for k, (lo, w) in enumerate(HCH):
                    ins = pe.matmul(P[:, j, 0:128], bufA[0:w, j, 512 + k * 128:512 + (k + 1) * 128],
                                    f_w2[0:w, p, k, :], start=False, stop=k == len(HCH) - 1)
                ins.then_inc(f["ffn"], 1)

            def layer_weights(r, p):
                pe.wait_ge(wt[p], 16 * LAYER_DMAS * (r + 1))

            def period(b, f):
                in_turn((x_turned, f), (q_proj, f), (k_proj, f), (probs_turned, b, 0), (v_proj, f), (probs_turned, b, 1),
                        (weigh, b, 0), (weigh, b, 1), (out_proj, b, 0), (out_proj, b, 1), (q_turned, f), (x_shifted, b),
                        (k_turned, f, 0), (k_turned, f, 1), (norm_turned, b), (inner, b, 1), (inner, b, 0), (score, f, 0),
                        (outer, b), (score, f, 1))

            over_layers(pe, period, layer_weights)

            pe.wait_ge(load["c"], 16 * N_C)

            def causal(j, n):
                yield
                pe.wait_ge(c["x_in"], n + 1)
                pe.transpose(P[:, j, 0:128], xl[:, j, :], ident[:])
                pe.transpose(P[:, j, 128:256], cl[:, j, :], ident[:]).then_inc(c["xT"], 1)
                yield
                pe.wait_ge(c["xT_sb"], n + 1)
                project(P[:, j, 0:384], xcT[:, j, 0:D], c_wqkv[:], c_bias[:, 0:384]).then_inc(c["kvq"], 1)
                yield
                pe.wait_ge(c["kvq_sb"], n + 1)
                transposes(j, pad[:, j, :], 8).then_inc(c["qkT"], 1)
                yield
                pe.wait_ge(c["qkT_sb"], n + 1)
                for u in HALVES:
                    for r in (2 * u, 2 * u + 1):
                        pe.matmul(P[:, j, r * 512:(r + 1) * 512], ident_bf[:], causal_mask[:],
                                  start=True, stop=False, skip_group_check=True)
                    for b in range(4):
                        for r in (2 * u, 2 * u + 1):
                            at = r * 512 + b * 128
                            ins = pe.matmul(P[:, j, at:at + 128], bufB[32 * r:32 * r + 32, j, b * 128:(b + 1) * 128],
                                            bufB[32 * r:32 * r + 32, j, 512 + b * 128:512 + (b + 1) * 128],
                                            start=False, stop=b == 3, skip_group_check=True)
                    ins.then_inc(cau["scores"], 1)
                yield
                turn_probs(cau, n + 1, j, 16)
                yield
                weigh_values(cau, n + 1, j, BY_ROW_16, 1, 8, 16, lambda h, k: h * 9)
                yield
                pe.wait_ge(cau["o"], n + 1)
                transposes(j, bufB[:, j, 1024:1152], 1).then_inc(cau["oT"], 1)
                yield
                pe.wait_ge(cau["oT_sb"], n + 1)
                project(P[:, j, 0:128], bufB[:, j, 1152:1280], c_wd[:], c_bias[:, 384:512]).then_inc(cau["proj"], 1)
                yield
                yield

            def cross(j, n):
                cnt = CORE_C + n + 1
                pe.wait_ge(c["x1"], n + 1)
                pe.transpose(P[:, j, 0:128], xl[:, j, :], ident[:]).then_inc(y["xT"], 1)
                yield
                pe.wait_ge(y["xT_sb"], n + 1)
                w = xwT[:, 8:11, :].rearrange("p k d -> p (k d)")
                pe.matmul(P[:, j, 0:128], xcT[:, j, 0:D], w[:, 0:128], start=True, stop=True)
                pe.matmul(P[:, j, 128:384], xcT[:, j, D:2 * D], w[:, 128:384], start=True, stop=True).then_inc(y["qkv"], 1)
                yield
                pe.wait_ge(y["qkv_sb"], n + 1)
                transposes(j, pad[:, j, 1024:1536], 4).then_inc(y["qkT"], 1)
                yield
                pe.wait_ge(y["qkT_sb"], n + 1)
                for u in HALVES:
                    for b in range(2):
                        for r in (2 * u, 2 * u + 1):
                            at = r * 512 + b * 128
                            ins = pe.matmul(P[:, j, at:at + 128], bufB[32 * r:32 * r + 32, j, b * 128:(b + 1) * 128],
                                            bufB[32 * r:32 * r + 32, j, 256 + b * 128:256 + (b + 1) * 128], start=True, stop=True)
                    ins.then_inc(core["scores"], 1)
                yield
                turn_probs(core, cnt, j, 8)
                yield
                weigh_values(core, cnt, j, BY_ROW_8, 1, 16, 32, lambda h, k: 256 + h * 17)
                yield
                yield
                yield

            over_sequences(pe, causal, cross)

            pe.wait_ge(load["m"], 16 * N_M)
            with pe.Fori(0, GROUPS) as g:
                pe.wait_ge(m["x_in"], g + 1)
                for k in range(TILES):
                    ins = pe.transpose(P[:, 0, k * 128:(k + 1) * 128], bufC[:, 0, k * 128:(k + 1) * 128], ident[:])
                ins.then_inc(m["xT"], 1)
                pe.wait_ge(m["xT_sb"], g + 1)
                xT = bufC[:, 0, 512:1024]
                for k in range(TILES):
                    ins = project(P[:, 1, k * NE:(k + 1) * NE], xT[:, k * 128:(k + 1) * 128], m_gate[:], m_gate_b[:])
                ins.then_inc(m["logits"], 1)

                def inner(e):
                    for k in range(EI // 128):
                        turn = e * (EI // 128) + k
                        if turn >= 4:
                            pe.wait_ge(m["g"], g * 36 + turn - 3)
                        pe.matmul(P[:, 0, k * 512:(k + 1) * 512], m_w1[:, e, k * 128:(k + 1) * 128], xT,
                                  start=True, stop=True).then_inc(m["h"], 1)

                def outer(e):
                    pe.wait_ge(m["g"], g * 36 + 4 * e + 4)
                    if e >= 4:
                        pe.wait_ge(m["acc"], g * (NE + 1) + e - 3)
                    bank = P[:, 1, (e % 4) * 512:(e % 4 + 1) * 512]
                    src = (bufA, bufB)[e % 2]
                    for q in range(TILES):
                        dst = bank[:, q * 128:(q + 1) * 128]
                        if e == NE:
                            pe.matmul(dst, ones_row[:], m_sb2[:], start=True, stop=False)
                            pe.matmul(dst, bufC[0:NE, 1, q * 128:(q + 1) * 128], m_b2[:], start=False, stop=False)
                        for k in range(EI // 128):
                            ins = pe.matmul(dst, src[:, 0, k * 512 + q * 128:k * 512 + (q + 1) * 128], m_w2[:, e, k, :],
                                            start=e < NE and k == 0, stop=k == EI // 128 - 1)
                    ins.then_inc(m["y"], 1)

                inner(0)
                pe.wait_ge(m["w"], g + 1)
                for k in range(TILES):
                    ins = pe.transpose(P[0:NE, 1, 1536 + k * 128:1536 + (k + 1) * 128], bufC[:, 1, 1024 + k * NE:1024 + (k + 1) * NE], ident[:])
                ins.then_inc(m["wT"], 1)
                pe.wait_ge(m["wT_sb"], g + 1)
                for e in range(NE + 1):
                    if e < NE:
                        inner(e + 1)
                    outer(e)

        @block.vector
        def _(dve):
            def hold():
                dve.sem_inc(gate_seen, 1)

            def moments(s, cnt, src, k):
                dve.bn_stats(st[:, k, :], src).then_inc(s["stats"], 1)
                dve.wait_ge(s["stats"], cnt)
                hold()
                dve.bn_aggr(mv[:, k, :], st[:, k, :]).then_inc(s["mv"], 1)

            def normalise(s, cnt, dst, src, k):
                dve.wait_ge(s["rstd"], cnt)
                return dve.tensor_scalar(dst, src, mv[:, k, 0:1], rstd[:, k, :], ALU.subtract, ALU.mult)

            def row_max(s, cnt, j, heads, keys):
                for u in HALVES:
                    dve.wait_ge(s["scores"], part(cnt, u))
                    dve.tensor_reduce(bias[:, j, u * heads // 2:(u + 1) * heads // 2],
                                      slots(P[:, j, u * 1024:(u + 1) * 1024], heads // 2, keys), AX.X, ALU.max,
                                      negate=True).then_inc(s["nb"], 1)

            def keep_probs(s, cnt, j, n_blocks):
                for u in HALVES:
                    dve.wait_ge(s["probsT"], part(cnt, u))
                    src = P[:, j, u * 1024:(u + 1) * 1024]
                    if n_blocks == 16:
                        ins = dve.tensor_copy(bufC[:, j, u * 1024:(u + 1) * 1024], src)
                    else:
                        ins = dve.tensor_copy(bufC[:, j, u * 512:(u + 1) * 512].rearrange("p (b w) -> p b w", w=128),
                                              src.rearrange("p (b k w) -> p b k w", k=2, w=128)[:, :, 0, :])
                    ins.then_inc(s["probsT_sb"], 1)

            def heads_out(s, cnt, j, heads, width, slot, dst):
                dve.wait_ge(s["av"], cnt)
                o = slots(P[:, j, :], heads, slot)
                dve.reciprocal(rz[:, j, 0:heads], o[:, :, width]).then_inc(s["rz"], 1)
                dve.wait_ge(s["rz"], cnt)
                dve.tensor_tensor(dst.rearrange("p (h w) -> p h w", w=width), o[:, :, 0:width],
                                  cols(rz[:, j, 0:heads], width), ALU.mult).then_inc(s["o"], 1)

            dve.memset(ones_row[:], 1.0)
            dve.memset(const_eps[:], EPS)
            dve.memset(const_mhalf[:], -0.5)
            dve.memset(vals[:], 1.0)
            dve.memset(pad[:], 0.0).then_inc(setup["const"], 1)
            dve.sem_inc(x["x_done"], 2)
            dve.sem_inc(f["x1"], 2)
            dve.sem_inc(f["x_done"], BATCH)
            dve.sem_inc(y["x_done"], 2)
            dve.sem_inc(m["x_done"], 1)
            dve.wait_ge(load["consts"], 16 * N_CONSTS)
            dve.wait_ge(load["a"], 16 * N_A)
            dve.tensor_copy(local_mask[:], bufB[:, 0, 0:512])
            dve.tensor_copy(causal_mask[:], bufB[:, 0, 512:1024])
            dve.tensor_copy(ident_bf[:], ident[:])
            dve.tensor_scalar(mask_temp[:], head_mask[:], head_temp[:, 0:1], None, ALU.mult).then_inc(setup["temp"], 1)
            dve.wait_ge(setup["gate"], 1)
            dve.tensor_scalar(gate_1e[:], gate_e[:], 1.0, None, ALU.add).then_inc(setup["gate"], 1)
            dve.wait_ge(setup["gate"], 2)
            dve.reciprocal(ratio[:], gate_1e[:]).then_inc(setup["gate"], 1)
            dve.wait_ge(setup["gate"], 3)
            dve.tensor_scalar(x_cos[:, D:2 * D], x_cos[:, D:2 * D], ratio[:, 0:1], None, ALU.mult)
            dve.tensor_scalar(x_sin[:, D:2 * D], x_sin[:, D:2 * D], ratio[:, 0:1], None, ALU.mult).then_inc(setup["gate"], 1)
            dve.wait_ge(setup["gate"], 4)
            dve.wait_ge(setup["wT_ps"], 1)
            dve.tensor_copy(xwT[:].rearrange("p k d -> p (k d)"), P[:, 0, 0:11 * 128]).then_inc(setup["wT"], 1)

            def mixing(j, n):
                dve.wait_ge(x["x_done"], n + 1)
                dve.tensor_scalar(xl[:, j, :], one(x_all, n), 1.0, None, ALU.mult)
                dve.tensor_scalar(cl[:, j, :], one(ctx_all, n), 1.0, None, ALU.mult).then_inc(a["x_in"], 1)
                yield
                dve.wait_ge(a["xT"], n + 1)
                dve.tensor_copy(xcT[:, j, :], P[:, j, 0:256]).then_inc(a["xT_sb"], 1)
                yield
                yield
                yield
                yield
                row_max(a, n + 1, j, 16, 128)
                yield
                for u in HALVES:
                    hs = slice(8 * u, 8 * u + 8)
                    dve.wait_ge(a["probs"], part(n + 1, u))
                    dve.tensor_reduce(zsum[:, j, hs], slots(bufB[:, j, u * 1024:(u + 1) * 1024], 8, 128), AX.X, ALU.add).then_inc(a["z"], 1)
                    dve.wait_ge(a["z"], part(n + 1, u))
                    dve.reciprocal(rz[:, j, hs], zsum[:, j, hs]).then_inc(a["rz"], 1)
                    dve.wait_ge(a["rz"], part(n + 1, u))
                    dve.tensor_tensor(slots(bufA[:, j, 768 + 64 * u:832 + 64 * u], 8, 8), slots(bufA[:, j, 640 + 64 * u:704 + 64 * u], 8, 8),
                                      cols(rz[:, j, hs], 8), ALU.mult).then_inc(a["qn"], 1)
                yield
                dve.wait_ge(a["oT"], n + 1)
                dve.tensor_copy(bufC[:, j, 0:128], P[:, j, 0:128]).then_inc(a["oT_sb"], 1)
                yield
                dve.wait_ge(a["attn"], n + 1)
                dve.tensor_tensor(res[:, j, :], P[:, j, 0:128], xl[:, j, :], ALU.add).then_inc(a["sum"], 1)
                dve.wait_ge(a["sum"], n + 1)
                moments(norm_front, n + 1, res[:, j, :], j)
                yield
                normalise(norm_front, n + 1, xl[:, j, :], res[:, j, :], j).then_inc(a["x1"], 1)
                yield

            def expert(j, n):
                dve.wait_ge(x["xT"], n + 1)
                dve.tensor_copy(xcT[:, j, 0:D], P[:, j, 0:D]).then_inc(x["xT_sb"], 1)
                yield
                dve.wait_ge(x["qkv"], n + 1)
                qk = P[:, j, 0:512].rearrange("p (s two) -> p s two", two=2)
                t2 = bufA[:, j, 512:1024].rearrange("p (s two) -> p s two", two=2)
                sn = x_sin[:].rearrange("p (s two) -> p s two", two=2)
                dve.tensor_tensor(bufA[:, j, 0:512], P[:, j, 0:512], x_cos[:], ALU.mult)
                for s in range(2):
                    ins = dve.tensor_tensor(t2[:, :, s], qk[:, :, 1 - s], sn[:, :, s], ALU.mult)
                ins.then_inc(x["rope"], 1)
                dve.wait_ge(x["rope"], n + 1)
                dve.tensor_tensor(slots(pad[:, j, 0:1024], 32, 32)[:, :, 0:16], slots(bufA[:, j, 0:512], 32, 16),
                                  slots(bufA[:, j, 512:1024], 32, 16), ALU.add).then_inc(x["qk"], 1)
                yield
                yield
                row_max(core, n + 1, j, 8, 256)
                yield
                keep_probs(core, n + 1, j, 16)
                yield
                heads_out(core, n + 1, j, 8, 16, 32, bufB[:, j, 1024:1152])
                yield
                dve.wait_ge(core["oT"], n + 1)
                dve.tensor_copy(bufB[:, j, 1152:1280], P[:, j, 0:128]).then_inc(core["oT_sb"], 1)
                yield
                dve.wait_ge(core["proj"], n + 1)
                dve.tensor_tensor(res[:, j, :], P[:, j, 0:128], xl[:, j, :], ALU.add).then_inc(x["sum"], 1)
                dve.wait_ge(x["sum"], n + 1)
                moments(norm_mid, n + 1, res[:, j, :], j)
                yield
                normalise(norm_mid, n + 1, nrm[:, j, :], res[:, j, :], j).then_inc(x["yn"], 1)
                yield
                dve.wait_ge(x["ynT"], n + 1)
                dve.tensor_scalar(nrmT[:, j, :], P[:, j, 0:128], x_gamma[:, 0:1], x_beta[:, 0:1],
                                  ALU.mult, ALU.add).then_inc(x["ynT_sb"], 1)
                yield
                dve.wait_ge(x["ffn"], n + 1)
                dve.scalar_tensor_tensor(res[:, j, :], P[:, j, 0:128], 0.0, xl[:, j, :], ALU.max, ALU.add).then_inc(x["sum2"], 1)
                dve.wait_ge(x["sum2"], n + 1)
                moments(norm_back, n + 1, res[:, j, :], j)
                yield
                normalise(norm_back, n + 1, one(x_all, n), res[:, j, :], j).then_inc(x["x_done"], 1)

            over_sequences(dve, mixing, expert)

            dve.wait_ge(x["x_done"], BATCH + 2)
            dve.tensor_copy(x_base[:], x_all[:])
            dve.memset(xcT[64:128, :, 0:1], 0.0).then_inc(setup["shift_zero"], 1)
            dve.wait_ge(setup["shift_zero"], 1)

            def heads(ap):
                return ap.rearrange("p (h w) -> p h w", w=LD)

            def layer_tables(r, p):
                dve.wait_ge(wt[p], 16 * LAYER_DMAS * (r + 1))
                if not (isinstance(r, int) and 2 * r + p == 0):
                    dve.wait_ge(f["x_done"], (2 * r + p) * BATCH)
                dve.tensor_tensor(f_cos[:, p], f_cosb[:], f_scale[:, p], ALU.mult)
                for s in range(2):
                    ins = dve.tensor_tensor(f_sin[:, p, :, 32 * s:32 * s + 32], f_sinb[:, :, 32 * s:32 * s + 32],
                                            f_scale[:, p, :, 32 - 32 * s:64 - 32 * s], ALU.mult)
                ins.then_inc(f["tables"], 1)
                dve.wait_ge(f["tables"], 2 * r + p + 1)

            def x_in(j, p, q, n):
                dve.wait_ge(f["x1"], n + 1)
                dve.wait_ge(f["x_done"], n + 1)
                dve.tensor_scalar(xin[:, j, :], one(x_all, q), 1.0, None, ALU.mult).then_inc(f["x_in"], 1)

            def shift_x(j, p, q, n):
                dve.wait_ge(f["xT"], n + 1)
                dve.tensor_copy(xcT[0:64, j, 0:T], P[0:64, j, 1024:1024 + T])
                dve.tensor_copy(xcT[64:128, j, 1:T], P[64:128, j, 1024:1024 + T - 1]).then_inc(f["xT_sb"], 1)

            def guarded_sums(j, n, k, s):
                hs = slice(k * LH, (k + 1) * LH)
                dve.wait_ge(f["sq_" + s], n + 1)
                dve.tensor_reduce(sumsq[:, j, hs], heads(bufB[:, j, k * INNER:(k + 1) * INNER]), AX.X, ALU.add).then_inc(f["ss_" + s], 1)
                dve.wait_ge(f["ss_" + s], n + 1)
                dve.tensor_scalar(sumsq_g[:, j, hs], sumsq[:, j, hs], 1e-24, None, ALU.max).then_inc(f["ssg_" + s], 1)

            def k_squares(j, p, q, n):
                guarded_sums(j, n, 1, "k")

            def q_squares(j, p, q, n):
                guarded_sums(j, n, 0, "q")

            def rotation(j, p, k, term, src):
                dst = heads((bufA, bufC)[term][:, j, k * INNER:(k + 1) * INNER])
                if term == 0:
                    return dve.tensor_tensor(dst, src, f_cos[:, p, k, :].unsqueeze(1).broadcast_to([T, LH, LD]), ALU.mult)
                for s in range(2):
                    ins = dve.tensor_tensor(dst[:, :, 32 * s:32 * s + 32], src[:, :, 32 - 32 * s:64 - 32 * s],
                                            f_sin[:, p, k, 32 * s:32 * s + 32].unsqueeze(1).broadcast_to([T, LH, 32]), ALU.mult)
                return ins

            def rotate_q(j, p, q, n):
                dve.wait_ge(f["sq_q"], n + 1)
                rotation(j, p, 0, 0, heads(P[:, j, 0:INNER]))
                rotation(j, p, 0, 1, heads(P[:, j, 0:INNER])).then_inc(f["t12q"], 1)

            def normalise_k(j, p, q, n):
                dve.wait_ge(f["rn_k"], n + 1)
                dve.tensor_tensor(heads(bufB[:, j, INNER:2 * INNER]), heads(P[:, j, INNER:2 * INNER]),
                                  cols(rnorm[:, j, LH:], LD), ALU.mult).then_inc(f["kn"], 1)

            def rotate_k(j, p, q, n, term):
                dve.wait_ge(f["kn"], n + 1)
                ins = rotation(j, p, 1, term, heads(bufB[:, j, INNER:2 * INNER]))
                if term == 1:
                    ins.then_inc(f["t2k"], 1)

            def row_maxima(j, p, q, n, u):
                hs = slice(8 * u, 8 * u + 8)
                dve.wait_ge(core["scores"], part(CORE_B + n + 1, u))
                dve.tensor_reduce(negmax[:, j, hs], slots(P[:, j, u * 1024:(u + 1) * 1024], 8, 128), AX.X, ALU.max,
                                  negate=True).then_inc(f["negmax"], 1)
                if u == 0:
                    dve.wait_ge(f["rn_q"], n + 1)
                dve.wait_ge(f["negmax"], part(n + 1, u))
                dve.tensor_tensor(bias[:, j, hs].rearrange("p (r b) -> p r b", r=2), negmax[:, j, hs].rearrange("p (r b) -> p r b", r=2),
                                  rnorm[:, j, hs].rearrange("p (b r) -> p r b", r=2), ALU.mult).then_inc(core["nb"], 1)

            def normalise_probs(j, p, q, n, u):
                hs = slice(8 * u, 8 * u + 8)
                dve.wait_ge(core["probs"], part(CORE_B + n + 1, u))
                dve.reciprocal(rz[:, j, hs], zsum[:, j, hs]).then_inc(core["rz"], 1)
                dve.wait_ge(core["rz"], av_cnt(n, u))
                e = slots(bufA[:, j, u * 1024:(u + 1) * 1024], 8, 128)
                dve.tensor_tensor(e, e, cols(rz[:, j, hs], 128), ALU.mult).then_inc(f["pn"], 1)

            def keep_turned(j, p, q, n, u):
                dve.wait_ge(core["probsT"], part(CORE_B + n + 1, u))
                dve.tensor_copy(bufC[:, j, u * 1024:(u + 1) * 1024], P[:, j, u * 1024:(u + 1) * 1024]).then_inc(core["probsT_sb"], 1)

            def residual(j, p, q, n):
                dve.wait_ge(core["proj"], CORE_B + n + 1)
                dve.wait_ge(f["x_done"], n + BATCH - 1)
                dve.tensor_tensor(xl[:, j, :], P[:, j, 512:640], xin[:, j, :], ALU.add).then_inc(f["x1"], 1)

            def moments_local(j, p, q, n):
                dve.wait_ge(f["x1"], n + 3)
                dve.tensor_copy(res[:, j, 0:64], xl[:, j, 0:64])
                dve.wait_ge(f["sh"], n + 1)
                dve.tensor_copy(res[:, j, 64:128], P[:, j, 0:64]).then_inc(f["xs"], 1)
                dve.wait_ge(f["xs"], n + 1)
                moments(norm_back, BATCH + n + 1, res[:, j, :], j)

            def normalise_local(j, p, q, n):
                normalise(norm_back, BATCH + n + 1, nrm[:, j, :], res[:, j, :], j).then_inc(f["xn"], 1)

            def gamma_beta(j, p, q, n):
                dve.wait_ge(f["xnT"], n + 1)
                dve.tensor_scalar(nrmT[:, j, :], P[:, j, 0:128], f_ln[:, p, 0:1], f_ln[:, p, 1:2],
                                  ALU.mult, ALU.add).then_inc(f["xnT_sb"], 1)

            def gated(j, p, q, n):
                dve.wait_ge(f["h"], part(n + 1, 1))
                dve.wait_ge(f["gl"], n + 1)
                for k, (lo, w) in enumerate(HCH):
                    ins = dve.scalar_tensor_tensor(bufA[0:w, j, 512 + k * 128:512 + (k + 1) * 128],
                                                   P[0:w, j, k * 128:(k + 1) * 128], f_b1[0:w, p, 0, k:k + 1],
                                                   bufA[0:w, j, k * 128:(k + 1) * 128], ALU.add, ALU.mult)
                ins.then_inc(f["g"], 1)

            def x_out(j, p, q, n):
                dve.wait_ge(f["ffn"], n + 1)
                dve.tensor_tensor(one(x_all, q), P[:, j, 0:128], xl[:, j, :], ALU.add).then_inc(f["x_done"], 1)

            def period(b, f):
                in_turn((x_in, f), (shift_x, f), (row_maxima, b, 1), (normalise_probs, b, 0), (rotate_q, f),
                        (keep_turned, b, 0), (normalise_probs, b, 1), (k_squares, f), (keep_turned, b, 1),
                        (normalise_k, f), (q_squares, f), (rotate_k, f, 0), (residual, b), (rotate_k, f, 1),
                        (moments_local, b), (normalise_local, b), (gamma_beta, b), (gated, b), (row_maxima, f, 0),
                        (x_out, b))

            over_layers(dve, period, layer_tables)

            dve.wait_ge(f["x_done"], (DEPTH + 1) * BATCH)
            dve.memset(vals[:], 1.0)
            dve.memset(pad[:], 0.0).then_inc(setup["pad_c"], 1)
            dve.wait_ge(setup["pad_c"], 1)

            def causal(j, n):
                dve.wait_ge(y["x_done"], n + 1)
                dve.tensor_scalar(cl[:, j, :], one(ctx_all, n), 1.0, None, ALU.mult)
                dve.tensor_tensor(res[:, j, :], one(x_all, n), one(x_base, n), ALU.add).then_inc(c["x_raw"], 1)
                dve.wait_ge(c["x_raw"], n + 1)
                moments(norm_mid, BATCH + n + 1, res[:, j, :], j)
                yield
                normalise(norm_mid, BATCH + n + 1, xl[:, j, :], res[:, j, :], j).then_inc(c["x_in"], 1)
                yield
                dve.wait_ge(c["xT"], n + 1)
                dve.tensor_copy(xcT[:, j, :], P[:, j, 0:256]).then_inc(c["xT_sb"], 1)
                yield
                yield
                row_max(cau, n + 1, j, 16, 128)
                yield
                keep_probs(cau, n + 1, j, 16)
                yield
                heads_out(cau, n + 1, j, 16, 8, 16, bufB[:, j, 1024:1152])
                yield
                dve.wait_ge(cau["oT"], n + 1)
                dve.tensor_copy(bufB[:, j, 1152:1280], P[:, j, 0:128]).then_inc(cau["oT_sb"], 1)
                yield
                dve.wait_ge(cau["proj"], n + 1)
                dve.tensor_tensor(res[:, j, :], P[:, j, 0:128], xl[:, j, :], ALU.add).then_inc(c["sum"], 1)
                dve.wait_ge(c["sum"], n + 1)
                moments(norm_front, BATCH + n + 1, res[:, j, :], j)
                yield
                normalise(norm_front, BATCH + n + 1, xl[:, j, :], res[:, j, :], j).then_inc(c["x1"], 1)
                yield

            def cross(j, n):
                cnt = CORE_C + n + 1
                dve.wait_ge(y["xT"], n + 1)
                dve.tensor_copy(xcT[:, j, 0:D], P[:, j, 0:D]).then_inc(y["xT_sb"], 1)
                yield
                yield
                yield
                for u in HALVES:
                    dve.wait_ge(core["scores"], part(cnt, u))
                    dve.tensor_reduce(bias[:, j, 4 * u:4 * u + 4].rearrange("p (r b) -> p r b", b=2),
                                      P[:, j, u * 1024:(u + 1) * 1024].rearrange("p (r b k) -> p r b k", b=4, k=128)[:, :, 0:2, :],
                                      AX.X, ALU.max, negate=True).then_inc(core["nb"], 1)
                yield
                keep_probs(core, cnt, j, 8)
                yield
                heads_out(core, CORE_AV_C + n + 1, j, 8, 16, 32, bufB[:, j, 1024:1152])
                yield
                dve.wait_ge(core["o"], BATCH + n + 1)
                dve.tensor_tensor(res[:, j, :], bufB[:, j, 1024:1152], xl[:, j, :], ALU.add).then_inc(y["sum"], 1)
                dve.wait_ge(y["sum"], n + 1)
                moments(norm_back, NORM_C + n + 1, res[:, j, :], j)
                yield
                normalise(norm_back, NORM_C + n + 1, one(x_all, n), res[:, j, :], j).then_inc(y["x_done"], 1)

            over_sequences(dve, causal, cross)

            dve.wait_ge(y["x_done"], BATCH + 2)
            lg, ex, prob, top, idxf, hot1, hot2, w = (
                bufC[:, 1, 1024 + 32 * k:1056 + 32 * k].rearrange("p (t e) -> p t e", e=NE) for k in (1, 2, 3, 4, 5, 6, 7, 0))
            nmax, z, zr, den, rden = (bufC[:, 1, 1408 + 4 * k:1412 + 4 * k] for k in range(5))
            share = bufC[:, 1, 1440:1448].rearrange("p (t e) -> p t e", e=2)
            xg = bufC[:, 0, 0:512]
            acc = bufB[:, 1, 0:512]
            x2 = bufB[:, 1, 512:1024]
            with dve.Fori(0, GROUPS) as g:
                dve.wait_ge(m["x_done"], TILES * g + 1)
                dve.tensor_scalar(xg.rearrange("p (t d) -> p t d", d=D), x_all[:, bass.ds(g * TILES, TILES), :], 1.0, None,
                                  ALU.mult).then_inc(m["x_in"], 1)
                dve.wait_ge(m["xT"], g + 1)
                dve.tensor_copy(bufC[:, 0, 512:1024], P[:, 0, 0:512]).then_inc(m["xT_sb"], 1)
                dve.tensor_scalar(x2, xg, 2.0, None, ALU.mult).then_inc(m["x2"], 1)
                dve.wait_ge(m["logits"], g + 1)
                dve.tensor_copy(lg, P[:, 1, 0:TILES * NE].rearrange("p (t e) -> p t e", e=NE)).then_inc(m["router"], 1)
                dve.wait_ge(m["router"], ROUTER_STEPS * g + LOGITS)
                dve.tensor_reduce(nmax, lg, AX.X, ALU.max, negate=True).then_inc(m["router"], 1)
                dve.wait_ge(m["router"], ROUTER_STEPS * g + NMAX)
                dve.tensor_tensor(lg, lg, cols(nmax, NE), ALU.add).then_inc(m["sub"], 1)
                dve.wait_ge(m["ex"], g + 1)
                dve.tensor_reduce(z, ex, AX.X, ALU.add).then_inc(m["router"], 1)
                dve.wait_ge(m["router"], ROUTER_STEPS * g + ZSUM)
                dve.reciprocal(zr, z).then_inc(m["router"], 1)
                dve.wait_ge(m["router"], ROUTER_STEPS * g + RZ)
                dve.tensor_tensor(prob, ex, cols(zr, NE), ALU.mult).then_inc(m["router"], 1)
                dve.wait_ge(m["router"], ROUTER_STEPS * g + PROB)
                hold()
                for k in range(TILES):
                    ins = dve.max(top[:, k, :], prob[:, k, :])
                ins.then_inc(m["router"], 1)
                dve.wait_ge(m["router"], ROUTER_STEPS * g + TOP)
                hold()
                for k in range(TILES):
                    ins = dve.max_index(idx[:, k, :], top[:, k, :], prob[:, k, :])
                ins.then_inc(m["router"], 1)
                dve.wait_ge(m["router"], ROUTER_STEPS * g + IDX)
                dve.tensor_copy(idxf, idx).then_inc(m["idxf"], 1)
                dve.tensor_tensor(den, top[:, :, 0], top[:, :, 1], ALU.add).then_inc(m["router"], 1)
                dve.wait_ge(m["router"], ROUTER_STEPS * g + DEN)
                dve.tensor_scalar(den, den, 1e-9, None, ALU.add).then_inc(m["router"], 1)
                dve.wait_ge(m["router"], ROUTER_STEPS * g + DEN_EPS)
                dve.reciprocal(rden, den).then_inc(m["router"], 1)
                dve.wait_ge(m["router"], ROUTER_STEPS * (g + 1))
                dve.tensor_tensor(share, top[:, :, 0:2], cols(rden, 2), ALU.mult).then_inc(m["share"], 1)
                dve.wait_ge(m["idxf"], g + 1)
                for k, hot in enumerate((hot1, hot2)):
                    dve.tensor_tensor(hot, expert_no[:], idxf[:, :, k:k + 1].broadcast_to([128, TILES, NE]), ALU.is_equal).then_inc(m["hot"], 1)
                dve.wait_ge(m["share"], g + 1)
                for k, hot in enumerate((hot1, hot2)):
                    dve.wait_ge(m["hot"], 4 * g + 1 + k)
                    dve.tensor_tensor(hot, hot, share[:, :, k:k + 1].broadcast_to([128, TILES, NE]), ALU.mult).then_inc(m["hot"], 1)
                dve.wait_ge(m["hot"], 4 * g + 4)
                dve.tensor_tensor(w, hot1, hot2, ALU.add).then_inc(m["w"], 1)
                dve.wait_ge(m["wT"], g + 1)
                dve.tensor_copy(bufC[0:NE, 1, 0:512], P[0:NE, 1, 1536:2048]).then_inc(m["wT_sb"], 1)
                dve.wait_ge(m["w"], g + 1)
                dve.wait_ge(m["x2"], g + 1)
                for e in range(NE + 1):
                    last = x2 if e == 0 else acc
                    bank = P[:, 1, (e % 4) * 512:(e % 4 + 1) * 512]
                    dve.wait_ge(m["y"], g * (NE + 1) + e + 1)
                    if e > 0:
                        dve.wait_ge(m["acc"], g * (NE + 1) + e)
                    if e == NE:
                        ins = dve.tensor_tensor(acc, bank, acc, ALU.add)
                    else:
                        for k in range(TILES):
                            tk = slice(k * D, (k + 1) * D)
                            ins = dve.scalar_tensor_tensor(acc[:, tk], bank[:, tk], w[:, k, e:e + 1], last[:, tk], ALU.mult, ALU.add)
                    ins.then_inc(m["acc"], 1)
                dve.wait_ge(m["acc"], (g + 1) * (NE + 1))
                for k in range(TILES):
                    moments(norm_mid, NORM_D + g * TILES + k + 1, acc[:, k * D:(k + 1) * D], k)
                for k in range(TILES):
                    normalise(norm_mid, NORM_D + g * TILES + k + 1, one(x_all, g * TILES + k), acc[:, k * D:(k + 1) * D], k).then_inc(m["x_done"], 1)

        @block.gpsimd
        def _(pool):
            def inv_std(s, cnt, k):
                pool.wait_ge(s["mv"], cnt)
                pool.tensor_tensor(veps[:, k, :], mv[:, k, 1:2], const_eps[:], ALU.add).then_inc(s["veps"], 1)
                pool.wait_ge(s["veps"], cnt)
                pool.tensor_tensor(rstd[:, k, :], veps[:, k, :], const_mhalf[:, 0:1], ALU.pow).then_inc(s["rstd"], 1)

            pool.wait_ge(setup["const"], 1)

            def steps(n):
                for _ in range(n):
                    yield

            def mixing(j, n):
                yield from steps(8)
                inv_std(norm_front, n + 1, j)
                yield

            def expert(j, n):
                yield from steps(8)
                inv_std(norm_mid, n + 1, j)
                yield from steps(3)
                inv_std(norm_back, n + 1, j)
                yield

            over_sequences(pool, mixing, expert)

            def norms(j, n, k, s):
                hs = slice(k * LH, (k + 1) * LH)
                pool.wait_ge(f["ssg_" + s], n + 1)
                pool.tensor_tensor(rnorm[:, j, hs], sumsq_g[:, j, hs], const_mhalf[:], ALU.pow).then_inc(f["rn_" + s], 1)

            def k_norms(j, p, q, n):
                norms(j, n, 1, "k")

            def q_norms(j, p, q, n):
                norms(j, n, 0, "q")

            def inv_std_local(j, p, q, n):
                inv_std(norm_back, BATCH + n + 1, j)

            def period(b, f):
                in_turn((k_norms, f), (inv_std_local, b), (q_norms, f))

            over_layers(pool, period)

            def causal(j, n):
                inv_std(norm_mid, BATCH + n + 1, j)
                yield from steps(8)
                inv_std(norm_front, BATCH + n + 1, j)
                yield

            def cross(j, n):
                yield from steps(6)
                inv_std(norm_back, NORM_C + n + 1, j)
                yield

            over_sequences(pool, causal, cross)

            with pool.Fori(0, GROUPS) as g:
                for k in range(TILES):
                    inv_std(norm_mid, NORM_D + g * TILES + k + 1, k)

        @block.scalar
        def _(act):
            def exps(s, cnt, j, heads, keys, dst, scale=None, src=lambda n, keys: n * keys):
                for u in HALVES:
                    act.wait_ge(s["nb"], part(cnt, u))
                    for n in range(u * heads // 2, (u + 1) * heads // 2):
                        at = src(n, keys)
                        ins = act.activation(dst[:, j, n * keys:(n + 1) * keys], P[:, j, at:at + keys], ACT.Exp,
                                             bias=bias[:, j, n:n + 1], scale=1.0 if scale is None else scale(j, n))
                    ins.then_inc(s["probs"], 1)

            def copy(dst, src, scale=1.0):
                return act.activation(dst, src, ACT.Copy, scale=scale)

            act.wait_ge(load["x"], 16 * N_X)
            act.activation(gate_e[:], gate_col[:], ACT.Exp, scale=-1.0).then_inc(setup["gate"], 1)
            act.wait_ge(setup["temp"], 1)
            act.wait_ge(setup["const"], 1)

            def mixing(j, n):
                yield
                yield
                act.wait_ge(a["kvq"], n + 1)
                for v in range(4):
                    copy(bufA[:, j, v * 128:(v + 1) * 128], P[:, j, 0:128], mask_temp[:, v:v + 1])
                copy(bufA[:, j, 512:640], P[:, j, 128:256])
                copy(bufA[:, j, 640:768], P[:, j, 512:640]).then_inc(a["kvq_sb"], 1)
                yield
                yield
                yield
                exps(a, n + 1, j, 16, 128, bufB)
                yield

            def expert(j, n):
                yield
                act.wait_ge(x["qkv"], n + 1)
                copy(slots(vals[:, j, 0:272], 16, 17)[:, :, 0:16], slots(P[:, j, 512:768], 16, 16)).then_inc(x["v"], 1)
                yield
                act.wait_ge(x["qkT"], n + 1)
                copy(bufB[:, j, 0:1024], P[:, j, 0:1024]).then_inc(x["qkT_sb"], 1)
                yield
                exps(core, n + 1, j, 8, 256, bufA)
                yield

            over_sequences(act, mixing, expert)

            act.wait_ge(setup["shift_zero"], 1)

            def q_squared(j, p, q, n):
                act.wait_ge(f["q"], n + 1)
                act.activation(bufB[:, j, 0:INNER], P[:, j, 0:INNER], ACT.Square).then_inc(f["sq_q"], 1)

            def k_squared(j, p, q, n):
                act.wait_ge(f["k"], n + 1)
                act.activation(bufB[:, j, INNER:2 * INNER], P[:, j, INNER:2 * INNER], ACT.Square).then_inc(f["sq_k"], 1)

            def keep_v(j, p, q, n):
                act.wait_ge(f["v"], n + 1)
                copy(vals[:, j, 0:INNER], P[:, j, 0:INNER]).then_inc(f["v_sb"], 1)

            def keep_q(j, p, q, n):
                act.wait_ge(f["qT"], n + 1)
                act.wait_ge(f["ssg_q"], n + 1)
                copy(bufB[:, j, 0:INNER], P[:, j, 0:INNER]).then_inc(f["qT_sb"], 1)

            def keep_k(j, p, q, n, u):
                act.wait_ge(f["kT"], part(n + 1, u))
                half = slice(INNER + 512 * u, INNER + 512 * u + 512)
                copy(bufB[:, j, half], P[:, j, half]).then_inc(f["kT_sb"], 1)

            def exp_scores(j, p, q, n, u):
                act.wait_ge(core["nb"], part(CORE_B + n + 1, u))
                for k in range(8 * u, 8 * u + 8):
                    h = BY_ROW_LOCAL[k]
                    ins = act.activation(bufA[:, j, k * 128:(k + 1) * 128], P[:, j, k * 128:(k + 1) * 128], ACT.Exp,
                                         bias=bias[:, j, k:k + 1], scale=rnorm[:, j, h:h + 1], accum_out=zsum[:, j, k:k + 1])
                ins.then_inc(core["probs"], 1)

            def keep_heads(j, p, q, n, u):
                act.wait_ge(core["av"], av_cnt(n, u))
                copy(bufB[:, j, INNER + 512 * u:INNER + 512 * u + 512], P[:, j, 1024 * u:1024 * u + 512]).then_inc(core["oT_sb"], 1)

            def gelu(j, p, q, n):
                act.wait_ge(f["h"], part(n + 1, 0))
                for k, (lo, w) in enumerate(HCH):
                    at = slice(k * 128, (k + 1) * 128)
                    ins = act.activation(bufA[0:w, j, at], P[0:w, j, 512 + k * 128:512 + (k + 1) * 128], ACT.Gelu,
                                         bias=f_b1[0:w, p, 1, k:k + 1])
                ins.then_inc(f["gl"], 1)

            def layer_bias(r, p):
                act.wait_ge(wt[p], 16 * LAYER_DMAS * (r + 1))

            def period(b, f):
                in_turn((exp_scores, b, 0), (q_squared, f), (exp_scores, b, 1), (k_squared, f), (keep_heads, b, 0),
                        (keep_v, f), (keep_heads, b, 1), (keep_q, f), (keep_k, f, 0), (gelu, b), (keep_k, f, 1))

            over_layers(act, period, layer_bias)

            act.wait_ge(setup["pad_c"], 1)

            def causal(j, n):
                yield
                yield
                act.wait_ge(c["kvq"], n + 1)
                copy(slots(pad[:, j, 512:1024], 16, 32)[:, :, 0:8], slots(P[:, j, 0:128], 16, 8))
                copy(slots(vals[:, j, 0:144], 16, 9)[:, :, 0:8], slots(P[:, j, 128:256], 16, 8))
                copy(slots(pad[:, j, 0:512], 16, 32)[:, :, 0:8], slots(P[:, j, 256:384], 16, 8), 8 ** -0.5).then_inc(c["kvq_sb"], 1)
                yield
                act.wait_ge(c["qkT"], n + 1)
                copy(bufB[:, j, 0:1024], P[:, j, 0:1024]).then_inc(c["qkT_sb"], 1)
                yield
                exps(cau, n + 1, j, 16, 128, bufA)
                yield

            def cross(j, n):
                yield
                act.wait_ge(y["qkv"], n + 1)
                copy(slots(pad[:, j, 1024:1280], 8, 32)[:, :, 0:16], slots(P[:, j, 0:128], 8, 16), 16 ** -0.5)
                copy(slots(pad[:, j, 1280:1536], 8, 32)[:, :, 0:16], slots(P[:, j, 128:256], 8, 16))
                copy(slots(vals[:, j, 256:392], 8, 17)[:, :, 0:16], slots(P[:, j, 256:384], 8, 16)).then_inc(y["qkv_sb"], 1)
                yield
                act.wait_ge(y["qkT"], n + 1)
                copy(bufB[:, j, 0:512], P[:, j, 0:512]).then_inc(y["qkT_sb"], 1)
                yield
                exps(core, CORE_C + n + 1, j, 8, 128, bufA, src=lambda n, keys: n // 2 * 512 + n % 2 * keys)
                yield

            over_sequences(act, causal, cross)

            act.wait_ge(load["m"], 16 * N_M)
            with act.Fori(0, GROUPS) as g:
                act.wait_ge(m["sub"], g + 1)
                act.activation(bufC[:, 1, 1088:1120], bufC[:, 1, 1056:1088], ACT.Exp).then_inc(m["ex"], 1)
                for e in range(NE + 1):
                    if e >= 2:
                        act.wait_ge(m["y"], g * (NE + 1) + e - 1)
                    for k in range(EI // 128):
                        turn = e * (EI // 128) + k
                        act.wait_ge(m["h"], g * 36 + turn + 1)
                        act.activation((bufA, bufB)[e % 2][:, 0, k * 512:(k + 1) * 512], P[:, 0, k * 512:(k + 1) * 512],
                                       ACT.Gelu_apprx_tanh, bias=m_b1[:, e, k:k + 1]).then_inc(m["g"], 1)


def constants():
    tok = np.arange(T, dtype=np.float32)
    hd = 16
    inv = (1.0 / 10000.0 ** (np.arange(0, hd, 2, dtype=np.float32) / hd)).astype(np.float32)
    fr = tok[:, None] * inv[None, :]
    emb = np.concatenate([fr, fr], -1)
    sign = np.where(np.arange(hd) % 2 == 0, -1.0, 1.0)
    fold = np.repeat([0.25, 0.25, 1.0, 1.0], D)[None, :]
    x_cos = np.tile(np.cos(emb), (1, 4 * D // hd)) * fold
    x_sin = np.tile(np.sin(emb) * sign, (1, 4 * D // hd)) * fold
    half = np.arange(0, LD, 2, dtype=np.float32)
    inv = (1.0 / 10000.0 ** (half / LD)).astype(np.float32)
    fr = tok[:, None] * inv[None, :]
    emb = np.concatenate([fr, fr], -1)
    base = (half + 0.4 * LD) / (1.4 * LD)
    scale = base[None, :] ** ((tok - T // 2) / 16.0)[:, None]
    scale = np.concatenate([scale, scale], -1)
    sign = np.where(np.arange(LD) < LD // 2, -1.0, 1.0)
    f_cos = np.stack([8.0 * np.cos(emb) * scale, np.cos(emb) / scale], 1)
    f_sin = np.stack([8.0 * np.sin(emb) * sign * scale, np.sin(emb) * sign / scale], 1)
    q, k = np.arange(T)[:, None], np.arange(T)[None, :]
    local = (k <= q) & (q <= k + 32) & (k // 32 >= q // 32 - 1)
    low = np.float32(-1e30)
    return {
        "ident": np.eye(128, dtype=np.float32),
        "shift": np.eye(128, k=1, dtype=np.float32),
        "local_mask": np.tile(np.where(local, 0, low), (1, 4)).astype(np.float32),
        "causal_mask": np.tile(np.where(k <= q, 0, low), (1, 4)).astype(np.float32),
        "head_mask": (np.arange(128)[:, None] % 32 // 8 == np.arange(4)[None, :]).astype(np.float32),
        "x_cos": x_cos.astype(np.float32), "x_sin": x_sin.astype(np.float32),
        "f_cos": f_cos.astype(np.float32), "f_sin": f_sin.astype(np.float32),
        "expert_no": np.tile(np.arange(NE, dtype=np.float32), (128, TILES, 1)),
    }


def kernel(**inputs):
    import concourse.bacc as bacc
    from concourse.bass_utils import run_bass_kernel_spmd as run

    nc = bacc.Bacc("TRN2", target_bir_lowering=False, num_devices=1)
    arrays, args = {}, {}
    for name, value in [*inputs.items(), *constants().items()]:
        a = np.ascontiguousarray(value)
        arrays[f"in_{name}"] = a
        args[name] = nc.dram_tensor(f"in_{name}", a.shape, mybir.dt.from_np(a.dtype), kind="ExternalInput").ap()
    out = nc.dram_tensor("out_x", (BATCH, T, D), fp32, kind="ExternalOutput").ap()
    program(nc, args, out)
    return run(nc, [arrays], core_ids=[0]).results[0]["out_x"]
```

```python
import numpy as np
import concourse.bass as bass
from concourse import mybir
from contextlib import ExitStack

fp32 = mybir.dt.float32
bf16 = mybir.dt.bfloat16
u32 = mybir.dt.uint32
ALU = mybir.AluOpType
ACT = mybir.ActivationFunctionType
AX = mybir.AxisListType

BATCH, T, D = 16, 128, 128
HALVES = range(2)
PAIRS = BATCH // 2
EXPERT = 3
DEPTH, LH, LD = 6, 16, 64
INNER = LH * LD
HALF = int(D * 4 * 2 / 3)
HCH = [(c, min(128, HALF - c)) for c in range(0, HALF, 128)]
NE, EI = 8, 512
EPS = 1e-5
TILES = 4
GROUPS = BATCH // TILES


def in_turn(*steps):
    for step, seq, *half in steps:
        if seq is not None:
            step(*seq, *half)


def over_sequences(eng, period):
    period(None, (0, 0))
    with eng.Fori(0, PAIRS - 1) as i:
        period((0, 2 * i), (1, 2 * i + 1))
        period((1, 2 * i + 1), (0, 2 * i + 2))
    period((0, BATCH - 2), (1, BATCH - 1))
    period((1, BATCH - 1), None)


def over_layers(eng, period, start=None):
    def seq(r, p, q, lane):
        return lane, p, q, (2 * r + p) * BATCH + q

    def layer(r, p, last):
        with eng.Fori(0, PAIRS - 1) as i:
            period(seq(r, p, 2 * i, 0), seq(r, p, 2 * i + 1, 1))
            period(seq(r, p, 2 * i + 1, 1), seq(r, p, 2 * i + 2, 0))
        period(seq(r, p, BATCH - 2, 0), seq(r, p, BATCH - 1, 1))
        if last:
            period(seq(r, p, BATCH - 1, 1), None)
        else:
            if start:
                start(r + p, 1 - p)
            period(seq(r, p, BATCH - 1, 1), seq(r + p, 1 - p, 0, 0))

    if start:
        start(0, 0)
    period(None, seq(0, 0, 0, 0))
    with eng.Fori(0, DEPTH // 2 - 1) as r:
        layer(r, 0, False)
        layer(r, 1, False)
    layer(DEPTH // 2 - 1, 0, False)
    layer(DEPTH // 2 - 1, 1, True)


def part(cnt, u):
    return 2 * cnt - 1 + u


def program(nc, t, out):
    ctx = ExitStack()
    with ctx:
        def sb(name, shape, dt=fp32):
            return ctx.enter_context(nc.sbuf_tensor(name, shape, dt))

        def sem(name):
            return ctx.enter_context(nc.semaphore(name))

        def sems(prefix, names):
            return {n: sem(f"{prefix}_{n}") for n in names.split()}

        x_all = sb("x_all", [T, BATCH, D])
        x_base = sb("x_base", [T, BATCH, D])
        ctx_all = sb("ctx_all", [T, BATCH, D])
        ident = sb("ident", [128, 128])
        ident_bf = sb("ident_bf", [128, 128], bf16)
        shift = sb("shift", [128, 128])
        local_mask = sb("local_mask", [128, 512], bf16)
        causal_mask = sb("causal_mask", [128, 512], bf16)
        ones_row = sb("ones_row", [1, 128])
        const_eps = sb("const_eps", [128, 1])
        const_mhalf = sb("const_mhalf", [128, LH])
        expert_no = sb("expert_no", [128, TILES, NE])
        a_wkv = sb("a_wkv", [D, 2 * D])
        a_wq = sb("a_wq", [D, D])
        a_bias = sb("a_bias", [1, 3 * D])
        mask_of_8 = sb("mask_of_8", [128, 16])
        mask_of_16 = sb("mask_of_16", [128, 8])
        head_temp = sb("head_temp", [128, 1])
        xwT = sb("xwT", [D, 11, D])
        x_bias = sb("x_bias", [1, 8 * D])
        x_cos = sb("x_cos", [T, 4 * D])
        x_sin = sb("x_sin", [T, 4 * D])
        gate_col = sb("gate_col", [128, 1])
        gate_e = sb("gate_e", [128, 1])
        gate_1e = sb("gate_1e", [128, 1])
        ratio = sb("ratio", [128, 1])
        x_gamma = sb("x_gamma", [D, 1])
        x_beta = sb("x_beta", [D, 1])
        f_wqkv = sb("f_wqkv", [D, 2, 3 * INNER])
        f_wo = sb("f_wo", [128, 2, INNER // 128, D])
        f_w1 = sb("f_w1", [D, 2, 2 * HALF])
        f_w2 = sb("f_w2", [128, 2, len(HCH), D])
        f_b1 = sb("f_b1", [128, 2, 2, len(HCH)])
        f_ln = sb("f_ln", [D, 2, 2])
        f_b2 = sb("f_b2", [1, 2, D])
        f_scale = sb("f_scale", [T, 2, 2, LD])
        f_cosb = sb("f_cosb", [T, 2, LD])
        f_sinb = sb("f_sinb", [T, 2, LD])
        f_cos = sb("f_cos", [T, 2, 2, LD])
        f_sin = sb("f_sin", [T, 2, 2, LD])
        c_wqkv = sb("c_wqkv", [D, 3 * D])
        c_wd = sb("c_wd", [D, D])
        c_bias = sb("c_bias", [1, 4 * D])
        m_gate = sb("m_gate", [D, NE])
        m_gate_b = sb("m_gate_b", [1, NE])
        m_w1 = sb("m_w1", [D, NE + 1, EI])
        m_b1 = sb("m_b1", [128, NE + 1, EI // 128])
        m_w2 = sb("m_w2", [128, NE + 1, EI // 128, D])
        m_b2 = sb("m_b2", [NE, D])
        m_sb2 = sb("m_sb2", [1, D])

        xl = sb("xl", [T, 2, D])
        cl = sb("cl", [T, 2, D])
        xcT = sb("xcT", [D, 2, 2 * D])
        bufA = sb("bufA", [128, 2, 2048])
        xw_raw = bufA[:, 0, 0:11 * D].rearrange("p (k d) -> p k d", d=D)
        bufB = sb("bufB", [128, 2, 2048])
        bufC = sb("bufC", [128, 2, 2048])
        vals = sb("vals", [128, 2, LH * (LD + 1)])
        flat = sb("flat", [128, 2, 4 * D])
        res = sb("res", [T, 2, D])
        nrm = sb("nrm", [T, 2, D])
        negmax = sb("negmax", [128, 2, 16])
        bias = sb("bias", [128, 2, 16])
        zsum = sb("zsum", [128, 2, 16])
        rz = sb("rz", [128, 2, 16])
        sumsq = sb("sumsq", [128, 2, 2 * LH])
        sumsq_g = sb("sumsq_g", [128, 2, 2 * LH])
        rnorm = sb("rnorm", [128, 2, 2 * LH])
        st = sb("st", [128, TILES, 6])
        mv = sb("mv", [128, TILES, 2])
        veps = sb("veps", [128, TILES, 1])
        rstd = sb("rstd", [128, TILES, 1])

        xin = flat[:, :, 0:D]
        nrmT = cl
        idx = bufC[:, 1, 1472:1504].bitcast(u32).rearrange("p (t e) -> p t e", e=NE)

        P = ctx.enter_context(nc.psum_tensor("P", [128, 2, 2048], fp32))

        load = sems("load", "a x c m consts out")
        wt = [sem("layer_weights_even"), sem("layer_weights_odd")]
        setup = sems("setup", "const wT_ps wT masks gate shift_zero ones_c")
        gate_seen = sem("gate_seen")
        norm_front, norm_mid, norm_back = (sems("norm_" + k, "stats mv veps rstd") for k in ("front", "mid", "back"))
        core, cau = (sems(k, "scores nb probs probsT probsT_sb av rz o oT oT_sb proj") for k in ("core", "cau_core"))
        a = sems("mix", "x_in xT xT_sb kvq kvq_sb scores nb probs z rz qn oT oT_sb attn sum x1")
        x = sems("xat", "xT xT_sb qkv rope qk v qkT qkT_sb sum yn ynT ynT_sb ffn sum2 x_done")
        f = sems("loc", "x_in xT xT_sb k q v sq_k sq_q ss_k ss_q ssg_k ssg_q rn_k rn_q t12q kn t2k v_sb qT qT_sb kT kT_sb "
                        "negmax pn x1 tables sh xs xn xnT xnT_sb h gl g ffn x_done")
        c = sems("cau", "x_raw x_in xT xT_sb kvq kvq_sb qkT qkT_sb sum x1")
        y = sems("crs", "xT xT_sb qkv qkv_sb qkT qkT_sb sum x_done")
        m = sems("moe", "x2 x_in xT xT_sb logits router sub ex idxf share hot w wT wT_sb h g y acc x_done")
        LOGITS, NMAX, ZSUM, RZ, PROB, TOP, IDX, DEN, DEN_EPS, ROUTER_STEPS = range(1, 11)
        CORE_B = BATCH
        CORE_C = CORE_B + DEPTH * BATCH
        CORE_AV_C = BATCH + 2 * DEPTH * BATCH
        NORM_C = BATCH + DEPTH * BATCH
        NORM_D = 2 * BATCH

        def av_cnt(n, u):
            return CORE_B + 2 * n + u + 1

        block = ctx.enter_context(nc.Block())

        BY_ROW_LOCAL = [2 * (4 * u + i) + r for u in HALVES for r in range(2) for i in range(4)]

        def slots(ap, n, w):
            return ap.rearrange("p (s w) -> p s w", w=w)[:, 0:n, :]

        def cols(ap, n):
            return ap.unsqueeze(2).broadcast_to([ap.shape[0], ap.shape[1], n])

        def one(buf, n):
            return buf[:, n, :] if isinstance(n, int) else buf[:, bass.ds(n, 1), :].rearrange("p a d -> p (a d)")

        LAYER_DMAS = 8 + 3 * len(HCH)
        N_CONSTS, N_A, N_X, N_C, N_M = 11, 9, 22, 4, 8 + 2 * NE

        @block.sync
        def _(sp):
            for name, dst in [("ident", ident[:]), ("mask_of_8", mask_of_8[:]), ("mask_of_16", mask_of_16[:]),
                              ("x_cos", x_cos[:]), ("x_sin", x_sin[:]), ("shift", shift[:]),
                              ("local_mask", bufB[:, 0, 0:512]), ("causal_mask", bufB[:, 0, 512:1024]),
                              ("f_cos", f_cosb[:]), ("f_sin", f_sinb[:]), ("expert_no", expert_no[:])]:
                sp.dma_start(dst, t[name]).then_inc(load["consts"], 16)
            sp.dma_start(x_all[:], t["x"].rearrange("b t d -> t b d")).then_inc(load["a"], 16)
            sp.dma_start(ctx_all[:], t["ctx_1024"].rearrange("b t d -> t b d")).then_inc(load["a"], 16)
            for k, wn in enumerate(["Wk", "Wv"]):
                sp.dma_start(a_wkv[:, k * D:(k + 1) * D], t["L0_attn_" + wn]).then_inc(load["a"], 16)
            sp.dma_start(a_wq[:], t["L0_attn_Wq"]).then_inc(load["a"], 16)
            for k, bn in enumerate(["bk", "bv", "bq"]):
                sp.dma_start(a_bias[:, k * D:(k + 1) * D], t["L0_attn_" + bn].unsqueeze(0)).then_inc(load["a"], 16)
            temp = t["L0_attn_temperature"]
            sp.dma_start(head_temp[:], bass.AP(temp.tensor, 0, [[1, 16], [0, 8], [1, 1]])).then_inc(load["a"], 16)
            for k, wn in enumerate(["qa", "qt", "ka", "kt", "va", "vt", "o", "ffn"]):
                sp.dma_start(xw_raw[:, k, :], t["L0_xattn_W_" + wn][EXPERT]).then_inc(load["x"], 16)
                sp.dma_start(x_bias[:, k * D:(k + 1) * D], t["L0_xattn_b_" + wn][EXPERT:EXPERT + 1, :]).then_inc(load["x"], 16)
            for k, wn in enumerate(["Wq", "Wk", "Wv"]):
                sp.dma_start(xw_raw[:, 8 + k, :], t["L1_xattn_" + wn]).then_inc(load["x"], 16)
            sp.dma_start(gate_col[:], t["L0_xattn_gating_factor"][EXPERT:EXPERT + 1].partition_broadcast(128)).then_inc(load["x"], 16)
            sp.dma_start(x_gamma[:], t["L0_xattn_gamma"][EXPERT].unsqueeze(1)).then_inc(load["x"], 16)
            sp.dma_start(x_beta[:], t["L0_xattn_beta"][EXPERT].unsqueeze(1)).then_inc(load["x"], 16)

            def layer(p, L):
                def pick(name):
                    ap = t["L0_ffn_" + name]
                    if isinstance(L, int):
                        return ap[L]
                    ap = ap[bass.ds(L, 1)]
                    return ap.rearrange("a b c -> (a b) c") if len(ap.shape) == 3 else ap.rearrange("a b -> (a b)")
                w2, b1 = pick("W2"), pick("b1")
                moves = [(f_wqkv[:, p, :], pick("Wqkv")),
                         (f_scale[:, p, 0, :], pick("q_scale").partition_broadcast(128)),
                         (f_scale[:, p, 1, :], pick("k_scale").partition_broadcast(128)),
                         (f_wo[:, p], pick("Wo").rearrange("(k p) d -> p k d", p=128)),
                         (f_w1[:, p, :], pick("W1")),
                         (f_ln[:, p, 0:1], pick("ln_g").unsqueeze(1)),
                         (f_ln[:, p, 1:2], pick("ln_b").unsqueeze(1)),
                         (f_b2[:, p, :], pick("b2").unsqueeze(0))]
                for k, (lo, w) in enumerate(HCH):
                    moves.append((f_w2[0:w, p, k, :], w2[lo:lo + w, :]))
                    for s in range(2):
                        moves.append((f_b1[0:w, p, s, k:k + 1], b1[s * HALF + lo:s * HALF + lo + w].unsqueeze(1)))
                for dst, src in moves:
                    sp.dma_start(dst, src).then_inc(wt[p], 16)
                assert len(moves) == LAYER_DMAS

            layer(0, 0)
            layer(1, 1)
            sp.dma_start(c_wqkv[:], t["L1_attn_w_qkv"]).then_inc(load["c"], 16)
            sp.dma_start(c_wd[:], t["L1_attn_w_dense"]).then_inc(load["c"], 16)
            sp.dma_start(c_bias[:, 0:3 * D], t["L1_attn_b_qkv"].unsqueeze(0)).then_inc(load["c"], 16)
            sp.dma_start(c_bias[:, 3 * D:4 * D], t["L1_attn_b_dense"].unsqueeze(0)).then_inc(load["c"], 16)
            sp.dma_start(m_gate[:], t["L1_ffn_gate_w"]).then_inc(load["m"], 16)
            sp.dma_start(m_gate_b[:], t["L1_ffn_gate_b"].unsqueeze(0)).then_inc(load["m"], 16)
            sp.dma_start(m_w1[:, 0:NE, :], t["L1_ffn_ew1"].rearrange("e d i -> d e i")).then_inc(load["m"], 16)
            sp.dma_start(m_w1[:, NE, :], t["L1_ffn_sh_w1"]).then_inc(load["m"], 16)
            sp.dma_start(m_w2[:, NE], t["L1_ffn_sh_w2"].rearrange("(k p) d -> p k d", p=128)).then_inc(load["m"], 16)
            sp.dma_start(m_b1[:, NE, :], t["L1_ffn_sh_b1"].rearrange("(k p) -> p k", p=128), allow_slow_non_contiguous=True).then_inc(load["m"], 16)
            sp.dma_start(m_b2[:], t["L1_ffn_eb2"]).then_inc(load["m"], 16)
            sp.dma_start(m_sb2[:], t["L1_ffn_sh_b2"].unsqueeze(0)).then_inc(load["m"], 16)
            for e in range(NE):
                sp.dma_start(m_w2[:, e], t["L1_ffn_ew2"][e].rearrange("(k p) d -> p k d", p=128)).then_inc(load["m"], 16)
                sp.dma_start(m_b1[:, e, :], t["L1_ffn_eb1"][e].rearrange("(k p) -> p k", p=128), allow_slow_non_contiguous=True).then_inc(load["m"], 16)
            with sp.Fori(0, DEPTH // 2 - 1) as d2:
                for p in range(2):
                    sp.wait_ge(f["x_done"], BATCH * (2 * d2 + p + 2))
                    layer(p, 2 * d2 + 2 + p)
            with sp.Fori(0, GROUPS) as g:
                sp.wait_ge(m["x_done"], TILES * (g + 1) + 1)
                sp.dma_start(out[bass.ds(g * TILES, TILES)].rearrange("b t d -> t b d"),
                             x_all[:, bass.ds(g * TILES, TILES), :]).then_inc(load["out"], 16)
            sp.wait_ge(load["out"], 16 * GROUPS)

        @block.tensor
        def _(pe):
            def project(dst, lhsT, rhs, bias_row, stop=True):
                pe.matmul(dst, ones_row[:], bias_row, start=True, stop=False, skip_group_check=True)
                return pe.matmul(dst, lhsT, rhs, start=False, stop=stop, skip_group_check=True)

            def transposes(j, src, n, at=0):
                for k in range(n):
                    ins = pe.transpose(P[:, j, (at + k) * 128:(at + k + 1) * 128],
                                       src[:, k * 128:(k + 1) * 128], ident[:])
                return ins

            def turn_probs(s, cnt, u, j, n_blocks):
                pe.wait_ge(s["probs"], part(cnt, u))
                for k in range(u * n_blocks // 2, (u + 1) * n_blocks // 2):
                    at = (16 - n_blocks + k) * 128
                    ins = pe.transpose(P[:, j, at:at + 128], bufA[:, j, k * 128:(k + 1) * 128], ident[:])
                ins.then_inc(s["probsT"], 1)

            def weigh_values(s, cnt, u, j, n_heads, per_head, width, slot, vcol):
                pe.wait_ge(s["probsT_sb"], part(cnt, u))
                for h in range(u * n_heads // 2, (u + 1) * n_heads // 2):
                    for k in range(per_head):
                        lo, at = vcol(h, k), h * slot
                        ins = pe.matmul(P[:, j, at:at + width + 1],
                                        bufC[:, j, (h * per_head + k) * 128:(h * per_head + k + 1) * 128],
                                        vals[:, j, lo:lo + width + 1], start=k == 0, stop=k == per_head - 1)
                if u == 1:
                    ins.then_inc(s["av"], 1)

            pe.wait_ge(load["consts"], 16 * N_CONSTS)
            pe.wait_ge(load["x"], 16 * N_X)
            for k in range(11):
                ins = pe.transpose(P[:, 0, k * 128:(k + 1) * 128], xw_raw[:, k, :], ident[:])
            ins.then_inc(setup["wT_ps"], 1)
            pe.wait_ge(setup["const"], 1)
            pe.wait_ge(load["a"], 16 * N_A)
            pe.wait_ge(setup["wT"], 1)
            pe.wait_ge(setup["masks"], 1)

            def x_turned(j, n):
                pe.wait_ge(a["x_in"], n + 1)
                pe.transpose(P[:, j, 0:128], xl[:, j, :], ident[:])
                pe.transpose(P[:, j, 128:256], cl[:, j, :], ident[:]).then_inc(a["xT"], 1)

            def kvq_proj(j, n):
                pe.wait_ge(a["xT_sb"], n + 1)
                xT = xcT[:, j, 0:D]
                project(P[:, j, 1024:1024 + 2 * D], xT, a_wkv[:], a_bias[:, 0:2 * D])
                pe.matmul(P[:, j, 1536:1536 + D], a_bias[:, 2 * D:3 * D], ones_row[:], start=True, stop=False)
                pe.matmul(P[:, j, 1536:1536 + D], a_wq[:], xT, start=False, stop=True).then_inc(a["kvq"], 1)

            def mix_scores(j, n, u):
                pe.wait_ge(a["kvq_sb"], part(n + 1, u))
                for b in (2 * u, 2 * u + 1):
                    ins = pe.matmul(P[:, j, b * 512:(b + 1) * 512], bufA[:, j, 0:128], bufC[:, j, b * 512:(b + 1) * 512],
                                    start=True, stop=True)
                ins.then_inc(a["scores"], 1)

            def mix(j, n, u):
                pe.wait_ge(a["probs"], part(n + 1, u))
                pe.wait_ge(a["qn"], part(n + 1, u))
                for h in range(8 * u, 8 * u + 8):
                    ins = pe.matmul(P[:, j, 8 * h:8 * h + 8], bufB[:, j, h * 128:(h + 1) * 128],
                                    bufA[:, j, 768 + 8 * h:768 + 8 * h + 8], start=True, stop=True)
                if u == 1:
                    ins.then_inc(a["oT"], 1)

            def mix_turned(j, n):
                pe.wait_ge(a["oT_sb"], n + 1)
                pe.transpose(P[:, j, 0:128], bufC[:, j, 0:128], ident[:]).then_inc(a["attn"], 1)

            def x1_turned(j, n):
                pe.wait_ge(a["x1"], n + 1)
                pe.transpose(P[:, j, 0:128], xl[:, j, :], ident[:]).then_inc(x["xT"], 1)

            def qkv_proj(j, n):
                pe.wait_ge(x["xT_sb"], n + 1)
                xT, cT = xcT[:, j, 0:D], xcT[:, j, D:2 * D]
                w = xwT[:, 0:6, :].rearrange("p k d -> p (k d)")
                pe.matmul(P[:, j, 0:512], ones_row[:], x_bias[:, 0:512], start=True, stop=False, skip_group_check=True)
                pe.matmul(P[:, j, 0:256], xT, w[:, 0:256], start=False, stop=False, skip_group_check=True)
                pe.matmul(P[:, j, 256:512], cT, w[:, 256:512], start=False, stop=True, skip_group_check=True)
                project(P[:, j, 512:768], cT, w[:, 512:768], x_bias[:, 512:768]).then_inc(x["qkv"], 1)

            def qk_turned(j, n):
                pe.wait_ge(x["qk"], n + 1)
                pe.wait_ge(x["v"], n + 1)
                transposes(j, flat[:, j, :], 4, 8).then_inc(x["qkT"], 1)

            def scores(j, n, u):
                pe.wait_ge(x["qkT_sb"], part(n + 1, u))
                for b in (2 * u, 2 * u + 1):
                    two = slice(b * 512, (b + 1) * 512)
                    for k in range(2):
                        ins = pe.matmul(P[:, j, two].rearrange("p (h k w) -> p h k w", k=2, w=128)[:, :, k, :],
                                        bufB[:, j, k * 128:(k + 1) * 128],
                                        bufC[:, j, two].rearrange("p (h k w) -> p h k w", k=2, w=128)[:, :, k, :],
                                        start=True, stop=True)
                ins.then_inc(core["scores"], 1)

            def probs_turned(j, n, u):
                turn_probs(core, n + 1, u, j, 16)

            def weigh(j, n, u):
                weigh_values(core, n + 1, u, j, 8, 2, 16, 32, lambda h, k: (8 * k + h) * 17)

            def heads_turned(j, n):
                pe.wait_ge(core["o"], n + 1)
                transposes(j, bufB[:, j, 1024:1152], 1).then_inc(core["oT"], 1)

            def out_proj(j, n):
                pe.wait_ge(core["oT_sb"], n + 1)
                project(P[:, j, 0:128], bufB[:, j, 1152:1280], xwT[:, 6, :], x_bias[:, 768:896]).then_inc(core["proj"], 1)

            def norm_turned(j, n):
                pe.wait_ge(x["yn"], n + 1)
                pe.transpose(P[:, j, 0:128], nrm[:, j, :], ident[:]).then_inc(x["ynT"], 1)

            def feed(j, n):
                pe.wait_ge(x["ynT_sb"], n + 1)
                project(P[:, j, 0:128], nrmT[:, j, :], xwT[:, 7, :], x_bias[:, 896:1024]).then_inc(x["ffn"], 1)

            def period(b, f):
                in_turn((x_turned, f), (kvq_proj, f), (qk_turned, b), (mix_scores, f, 0), (scores, b, 0), (scores, b, 1),
                        (mix_scores, f, 1), (probs_turned, b, 0), (probs_turned, b, 1), (weigh, b, 0), (weigh, b, 1),
                        (mix, f, 0), (heads_turned, b), (out_proj, b), (mix, f, 1), (mix_turned, f), (norm_turned, b),
                        (feed, b), (x1_turned, f), (qkv_proj, f))

            over_sequences(pe, period)

            def x_turned(j, p, q, n):
                pe.wait_ge(f["x_in"], n + 1)
                pe.transpose(P[:, j, 1024:1152], xin[:, j, :], ident[:]).then_inc(f["xT"], 1)

            def project_local(j, p, at, which, done):
                for k in range(2):
                    lo = which * INNER + k * 512
                    ins = pe.matmul(P[:, j, at + k * 512:at + (k + 1) * 512], xcT[:, j, 0:D], f_wqkv[:, p, lo:lo + 512],
                                    start=True, stop=True)
                ins.then_inc(f[done], 1)

            def k_proj(j, p, q, n):
                pe.wait_ge(f["xT_sb"], n + 1)
                project_local(j, p, INNER, 1, "k")

            def q_proj(j, p, q, n):
                pe.wait_ge(f["xT_sb"], n + 1)
                pe.wait_ge(f["x_done"], n + BATCH - 1)
                project_local(j, p, 0, 0, "q")

            def v_proj(j, p, q, n):
                pe.wait_ge(f["t12q"], n + 1)
                project_local(j, p, 0, 2, "v")

            def rotated(j, lo, n):
                for k in range(n):
                    at = lo + k * 128
                    pe.matmul(P[:, j, at:at + 128], bufA[:, j, at:at + 128], ident[:], is_transpose=True, start=True, stop=False)
                    ins = pe.matmul(P[:, j, at:at + 128], bufC[:, j, at:at + 128], ident[:], is_transpose=True, start=False, stop=True)
                return ins

            def q_turned(j, p, q, n):
                pe.wait_ge(f["v_sb"], n + 1)
                rotated(j, 0, 8).then_inc(f["qT"], 1)

            def k_turned(j, p, q, n, u):
                pe.wait_ge(f["t2k"], n + 1)
                rotated(j, INNER + 512 * u, 4).then_inc(f["kT"], 1)

            def score(j, p, q, n, u):
                pe.wait_ge(f["qT_sb"], n + 1)
                pe.wait_ge(f["kT_sb"], part(n + 1, u))
                for b in (2 * u, 2 * u + 1):
                    pe.matmul(P[:, j, b * 512:(b + 1) * 512], ident_bf[:], local_mask[:],
                              start=True, stop=False, skip_group_check=True)
                for i in range(4):
                    for r2 in range(2):
                        at, s = (4 * u + i) * 128, (2 * u + r2) * 512 + i * 128
                        ins = pe.matmul(P[:, j, s:s + 128], bufB[64 * r2:64 * r2 + 64, j, at:at + 128],
                                        bufB[64 * r2:64 * r2 + 64, j, INNER + at:INNER + at + 128],
                                        start=False, stop=i == 3, skip_group_check=True)
                ins.then_inc(core["scores"], 1)

            def probs_turned(j, p, q, n, u):
                pe.wait_ge(f["pn"], part(n + 1, u))
                transposes(j, bufA[:, j, u * 1024:(u + 1) * 1024], 8, 8 * u).then_inc(core["probsT"], 1)

            def weigh(j, p, q, n, u):
                pe.wait_ge(core["probsT_sb"], part(CORE_B + n + 1, u))
                for r2 in range(2):
                    for i in range(4):
                        h, s = 2 * (4 * u + i) + r2, (8 * u + 4 * r2 + i) * 128
                        ins = pe.matmul(P[64 * r2:64 * r2 + 64, j, 1024 * u + i * 128:1024 * u + (i + 1) * 128],
                                        vals[:, j, h * LD:(h + 1) * LD], bufC[:, j, s:s + 128], start=True, stop=True)
                ins.then_inc(core["av"], 1)

            def out_proj(j, p, q, n, u):
                pe.wait_ge(core["oT_sb"], av_cnt(n, u))
                for k in range(4 * u, 4 * u + 4):
                    ins = pe.matmul(P[:, j, 512:640], bufB[:, j, INNER + k * 128:INNER + (k + 1) * 128],
                                    f_wo[:, p, k, :], start=k == 0, stop=k == INNER // 128 - 1)
                if u == 1:
                    ins.then_inc(core["proj"], 1)

            def x_shifted(j, p, q, n):
                pe.wait_ge(f["x1"], n + 3)
                pe.matmul(P[:, j, 0:64], shift[:], xl[:, j, 64:128], start=True, stop=True).then_inc(f["sh"], 1)

            def norm_turned(j, p, q, n):
                pe.wait_ge(f["xn"], n + 1)
                pe.transpose(P[:, j, 0:128], nrm[:, j, :], ident[:]).then_inc(f["xnT"], 1)

            def inner(j, p, q, n, s):
                pe.wait_ge(f["xnT_sb"], n + 1)
                for k, (lo, w) in enumerate(HCH):
                    at = s * 512 + k * 128
                    ins = pe.matmul(P[0:w, j, at:at + 128], f_w1[:, p, s * HALF + lo:s * HALF + lo + w],
                                    nrmT[:, j, :], start=True, stop=True)
                ins.then_inc(f["h"], 1)

            def outer(j, p, q, n):
                pe.wait_ge(f["g"], n + 1)
                pe.matmul(P[:, j, 0:128], ones_row[:], f_b2[:, p, :], start=True, stop=False)
                for k, (lo, w) in enumerate(HCH):
                    ins = pe.matmul(P[:, j, 0:128], bufA[0:w, j, 512 + k * 128:512 + (k + 1) * 128],
                                    f_w2[0:w, p, k, :], start=False, stop=k == len(HCH) - 1)
                ins.then_inc(f["ffn"], 1)

            def layer_weights(r, p):
                pe.wait_ge(wt[p], 16 * LAYER_DMAS * (r + 1))

            def period(b, f):
                in_turn((x_turned, f), (q_proj, f), (k_proj, f), (probs_turned, b, 0), (weigh, b, 0), (probs_turned, b, 1),
                        (v_proj, f), (out_proj, b, 0), (weigh, b, 1), (out_proj, b, 1), (q_turned, f), (x_shifted, b),
                        (k_turned, f, 0), (k_turned, f, 1), (norm_turned, b), (inner, b, 1), (inner, b, 0), (score, f, 0),
                        (outer, b), (score, f, 1))

            over_layers(pe, period, layer_weights)

            pe.wait_ge(load["c"], 16 * N_C)

            def x_turned(j, n):
                pe.wait_ge(c["x_in"], n + 1)
                pe.transpose(P[:, j, 0:128], xl[:, j, :], ident[:])
                pe.transpose(P[:, j, 128:256], cl[:, j, :], ident[:]).then_inc(c["xT"], 1)

            def kvq_proj(j, n):
                pe.wait_ge(c["xT_sb"], n + 1)
                project(P[:, j, 0:384], xcT[:, j, 0:D], c_wqkv[:], c_bias[:, 0:384]).then_inc(c["kvq"], 1)

            def qk_turned(j, n):
                pe.wait_ge(c["kvq_sb"], n + 1)
                transposes(j, flat[:, j, :], 2, 8).then_inc(c["qkT"], 1)

            def scores(j, n, u):
                pe.wait_ge(c["qkT_sb"], part(n + 1, u))
                for b in (2 * u, 2 * u + 1):
                    bank = slice(b * 512, (b + 1) * 512)
                    pe.matmul(P[:, j, bank], ident_bf[:], causal_mask[:], start=True, stop=False, skip_group_check=True)
                    ins = pe.matmul(P[:, j, bank], bufB[:, j, 0:128], bufC[:, j, bank], start=False, stop=True, skip_group_check=True)
                ins.then_inc(cau["scores"], 1)

            def probs_turned(j, n, u):
                turn_probs(cau, n + 1, u, j, 16)

            def weigh(j, n, u):
                weigh_values(cau, n + 1, u, j, 16, 1, 8, 16, lambda h, k: h * 9)

            def heads_turned(j, n):
                pe.wait_ge(cau["o"], n + 1)
                transposes(j, bufB[:, j, 1024:1152], 1).then_inc(cau["oT"], 1)

            def out_proj(j, n):
                pe.wait_ge(cau["oT_sb"], n + 1)
                project(P[:, j, 0:128], bufB[:, j, 1152:1280], c_wd[:], c_bias[:, 384:512]).then_inc(cau["proj"], 1)

            def x1_turned(j, n):
                pe.wait_ge(c["x1"], n + 1)
                pe.transpose(P[:, j, 0:128], xl[:, j, :], ident[:]).then_inc(y["xT"], 1)

            def qkv_proj(j, n):
                pe.wait_ge(y["xT_sb"], n + 1)
                w = xwT[:, 8:11, :].rearrange("p k d -> p (k d)")
                pe.matmul(P[:, j, 0:128], xcT[:, j, 0:D], w[:, 0:128], start=True, stop=True)
                pe.matmul(P[:, j, 128:384], xcT[:, j, D:2 * D], w[:, 128:384], start=True, stop=True).then_inc(y["qkv"], 1)

            def cross_qk_turned(j, n):
                pe.wait_ge(y["qkv_sb"], n + 1)
                transposes(j, flat[:, j, 256:512], 2, 8).then_inc(y["qkT"], 1)

            def cross_scores(j, n, u):
                pe.wait_ge(y["qkT_sb"], part(n + 1, u))
                ins = pe.matmul(P[:, j, u * 512:(u + 1) * 512], bufB[:, j, 0:128], bufC[:, j, 1024 + u * 512:1536 + u * 512],
                                start=True, stop=True)
                ins.then_inc(core["scores"], 1)

            def cross_probs_turned(j, n, u):
                turn_probs(core, CORE_C + n + 1, u, j, 8)

            def cross_weigh(j, n, u):
                weigh_values(core, CORE_C + n + 1, u, j, 8, 1, 16, 32, lambda h, k: 256 + h * 17)

            def period(b, f):
                in_turn((weigh, b, 0), (weigh, b, 1), (heads_turned, b), (x_turned, f), (out_proj, b), (kvq_proj, f),
                        (qk_turned, f), (x1_turned, b), (qkv_proj, b), (scores, f, 0), (cross_qk_turned, b),
                        (scores, f, 1), (cross_scores, b, 0), (cross_scores, b, 1), (probs_turned, f, 0),
                        (cross_probs_turned, b, 0), (cross_probs_turned, b, 1), (cross_weigh, b, 0), (cross_weigh, b, 1),
                        (probs_turned, f, 1))

            over_sequences(pe, period)

            pe.wait_ge(load["m"], 16 * N_M)
            with pe.Fori(0, GROUPS) as g:
                pe.wait_ge(m["x_in"], g + 1)
                for k in range(TILES):
                    ins = pe.transpose(P[:, 0, k * 128:(k + 1) * 128], bufC[:, 0, k * 128:(k + 1) * 128], ident[:])
                ins.then_inc(m["xT"], 1)
                pe.wait_ge(m["xT_sb"], g + 1)
                xT = bufC[:, 0, 512:1024]
                for k in range(TILES):
                    ins = project(P[:, 1, k * NE:(k + 1) * NE], xT[:, k * 128:(k + 1) * 128], m_gate[:], m_gate_b[:])
                ins.then_inc(m["logits"], 1)

                def inner(e):
                    for k in range(EI // 128):
                        turn = e * (EI // 128) + k
                        if turn >= 4:
                            pe.wait_ge(m["g"], g * 36 + turn - 3)
                        pe.matmul(P[:, 0, k * 512:(k + 1) * 512], m_w1[:, e, k * 128:(k + 1) * 128], xT,
                                  start=True, stop=True).then_inc(m["h"], 1)

                def outer(e):
                    pe.wait_ge(m["g"], g * 36 + 4 * e + 4)
                    if e >= 4:
                        pe.wait_ge(m["acc"], g * (NE + 1) + e - 3)
                    bank = P[:, 1, (e % 4) * 512:(e % 4 + 1) * 512]
                    src = (bufA, bufB)[e % 2]
                    for q in range(TILES):
                        dst = bank[:, q * 128:(q + 1) * 128]
                        if e == NE:
                            pe.matmul(dst, ones_row[:], m_sb2[:], start=True, stop=False)
                            pe.matmul(dst, bufC[0:NE, 1, q * 128:(q + 1) * 128], m_b2[:], start=False, stop=False)
                        for k in range(EI // 128):
                            ins = pe.matmul(dst, src[:, 0, k * 512 + q * 128:k * 512 + (q + 1) * 128], m_w2[:, e, k, :],
                                            start=e < NE and k == 0, stop=k == EI // 128 - 1)
                    ins.then_inc(m["y"], 1)

                inner(0)
                pe.wait_ge(m["w"], g + 1)
                for k in range(TILES):
                    ins = pe.transpose(P[0:NE, 1, 1536 + k * 128:1536 + (k + 1) * 128], bufC[:, 1, 1024 + k * NE:1024 + (k + 1) * NE], ident[:])
                ins.then_inc(m["wT"], 1)
                pe.wait_ge(m["wT_sb"], g + 1)
                for e in range(NE + 1):
                    if e < NE:
                        inner(e + 1)
                    outer(e)

        @block.vector
        def _(dve):
            def hold():
                dve.sem_inc(gate_seen, 1)

            def moments(s, cnt, src, k):
                dve.bn_stats(st[:, k, :], src).then_inc(s["stats"], 1)
                dve.wait_ge(s["stats"], cnt)
                hold()
                dve.bn_aggr(mv[:, k, :], st[:, k, :]).then_inc(s["mv"], 1)

            def normalise(s, cnt, dst, src, k):
                dve.wait_ge(s["rstd"], cnt)
                return dve.tensor_scalar(dst, src, mv[:, k, 0:1], rstd[:, k, :], ALU.subtract, ALU.mult)

            def row_max(s, cnt, u, j, heads, keys):
                dve.wait_ge(s["scores"], part(cnt, u))
                dve.tensor_reduce(bias[:, j, u * heads // 2:(u + 1) * heads // 2],
                                  slots(P[:, j, u * 1024:(u + 1) * 1024], heads // 2, keys), AX.X, ALU.max,
                                  negate=True).then_inc(s["nb"], 1)

            def copy_probs(s, cnt, u, j, n_blocks):
                dve.wait_ge(s["probsT"], part(cnt, u))
                w = n_blocks * 64
                at = (16 - n_blocks) * 128 + u * w
                dve.tensor_copy(bufC[:, j, u * w:(u + 1) * w], P[:, j, at:at + w]).then_inc(s["probsT_sb"], 1)

            def divide_heads(s, cnt, j, heads, width, slot, dst):
                dve.wait_ge(s["av"], cnt)
                o = slots(P[:, j, :], heads, slot)
                dve.reciprocal(rz[:, j, 0:heads], o[:, :, width]).then_inc(s["rz"], 1)
                dve.wait_ge(s["rz"], cnt)
                dve.tensor_tensor(dst.rearrange("p (h w) -> p h w", w=width), o[:, :, 0:width],
                                  cols(rz[:, j, 0:heads], width), ALU.mult).then_inc(s["o"], 1)

            dve.memset(ones_row[:], 1.0)
            dve.memset(const_eps[:], EPS)
            dve.memset(const_mhalf[:], -0.5)
            dve.memset(vals[:], 1.0).then_inc(setup["const"], 1)
            dve.sem_inc(x["x_done"], 2)
            dve.sem_inc(f["x1"], 2)
            dve.sem_inc(f["x_done"], BATCH)
            dve.sem_inc(y["x_done"], 2)
            dve.sem_inc(m["x_done"], 1)
            dve.wait_ge(load["consts"], 16 * N_CONSTS)
            dve.wait_ge(load["a"], 16 * N_A)
            dve.tensor_copy(local_mask[:], bufB[:, 0, 0:512])
            dve.tensor_copy(causal_mask[:], bufB[:, 0, 512:1024])
            dve.tensor_copy(ident_bf[:], ident[:]).then_inc(setup["masks"], 1)
            dve.wait_ge(setup["gate"], 1)
            dve.tensor_scalar(gate_1e[:], gate_e[:], 1.0, None, ALU.add).then_inc(setup["gate"], 1)
            dve.wait_ge(setup["gate"], 2)
            dve.reciprocal(ratio[:], gate_1e[:]).then_inc(setup["gate"], 1)
            dve.wait_ge(setup["gate"], 3)
            dve.tensor_scalar(x_cos[:, D:2 * D], x_cos[:, D:2 * D], ratio[:, 0:1], None, ALU.mult)
            dve.tensor_scalar(x_sin[:, D:2 * D], x_sin[:, D:2 * D], ratio[:, 0:1], None, ALU.mult).then_inc(setup["gate"], 1)
            dve.wait_ge(setup["gate"], 4)
            dve.wait_ge(setup["wT_ps"], 1)
            dve.tensor_copy(xwT[:].rearrange("p k d -> p (k d)"), P[:, 0, 0:11 * 128]).then_inc(setup["wT"], 1)

            def x_in(j, n):
                dve.wait_ge(x["x_done"], n + 1)
                dve.tensor_scalar(xl[:, j, :], one(x_all, n), 1.0, None, ALU.mult)
                dve.tensor_scalar(cl[:, j, :], one(ctx_all, n), 1.0, None, ALU.mult).then_inc(a["x_in"], 1)

            def keep_x(j, n):
                dve.wait_ge(a["xT"], n + 1)
                dve.tensor_copy(xcT[:, j, :], P[:, j, 0:256]).then_inc(a["xT_sb"], 1)

            def mix_maxima(j, n, u):
                row_max(a, n + 1, u, j, 16, 128)

            def mix_sums(j, n, u):
                hs = slice(8 * u, 8 * u + 8)
                dve.wait_ge(a["probs"], part(n + 1, u))
                dve.tensor_reduce(zsum[:, j, hs], slots(bufB[:, j, u * 1024:(u + 1) * 1024], 8, 128), AX.X, ALU.add).then_inc(a["z"], 1)
                dve.wait_ge(a["z"], part(n + 1, u))
                dve.reciprocal(rz[:, j, hs], zsum[:, j, hs]).then_inc(a["rz"], 1)
                dve.wait_ge(a["rz"], part(n + 1, u))
                dve.tensor_tensor(slots(bufA[:, j, 768 + 64 * u:832 + 64 * u], 8, 8), slots(bufA[:, j, 640 + 64 * u:704 + 64 * u], 8, 8),
                                  cols(rz[:, j, hs], 8), ALU.mult).then_inc(a["qn"], 1)

            def keep_mixed(j, n):
                dve.wait_ge(a["oT"], n + 1)
                dve.tensor_copy(bufC[:, j, 0:128], P[:, j, 0:128]).then_inc(a["oT_sb"], 1)

            def residual(j, n):
                dve.wait_ge(a["attn"], n + 1)
                dve.tensor_tensor(res[:, j, :], P[:, j, 0:128], xl[:, j, :], ALU.add).then_inc(a["sum"], 1)
                dve.wait_ge(a["sum"], n + 1)
                moments(norm_front, n + 1, res[:, j, :], j)

            def x1_out(j, n):
                normalise(norm_front, n + 1, xl[:, j, :], res[:, j, :], j).then_inc(a["x1"], 1)

            def keep_x1(j, n):
                dve.wait_ge(x["xT"], n + 1)
                dve.tensor_copy(xcT[:, j, 0:D], P[:, j, 0:D]).then_inc(x["xT_sb"], 1)

            def rotate(j, n):
                dve.wait_ge(x["qkv"], n + 1)
                qk = P[:, j, 0:512].rearrange("p (s two) -> p s two", two=2)
                t2 = bufA[:, j, 512:1024].rearrange("p (s two) -> p s two", two=2)
                sn = x_sin[:].rearrange("p (s two) -> p s two", two=2)
                dve.tensor_tensor(bufA[:, j, 0:512], P[:, j, 0:512], x_cos[:], ALU.mult)
                for s in range(2):
                    ins = dve.tensor_tensor(t2[:, :, s], qk[:, :, 1 - s], sn[:, :, s], ALU.mult)
                ins.then_inc(x["rope"], 1)
                dve.wait_ge(x["rope"], n + 1)
                dve.tensor_tensor(flat[:, j, :], bufA[:, j, 0:512], bufA[:, j, 512:1024], ALU.add).then_inc(x["qk"], 1)

            def maxima(j, n, u):
                row_max(core, n + 1, u, j, 8, 256)

            def keep_probs(j, n, u):
                copy_probs(core, n + 1, u, j, 16)

            def heads_out(j, n):
                divide_heads(core, n + 1, j, 8, 16, 32, bufB[:, j, 1024:1152])

            def keep_heads(j, n):
                dve.wait_ge(core["oT"], n + 1)
                dve.tensor_copy(bufB[:, j, 1152:1280], P[:, j, 0:128]).then_inc(core["oT_sb"], 1)

            def residual1(j, n):
                dve.wait_ge(core["proj"], n + 1)
                dve.tensor_tensor(res[:, j, :], P[:, j, 0:128], xl[:, j, :], ALU.add).then_inc(x["sum"], 1)
                dve.wait_ge(x["sum"], n + 1)
                moments(norm_mid, n + 1, res[:, j, :], j)

            def norm1(j, n):
                normalise(norm_mid, n + 1, nrm[:, j, :], res[:, j, :], j).then_inc(x["yn"], 1)

            def gamma_beta(j, n):
                dve.wait_ge(x["ynT"], n + 1)
                dve.tensor_scalar(nrmT[:, j, :], P[:, j, 0:128], x_gamma[:, 0:1], x_beta[:, 0:1],
                                  ALU.mult, ALU.add).then_inc(x["ynT_sb"], 1)

            def residual2(j, n):
                dve.wait_ge(x["ffn"], n + 1)
                dve.scalar_tensor_tensor(res[:, j, :], P[:, j, 0:128], 0.0, xl[:, j, :], ALU.max, ALU.add).then_inc(x["sum2"], 1)
                dve.wait_ge(x["sum2"], n + 1)
                moments(norm_back, n + 1, res[:, j, :], j)

            def x_out(j, n):
                normalise(norm_back, n + 1, one(x_all, n), res[:, j, :], j).then_inc(x["x_done"], 1)

            def period(b, f):
                in_turn((x_in, f), (keep_x, f), (rotate, b), (mix_maxima, f, 0), (maxima, b, 0), (maxima, b, 1),
                        (mix_maxima, f, 1), (keep_probs, b, 0), (keep_probs, b, 1), (mix_sums, f, 0), (mix_sums, f, 1),
                        (heads_out, b), (keep_heads, b), (residual1, b), (keep_mixed, f), (norm1, b), (residual, f),
                        (gamma_beta, b), (x1_out, f), (keep_x1, f), (residual2, b), (x_out, b))

            over_sequences(dve, period)

            dve.wait_ge(x["x_done"], BATCH + 2)
            dve.tensor_copy(x_base[:], x_all[:])
            dve.memset(xcT[64:128, :, 0:1], 0.0).then_inc(setup["shift_zero"], 1)
            dve.wait_ge(setup["shift_zero"], 1)

            def heads(ap):
                return ap.rearrange("p (h w) -> p h w", w=LD)

            def layer_tables(r, p):
                dve.wait_ge(wt[p], 16 * LAYER_DMAS * (r + 1))
                if not (isinstance(r, int) and 2 * r + p == 0):
                    dve.wait_ge(f["x_done"], (2 * r + p) * BATCH)
                dve.tensor_tensor(f_cos[:, p], f_cosb[:], f_scale[:, p], ALU.mult)
                for s in range(2):
                    ins = dve.tensor_tensor(f_sin[:, p, :, 32 * s:32 * s + 32], f_sinb[:, :, 32 * s:32 * s + 32],
                                            f_scale[:, p, :, 32 - 32 * s:64 - 32 * s], ALU.mult)
                ins.then_inc(f["tables"], 1)
                dve.wait_ge(f["tables"], 2 * r + p + 1)

            def x_in(j, p, q, n):
                dve.wait_ge(f["x1"], n + 1)
                dve.wait_ge(f["x_done"], n + 1)
                dve.tensor_scalar(xin[:, j, :], one(x_all, q), 1.0, None, ALU.mult).then_inc(f["x_in"], 1)

            def shift_x(j, p, q, n):
                dve.wait_ge(f["xT"], n + 1)
                dve.tensor_copy(xcT[0:64, j, 0:T], P[0:64, j, 1024:1024 + T])
                dve.tensor_copy(xcT[64:128, j, 1:T], P[64:128, j, 1024:1024 + T - 1]).then_inc(f["xT_sb"], 1)

            def guarded_sums(j, n, k, s):
                hs = slice(k * LH, (k + 1) * LH)
                dve.wait_ge(f["sq_" + s], n + 1)
                dve.tensor_reduce(sumsq[:, j, hs], heads(bufB[:, j, k * INNER:(k + 1) * INNER]), AX.X, ALU.add).then_inc(f["ss_" + s], 1)
                dve.wait_ge(f["ss_" + s], n + 1)
                dve.tensor_scalar(sumsq_g[:, j, hs], sumsq[:, j, hs], 1e-24, None, ALU.max).then_inc(f["ssg_" + s], 1)

            def k_squares(j, p, q, n):
                guarded_sums(j, n, 1, "k")

            def q_squares(j, p, q, n):
                guarded_sums(j, n, 0, "q")

            def rotation(j, p, k, term, src):
                dst = heads((bufA, bufC)[term][:, j, k * INNER:(k + 1) * INNER])
                if term == 0:
                    return dve.tensor_tensor(dst, src, f_cos[:, p, k, :].unsqueeze(1).broadcast_to([T, LH, LD]), ALU.mult)
                for s in range(2):
                    ins = dve.tensor_tensor(dst[:, :, 32 * s:32 * s + 32], src[:, :, 32 - 32 * s:64 - 32 * s],
                                            f_sin[:, p, k, 32 * s:32 * s + 32].unsqueeze(1).broadcast_to([T, LH, 32]), ALU.mult)
                return ins

            def rotate_q(j, p, q, n):
                dve.wait_ge(f["sq_q"], n + 1)
                rotation(j, p, 0, 0, heads(P[:, j, 0:INNER]))
                rotation(j, p, 0, 1, heads(P[:, j, 0:INNER])).then_inc(f["t12q"], 1)

            def normalise_k(j, p, q, n):
                dve.wait_ge(f["rn_k"], n + 1)
                dve.tensor_tensor(heads(bufB[:, j, INNER:2 * INNER]), heads(P[:, j, INNER:2 * INNER]),
                                  cols(rnorm[:, j, LH:], LD), ALU.mult).then_inc(f["kn"], 1)

            def rotate_k(j, p, q, n, term):
                dve.wait_ge(f["kn"], n + 1)
                ins = rotation(j, p, 1, term, heads(bufB[:, j, INNER:2 * INNER]))
                if term == 1:
                    ins.then_inc(f["t2k"], 1)

            def row_maxima(j, p, q, n, u):
                hs = slice(8 * u, 8 * u + 8)
                dve.wait_ge(core["scores"], part(CORE_B + n + 1, u))
                dve.tensor_reduce(negmax[:, j, hs], slots(P[:, j, u * 1024:(u + 1) * 1024], 8, 128), AX.X, ALU.max,
                                  negate=True).then_inc(f["negmax"], 1)
                if u == 0:
                    dve.wait_ge(f["rn_q"], n + 1)
                dve.wait_ge(f["negmax"], part(n + 1, u))
                dve.tensor_tensor(bias[:, j, hs].rearrange("p (r b) -> p r b", r=2), negmax[:, j, hs].rearrange("p (r b) -> p r b", r=2),
                                  rnorm[:, j, hs].rearrange("p (b r) -> p r b", r=2), ALU.mult).then_inc(core["nb"], 1)

            def normalise_probs(j, p, q, n, u):
                hs = slice(8 * u, 8 * u + 8)
                dve.wait_ge(core["probs"], part(CORE_B + n + 1, u))
                dve.reciprocal(rz[:, j, hs], zsum[:, j, hs]).then_inc(core["rz"], 1)
                dve.wait_ge(core["rz"], av_cnt(n, u))
                e = slots(bufA[:, j, u * 1024:(u + 1) * 1024], 8, 128)
                dve.tensor_tensor(e, e, cols(rz[:, j, hs], 128), ALU.mult).then_inc(f["pn"], 1)

            def keep_turned(j, p, q, n, u):
                dve.wait_ge(core["probsT"], part(CORE_B + n + 1, u))
                dve.tensor_copy(bufC[:, j, u * 1024:(u + 1) * 1024], P[:, j, u * 1024:(u + 1) * 1024]).then_inc(core["probsT_sb"], 1)

            def residual(j, p, q, n):
                dve.wait_ge(core["proj"], CORE_B + n + 1)
                dve.wait_ge(f["x_done"], n + BATCH - 1)
                dve.tensor_tensor(xl[:, j, :], P[:, j, 512:640], xin[:, j, :], ALU.add).then_inc(f["x1"], 1)

            def moments_local(j, p, q, n):
                dve.wait_ge(f["x1"], n + 3)
                dve.tensor_copy(res[:, j, 0:64], xl[:, j, 0:64])
                dve.wait_ge(f["sh"], n + 1)
                dve.tensor_copy(res[:, j, 64:128], P[:, j, 0:64]).then_inc(f["xs"], 1)
                dve.wait_ge(f["xs"], n + 1)
                moments(norm_back, BATCH + n + 1, res[:, j, :], j)

            def normalise_local(j, p, q, n):
                normalise(norm_back, BATCH + n + 1, nrm[:, j, :], res[:, j, :], j).then_inc(f["xn"], 1)

            def gamma_beta(j, p, q, n):
                dve.wait_ge(f["xnT"], n + 1)
                dve.tensor_scalar(nrmT[:, j, :], P[:, j, 0:128], f_ln[:, p, 0:1], f_ln[:, p, 1:2],
                                  ALU.mult, ALU.add).then_inc(f["xnT_sb"], 1)

            def gated(j, p, q, n):
                dve.wait_ge(f["h"], part(n + 1, 1))
                dve.wait_ge(f["gl"], n + 1)
                for k, (lo, w) in enumerate(HCH):
                    ins = dve.scalar_tensor_tensor(bufA[0:w, j, 512 + k * 128:512 + (k + 1) * 128],
                                                   P[0:w, j, k * 128:(k + 1) * 128], f_b1[0:w, p, 0, k:k + 1],
                                                   bufA[0:w, j, k * 128:(k + 1) * 128], ALU.add, ALU.mult)
                ins.then_inc(f["g"], 1)

            def x_out(j, p, q, n):
                dve.wait_ge(f["ffn"], n + 1)
                dve.tensor_tensor(one(x_all, q), P[:, j, 0:128], xl[:, j, :], ALU.add).then_inc(f["x_done"], 1)

            def period(b, f):
                in_turn((x_in, f), (shift_x, f), (row_maxima, b, 1), (normalise_probs, b, 0), (rotate_q, f),
                        (keep_turned, b, 0), (normalise_probs, b, 1), (k_squares, f), (keep_turned, b, 1), (q_squares, f),
                        (normalise_k, f), (rotate_k, f, 0), (residual, b), (rotate_k, f, 1), (moments_local, b),
                        (normalise_local, b), (gamma_beta, b), (gated, b), (row_maxima, f, 0), (x_out, b))

            over_layers(dve, period, layer_tables)

            dve.wait_ge(f["x_done"], (DEPTH + 1) * BATCH)
            dve.memset(vals[:], 1.0).then_inc(setup["ones_c"], 1)
            dve.wait_ge(setup["ones_c"], 1)

            def x_in(j, n):
                dve.wait_ge(y["x_done"], n + 1)
                dve.tensor_scalar(cl[:, j, :], one(ctx_all, n), 1.0, None, ALU.mult)
                dve.tensor_tensor(res[:, j, :], one(x_all, n), one(x_base, n), ALU.add).then_inc(c["x_raw"], 1)
                dve.wait_ge(c["x_raw"], n + 1)
                moments(norm_mid, BATCH + n + 1, res[:, j, :], j)

            def norm0(j, n):
                normalise(norm_mid, BATCH + n + 1, xl[:, j, :], res[:, j, :], j).then_inc(c["x_in"], 1)

            def keep_x(j, n):
                dve.wait_ge(c["xT"], n + 1)
                dve.tensor_copy(xcT[:, j, :], P[:, j, 0:256]).then_inc(c["xT_sb"], 1)

            def maxima(j, n, u):
                row_max(cau, n + 1, u, j, 16, 128)

            def keep_probs(j, n, u):
                copy_probs(cau, n + 1, u, j, 16)

            def heads_out(j, n):
                divide_heads(cau, n + 1, j, 16, 8, 16, bufB[:, j, 1024:1152])

            def keep_heads(j, n):
                dve.wait_ge(cau["oT"], n + 1)
                dve.tensor_copy(bufB[:, j, 1152:1280], P[:, j, 0:128]).then_inc(cau["oT_sb"], 1)

            def residual(j, n):
                dve.wait_ge(cau["proj"], n + 1)
                dve.tensor_tensor(res[:, j, :], P[:, j, 0:128], xl[:, j, :], ALU.add).then_inc(c["sum"], 1)
                dve.wait_ge(c["sum"], n + 1)
                moments(norm_front, BATCH + n + 1, res[:, j, :], j)

            def x1_out(j, n):
                normalise(norm_front, BATCH + n + 1, xl[:, j, :], res[:, j, :], j).then_inc(c["x1"], 1)

            def keep_x1(j, n):
                dve.wait_ge(y["xT"], n + 1)
                dve.tensor_copy(xcT[:, j, 0:D], P[:, j, 0:D]).then_inc(y["xT_sb"], 1)

            def cross_maxima(j, n, u):
                dve.wait_ge(core["scores"], part(CORE_C + n + 1, u))
                dve.tensor_reduce(bias[:, j, 4 * u:4 * u + 4], slots(P[:, j, u * 512:(u + 1) * 512], 4, 128),
                                  AX.X, ALU.max, negate=True).then_inc(core["nb"], 1)

            def cross_keep_probs(j, n, u):
                copy_probs(core, CORE_C + n + 1, u, j, 8)

            def cross_heads_out(j, n):
                divide_heads(core, CORE_AV_C + n + 1, j, 8, 16, 32, bufB[:, j, 1024:1152])

            def residual2(j, n):
                dve.wait_ge(core["o"], BATCH + n + 1)
                dve.tensor_tensor(res[:, j, :], bufB[:, j, 1024:1152], xl[:, j, :], ALU.add).then_inc(y["sum"], 1)
                dve.wait_ge(y["sum"], n + 1)
                moments(norm_back, NORM_C + n + 1, res[:, j, :], j)

            def x_out(j, n):
                normalise(norm_back, NORM_C + n + 1, one(x_all, n), res[:, j, :], j).then_inc(y["x_done"], 1)

            def period(b, f):
                in_turn((x_in, f), (heads_out, b), (norm0, f), (keep_heads, b), (keep_x, f), (residual, b), (x1_out, b),
                        (keep_x1, b), (maxima, f, 0), (cross_maxima, b, 0), (cross_maxima, b, 1), (maxima, f, 1),
                        (cross_keep_probs, b, 0), (cross_keep_probs, b, 1), (keep_probs, f, 0), (cross_heads_out, b),
                        (residual2, b), (keep_probs, f, 1), (x_out, b))

            over_sequences(dve, period)

            dve.wait_ge(y["x_done"], BATCH + 2)
            lg, ex, prob, top, idxf, hot1, hot2, w = (
                bufC[:, 1, 1024 + 32 * k:1056 + 32 * k].rearrange("p (t e) -> p t e", e=NE) for k in (1, 2, 3, 4, 5, 6, 7, 0))
            nmax, z, zr, den, rden = (bufC[:, 1, 1408 + 4 * k:1412 + 4 * k] for k in range(5))
            share = bufC[:, 1, 1440:1448].rearrange("p (t e) -> p t e", e=2)
            xg = bufC[:, 0, 0:512]
            acc = bufB[:, 1, 0:512]
            x2 = bufB[:, 1, 512:1024]
            with dve.Fori(0, GROUPS) as g:
                dve.wait_ge(m["x_done"], TILES * g + 1)
                dve.tensor_scalar(xg.rearrange("p (t d) -> p t d", d=D), x_all[:, bass.ds(g * TILES, TILES), :], 1.0, None,
                                  ALU.mult).then_inc(m["x_in"], 1)
                dve.wait_ge(m["xT"], g + 1)
                dve.tensor_copy(bufC[:, 0, 512:1024], P[:, 0, 0:512]).then_inc(m["xT_sb"], 1)
                dve.tensor_scalar(x2, xg, 2.0, None, ALU.mult).then_inc(m["x2"], 1)
                dve.wait_ge(m["logits"], g + 1)
                dve.tensor_copy(lg, P[:, 1, 0:TILES * NE].rearrange("p (t e) -> p t e", e=NE)).then_inc(m["router"], 1)
                dve.wait_ge(m["router"], ROUTER_STEPS * g + LOGITS)
                dve.tensor_reduce(nmax, lg, AX.X, ALU.max, negate=True).then_inc(m["router"], 1)
                dve.wait_ge(m["router"], ROUTER_STEPS * g + NMAX)
                dve.tensor_tensor(lg, lg, cols(nmax, NE), ALU.add).then_inc(m["sub"], 1)
                dve.wait_ge(m["ex"], g + 1)
                dve.tensor_reduce(z, ex, AX.X, ALU.add).then_inc(m["router"], 1)
                dve.wait_ge(m["router"], ROUTER_STEPS * g + ZSUM)
                dve.reciprocal(zr, z).then_inc(m["router"], 1)
                dve.wait_ge(m["router"], ROUTER_STEPS * g + RZ)
                dve.tensor_tensor(prob, ex, cols(zr, NE), ALU.mult).then_inc(m["router"], 1)
                dve.wait_ge(m["router"], ROUTER_STEPS * g + PROB)
                hold()
                for k in range(TILES):
                    ins = dve.max(top[:, k, :], prob[:, k, :])
                ins.then_inc(m["router"], 1)
                dve.wait_ge(m["router"], ROUTER_STEPS * g + TOP)
                hold()
                for k in range(TILES):
                    ins = dve.max_index(idx[:, k, :], top[:, k, :], prob[:, k, :])
                ins.then_inc(m["router"], 1)
                dve.wait_ge(m["router"], ROUTER_STEPS * g + IDX)
                dve.tensor_copy(idxf, idx).then_inc(m["idxf"], 1)
                dve.tensor_tensor(den, top[:, :, 0], top[:, :, 1], ALU.add).then_inc(m["router"], 1)
                dve.wait_ge(m["router"], ROUTER_STEPS * g + DEN)
                dve.tensor_scalar(den, den, 1e-9, None, ALU.add).then_inc(m["router"], 1)
                dve.wait_ge(m["router"], ROUTER_STEPS * g + DEN_EPS)
                dve.reciprocal(rden, den).then_inc(m["router"], 1)
                dve.wait_ge(m["router"], ROUTER_STEPS * (g + 1))
                dve.tensor_tensor(share, top[:, :, 0:2], cols(rden, 2), ALU.mult).then_inc(m["share"], 1)
                dve.wait_ge(m["idxf"], g + 1)
                for k, hot in enumerate((hot1, hot2)):
                    dve.tensor_tensor(hot, expert_no[:], idxf[:, :, k:k + 1].broadcast_to([128, TILES, NE]), ALU.is_equal).then_inc(m["hot"], 1)
                dve.wait_ge(m["share"], g + 1)
                for k, hot in enumerate((hot1, hot2)):
                    dve.wait_ge(m["hot"], 4 * g + 1 + k)
                    dve.tensor_tensor(hot, hot, share[:, :, k:k + 1].broadcast_to([128, TILES, NE]), ALU.mult).then_inc(m["hot"], 1)
                dve.wait_ge(m["hot"], 4 * g + 4)
                dve.tensor_tensor(w, hot1, hot2, ALU.add).then_inc(m["w"], 1)
                dve.wait_ge(m["wT"], g + 1)
                dve.tensor_copy(bufC[0:NE, 1, 0:512], P[0:NE, 1, 1536:2048]).then_inc(m["wT_sb"], 1)
                dve.wait_ge(m["w"], g + 1)
                dve.wait_ge(m["x2"], g + 1)
                for e in range(NE + 1):
                    last = x2 if e == 0 else acc
                    bank = P[:, 1, (e % 4) * 512:(e % 4 + 1) * 512]
                    dve.wait_ge(m["y"], g * (NE + 1) + e + 1)
                    if e > 0:
                        dve.wait_ge(m["acc"], g * (NE + 1) + e)
                    if e == NE:
                        ins = dve.tensor_tensor(acc, bank, acc, ALU.add)
                    else:
                        for k in range(TILES):
                            tk = slice(k * D, (k + 1) * D)
                            ins = dve.scalar_tensor_tensor(acc[:, tk], bank[:, tk], w[:, k, e:e + 1], last[:, tk], ALU.mult, ALU.add)
                    ins.then_inc(m["acc"], 1)
                dve.wait_ge(m["acc"], (g + 1) * (NE + 1))
                for k in range(TILES):
                    moments(norm_mid, NORM_D + g * TILES + k + 1, acc[:, k * D:(k + 1) * D], k)
                for k in range(TILES):
                    normalise(norm_mid, NORM_D + g * TILES + k + 1, one(x_all, g * TILES + k), acc[:, k * D:(k + 1) * D], k).then_inc(m["x_done"], 1)

        @block.gpsimd
        def _(pool):
            def inv_std(s, cnt, k):
                pool.wait_ge(s["mv"], cnt)
                pool.tensor_tensor(veps[:, k, :], mv[:, k, 1:2], const_eps[:], ALU.add).then_inc(s["veps"], 1)
                pool.wait_ge(s["veps"], cnt)
                pool.tensor_tensor(rstd[:, k, :], veps[:, k, :], const_mhalf[:, 0:1], ALU.pow).then_inc(s["rstd"], 1)

            pool.wait_ge(setup["const"], 1)

            def inv_front(j, n):
                inv_std(norm_front, n + 1, j)

            def inv_mid(j, n):
                inv_std(norm_mid, n + 1, j)

            def inv_back(j, n):
                inv_std(norm_back, n + 1, j)

            def period(b, f):
                in_turn((inv_mid, b), (inv_front, f), (inv_back, b))

            over_sequences(pool, period)

            def norms(j, n, k, s):
                hs = slice(k * LH, (k + 1) * LH)
                pool.wait_ge(f["ssg_" + s], n + 1)
                pool.tensor_tensor(rnorm[:, j, hs], sumsq_g[:, j, hs], const_mhalf[:], ALU.pow).then_inc(f["rn_" + s], 1)

            def k_norms(j, p, q, n):
                norms(j, n, 1, "k")

            def q_norms(j, p, q, n):
                norms(j, n, 0, "q")

            def inv_std_local(j, p, q, n):
                inv_std(norm_back, BATCH + n + 1, j)

            def period(b, f):
                in_turn((k_norms, f), (q_norms, f), (inv_std_local, b))

            over_layers(pool, period)

            def inv_front(j, n):
                inv_std(norm_front, BATCH + n + 1, j)

            def inv_mid(j, n):
                inv_std(norm_mid, BATCH + n + 1, j)

            def inv_back(j, n):
                inv_std(norm_back, NORM_C + n + 1, j)

            def period(b, f):
                in_turn((inv_mid, f), (inv_front, b), (inv_back, b))

            over_sequences(pool, period)

            with pool.Fori(0, GROUPS) as g:
                for k in range(TILES):
                    inv_std(norm_mid, NORM_D + g * TILES + k + 1, k)

        @block.scalar
        def _(act):
            def exps(s, cnt, u, j, heads, keys, dst):
                act.wait_ge(s["nb"], part(cnt, u))
                for n in range(u * heads // 2, (u + 1) * heads // 2):
                    at = slice(n * keys, (n + 1) * keys)
                    ins = act.activation(dst[:, j, at], P[:, j, at], ACT.Exp, bias=bias[:, j, n:n + 1])
                ins.then_inc(s["probs"], 1)

            def copy(dst, src, scale=1.0):
                return act.activation(dst, src, ACT.Copy, scale=scale)

            act.wait_ge(load["x"], 16 * N_X)
            act.activation(gate_e[:], gate_col[:], ACT.Exp, scale=-1.0).then_inc(setup["gate"], 1)
            act.wait_ge(load["consts"], 16 * N_CONSTS)
            act.wait_ge(load["a"], 16 * N_A)
            act.wait_ge(setup["const"], 1)

            def keep_kvq(j, n, u):
                act.wait_ge(a["kvq"], n + 1)
                if u == 0:
                    copy(bufA[:, j, 0:128], P[:, j, 1024:1152], head_temp[:, 0:1])
                else:
                    copy(bufA[:, j, 640:768], P[:, j, 1536:1664])
                for h in range(8 * u, 8 * u + 8):
                    ins = copy(bufC[:, j, h * 128:(h + 1) * 128], P[:, j, 1152:1280], mask_of_8[:, h:h + 1])
                ins.then_inc(a["kvq_sb"], 1)

            def mix_exp(j, n, u):
                exps(a, n + 1, u, j, 16, 128, bufB)

            def keep_v(j, n):
                act.wait_ge(x["qkv"], n + 1)
                copy(slots(vals[:, j, 0:272], 16, 17)[:, :, 0:16], slots(P[:, j, 512:768], 16, 16)).then_inc(x["v"], 1)

            def keep_qk(j, n, u):
                act.wait_ge(x["qkT"], n + 1)
                if u == 0:
                    copy(bufB[:, j, 0:256], P[:, j, 1024:1280])
                for h in range(4 * u, 4 * u + 4):
                    ins = copy(bufC[:, j, h * 256:(h + 1) * 256], P[:, j, 1280:1536], mask_of_16[:, h:h + 1])
                ins.then_inc(x["qkT_sb"], 1)

            def exp_scores(j, n, u):
                exps(core, n + 1, u, j, 8, 256, bufA)

            def period(b, f):
                in_turn((keep_kvq, f, 0), (keep_qk, b, 0), (keep_qk, b, 1), (keep_kvq, f, 1), (exp_scores, b, 0),
                        (exp_scores, b, 1), (mix_exp, f, 0), (mix_exp, f, 1), (keep_v, f))

            over_sequences(act, period)

            act.wait_ge(setup["shift_zero"], 1)

            def q_squared(j, p, q, n):
                act.wait_ge(f["q"], n + 1)
                act.activation(bufB[:, j, 0:INNER], P[:, j, 0:INNER], ACT.Square).then_inc(f["sq_q"], 1)

            def k_squared(j, p, q, n):
                act.wait_ge(f["k"], n + 1)
                act.activation(bufB[:, j, INNER:2 * INNER], P[:, j, INNER:2 * INNER], ACT.Square).then_inc(f["sq_k"], 1)

            def keep_v(j, p, q, n):
                act.wait_ge(f["v"], n + 1)
                copy(vals[:, j, 0:INNER], P[:, j, 0:INNER]).then_inc(f["v_sb"], 1)

            def keep_q(j, p, q, n):
                act.wait_ge(f["qT"], n + 1)
                act.wait_ge(f["ssg_q"], n + 1)
                copy(bufB[:, j, 0:INNER], P[:, j, 0:INNER]).then_inc(f["qT_sb"], 1)

            def keep_k(j, p, q, n, u):
                act.wait_ge(f["kT"], part(n + 1, u))
                half = slice(INNER + 512 * u, INNER + 512 * u + 512)
                copy(bufB[:, j, half], P[:, j, half]).then_inc(f["kT_sb"], 1)

            def exp_scores(j, p, q, n, u):
                act.wait_ge(core["nb"], part(CORE_B + n + 1, u))
                for k in range(8 * u, 8 * u + 8):
                    h = BY_ROW_LOCAL[k]
                    ins = act.activation(bufA[:, j, k * 128:(k + 1) * 128], P[:, j, k * 128:(k + 1) * 128], ACT.Exp,
                                         bias=bias[:, j, k:k + 1], scale=rnorm[:, j, h:h + 1], accum_out=zsum[:, j, k:k + 1])
                ins.then_inc(core["probs"], 1)

            def keep_heads(j, p, q, n, u):
                act.wait_ge(core["av"], av_cnt(n, u))
                copy(bufB[:, j, INNER + 512 * u:INNER + 512 * u + 512], P[:, j, 1024 * u:1024 * u + 512]).then_inc(core["oT_sb"], 1)

            def gelu(j, p, q, n):
                act.wait_ge(f["h"], part(n + 1, 0))
                for k, (lo, w) in enumerate(HCH):
                    at = slice(k * 128, (k + 1) * 128)
                    ins = act.activation(bufA[0:w, j, at], P[0:w, j, 512 + k * 128:512 + (k + 1) * 128], ACT.Gelu,
                                         bias=f_b1[0:w, p, 1, k:k + 1])
                ins.then_inc(f["gl"], 1)

            def layer_bias(r, p):
                act.wait_ge(wt[p], 16 * LAYER_DMAS * (r + 1))

            def period(b, f):
                in_turn((exp_scores, b, 0), (q_squared, f), (exp_scores, b, 1), (k_squared, f), (keep_heads, b, 0),
                        (keep_v, f), (keep_heads, b, 1), (keep_q, f), (keep_k, f, 0), (keep_k, f, 1), (gelu, b))

            over_layers(act, period, layer_bias)

            act.wait_ge(setup["ones_c"], 1)

            def keep_kvq(j, n):
                act.wait_ge(c["kvq"], n + 1)
                copy(flat[:, j, 0:128], P[:, j, 256:384], 8 ** -0.5)
                copy(flat[:, j, 128:256], P[:, j, 0:128])
                copy(slots(vals[:, j, 0:144], 16, 9)[:, :, 0:8], slots(P[:, j, 128:256], 16, 8)).then_inc(c["kvq_sb"], 1)

            def keep_qk(j, n, u):
                act.wait_ge(c["qkT"], n + 1)
                if u == 0:
                    copy(bufB[:, j, 0:128], P[:, j, 1024:1152])
                for h in range(8 * u, 8 * u + 8):
                    ins = copy(bufC[:, j, h * 128:(h + 1) * 128], P[:, j, 1152:1280], mask_of_8[:, h:h + 1])
                ins.then_inc(c["qkT_sb"], 1)

            def exp_scores(j, n, u):
                exps(cau, n + 1, u, j, 16, 128, bufA)

            def keep_cross_qkv(j, n):
                act.wait_ge(y["qkv"], n + 1)
                copy(flat[:, j, 256:384], P[:, j, 0:128], 16 ** -0.5)
                copy(flat[:, j, 384:512], P[:, j, 128:256])
                copy(slots(vals[:, j, 256:392], 8, 17)[:, :, 0:16], slots(P[:, j, 256:384], 8, 16)).then_inc(y["qkv_sb"], 1)

            def keep_cross_qk(j, n, u):
                act.wait_ge(y["qkT"], n + 1)
                if u == 0:
                    copy(bufB[:, j, 0:128], P[:, j, 1024:1152])
                for h in range(4 * u, 4 * u + 4):
                    at = 1024 + h * 128
                    ins = copy(bufC[:, j, at:at + 128], P[:, j, 1152:1280], mask_of_16[:, h:h + 1])
                ins.then_inc(y["qkT_sb"], 1)

            def cross_exp(j, n, u):
                exps(core, CORE_C + n + 1, u, j, 8, 128, bufA)

            def period(b, f):
                in_turn((keep_kvq, f), (keep_qk, f, 0), (keep_cross_qkv, b), (keep_qk, f, 1), (keep_cross_qk, b, 0),
                        (keep_cross_qk, b, 1), (exp_scores, f, 0), (cross_exp, b, 0), (cross_exp, b, 1),
                        (exp_scores, f, 1))

            over_sequences(act, period)

            act.wait_ge(load["m"], 16 * N_M)
            with act.Fori(0, GROUPS) as g:
                act.wait_ge(m["sub"], g + 1)
                act.activation(bufC[:, 1, 1088:1120], bufC[:, 1, 1056:1088], ACT.Exp).then_inc(m["ex"], 1)
                for e in range(NE + 1):
                    if e >= 2:
                        act.wait_ge(m["y"], g * (NE + 1) + e - 1)
                    for k in range(EI // 128):
                        turn = e * (EI // 128) + k
                        act.wait_ge(m["h"], g * 36 + turn + 1)
                        act.activation((bufA, bufB)[e % 2][:, 0, k * 512:(k + 1) * 512], P[:, 0, k * 512:(k + 1) * 512],
                                       ACT.Gelu_apprx_tanh, bias=m_b1[:, e, k:k + 1]).then_inc(m["g"], 1)


def constants():
    tok = np.arange(T, dtype=np.float32)
    hd = 16
    inv = (1.0 / 10000.0 ** (np.arange(0, hd, 2, dtype=np.float32) / hd)).astype(np.float32)
    fr = tok[:, None] * inv[None, :]
    emb = np.concatenate([fr, fr], -1)
    sign = np.where(np.arange(hd) % 2 == 0, -1.0, 1.0)
    fold = np.repeat([0.25, 0.25, 1.0, 1.0], D)[None, :]
    x_cos = np.tile(np.cos(emb), (1, 4 * D // hd)) * fold
    x_sin = np.tile(np.sin(emb) * sign, (1, 4 * D // hd)) * fold
    half = np.arange(0, LD, 2, dtype=np.float32)
    inv = (1.0 / 10000.0 ** (half / LD)).astype(np.float32)
    fr = tok[:, None] * inv[None, :]
    emb = np.concatenate([fr, fr], -1)
    base = (half + 0.4 * LD) / (1.4 * LD)
    scale = base[None, :] ** ((tok - T // 2) / 16.0)[:, None]
    scale = np.concatenate([scale, scale], -1)
    sign = np.where(np.arange(LD) < LD // 2, -1.0, 1.0)
    f_cos = np.stack([8.0 * np.cos(emb) * scale, np.cos(emb) / scale], 1)
    f_sin = np.stack([8.0 * np.sin(emb) * sign * scale, np.sin(emb) * sign / scale], 1)
    q, k = np.arange(T)[:, None], np.arange(T)[None, :]
    local = (k <= q) & (q <= k + 32) & (k // 32 >= q // 32 - 1)
    low = np.float32(-1e30)
    return {
        "ident": np.eye(128, dtype=np.float32),
        "shift": np.eye(128, k=1, dtype=np.float32),
        "local_mask": np.tile(np.where(local, 0, low), (1, 4)).astype(np.float32),
        "causal_mask": np.tile(np.where(k <= q, 0, low), (1, 4)).astype(np.float32),
        "mask_of_8": (np.arange(128)[:, None] // 8 == np.arange(16)[None, :]).astype(np.float32),
        "mask_of_16": (np.arange(128)[:, None] // 16 == np.arange(8)[None, :]).astype(np.float32),
        "x_cos": x_cos.astype(np.float32), "x_sin": x_sin.astype(np.float32),
        "f_cos": f_cos.astype(np.float32), "f_sin": f_sin.astype(np.float32),
        "expert_no": np.tile(np.arange(NE, dtype=np.float32), (128, TILES, 1)),
    }


def kernel(**inputs):
    import concourse.bacc as bacc
    from concourse.bass_utils import run_bass_kernel_spmd as run

    nc = bacc.Bacc("TRN2", target_bir_lowering=False, num_devices=1)
    arrays, args = {}, {}
    for name, value in [*inputs.items(), *constants().items()]:
        a = np.ascontiguousarray(value)
        arrays[f"in_{name}"] = a
        args[name] = nc.dram_tensor(f"in_{name}", a.shape, mybir.dt.from_np(a.dtype), kind="ExternalInput").ap()
    out = nc.dram_tensor("out_x", (BATCH, T, D), fp32, kind="ExternalOutput").ap()
    program(nc, args, out)
    return run(nc, [arrays], core_ids=[0]).results[0]["out_x"]
```
